# Optimizing a Trainium2 kernel written in Bass

```python
import numpy as np
import jax
import jax.numpy as jnp

def _softmax(x, axis=-1):
    return jax.nn.softmax(x, axis=axis)

def _gelu(x):
    return jax.nn.gelu(x, approximate=True)

def _silu(x):
    return jax.nn.silu(x)

def _sigmoid(x):
    return jax.nn.sigmoid(x)

def _layernorm(x, axis=-1, eps=1e-05):
    m = jnp.mean(x, axis=axis, keepdims=True)
    v = jnp.var(x, axis=axis, keepdims=True)
    return (x - m) / jnp.sqrt(v + eps)

def _scatter_add(tgt, idx, src, axis=0):
    return tgt.at[idx].add(src)

def _segment_sum(src, seg, n):
    return jax.ops.segment_sum(src, seg, n)
kernel_name = 'mk_gnn_preln_d4_gnn_r32_c9dfab'

def setup_inputs(seed: int=0):
    np.random.seed(seed)
    _w = jnp.asarray

    def _rec_inputs():
        import jax
        import jax.numpy as jnp
        _gk = jax.random.key(seed)
        x = -0.0003713 + 1 * jax.random.normal(jax.random.fold_in(_gk, 1), (3125, 128), jnp.float32)
        _s = jax.random.randint(jax.random.fold_in(_gk, 2), (50000,), 0, 3125, jnp.int32)
        _d = jax.random.randint(jax.random.fold_in(_gk, 3), (50000,), 0, 3125, jnp.int32)
        _loop = jnp.arange(3125, dtype=jnp.int32)
        src = jnp.concatenate([_s, _d, _loop])
        dst = jnp.concatenate([_d, _s, _loop])
        _o = jnp.argsort(dst, stable=True)
        src = src[_o]
        dst = dst[_o]
        edge_attr_64 = jax.random.uniform(jax.random.fold_in(_gk, 12), (103125, 64), jnp.float32, 0.0, 1)
        return (x, src, dst, edge_attr_64)
    x, src, dst, edge_attr_64 = _rec_inputs()

    def _L0_gnn_setup():
        import jax, jax.numpy as jnp
        import numpy as np
        N_NODES = 3125
        N_EDGES = 50000
        F_IN = 128
        H1 = 128
        H2 = 128

        def _gcn_norm(edge_index, num_nodes):
            loop = jnp.arange(num_nodes, dtype=edge_index.dtype)
            row = jnp.concatenate([edge_index[0], loop])
            col = jnp.concatenate([edge_index[1], loop])
            ones = jnp.ones_like(col, dtype=jnp.float32)
            deg = jax.ops.segment_sum(ones, col, num_segments=num_nodes)
            dinv = jnp.where(deg > 0, 1.0 / jnp.sqrt(deg), 0.0)
            norm = dinv[row] * dinv[col]
            return (row, col, norm)

        def _gcn_conv(x, W, b, row, col, norm, num_nodes):
            h = x @ W
            msg = h[row] * norm[:, None]
            out = jax.ops.segment_sum(msg, col, num_segments=num_nodes)
            return out + b
        key = jax.random.key(seed)
        k1, k2, k3, k4 = jax.random.split(key, 4)
        x = jax.random.normal(k1, (N_NODES, F_IN), dtype=jnp.float32)
        edge_index = jax.random.randint(k2, (2, N_EDGES), 0, N_NODES, dtype=jnp.int64)
        W1 = jax.random.normal(k3, (F_IN, H1), dtype=jnp.float32) / np.sqrt(F_IN)
        b1 = jnp.zeros((H1,), dtype=jnp.float32)
        W2 = jax.random.normal(k4, (H1, H2), dtype=jnp.float32) / np.sqrt(H1)
        b2 = jnp.zeros((H2,), dtype=jnp.float32)
        return {'x': x, 'edge_index': edge_index, 'W1': W1, 'b1': b1, 'W2': W2, 'b2': b2}
    _L0_gnn_all = _L0_gnn_setup()
    _L0_gnn_in = {k: v for k, v in _L0_gnn_all.items() if k in ('W1', 'b1', 'W2', 'b2')}
    del _L0_gnn_all

    def _L1_gnn_setup():
        import jax, jax.numpy as jnp
        import numpy as np
        N_NODES = 3125
        N_EDGES = 50000
        IN_CH = 128
        HEADS = 4
        OUT_CH = 32
        key = jax.random.key(seed)
        k1, k2, k3, k4 = jax.random.split(key, 4)
        x = jax.random.normal(k1, (N_NODES, IN_CH), dtype=jnp.float32)
        edge_index = jax.random.randint(k2, (2, N_EDGES), 0, N_NODES, dtype=jnp.int64)
        W = jax.random.normal(k3, (IN_CH, HEADS * OUT_CH), dtype=jnp.float32) * (1.0 / np.sqrt(IN_CH))
        att = jax.random.normal(k4, (HEADS, OUT_CH), dtype=jnp.float32)
        return {'x': x, 'edge_index': edge_index, 'W': W, 'att': att}
    _L1_gnn_all = _L1_gnn_setup()
    _L1_gnn_in = {k: v for k, v in _L1_gnn_all.items() if k in ('W', 'att')}
    del _L1_gnn_all

    def _L2_gnn_setup():
        import jax, jax.numpy as jnp
        import numpy as np
        N, E, D, H = (3125, 50000, 128, 2)
        NEG_SLOPE = 0.2
        EPS = 1e-16

        def _segment_softmax(alpha, seg, num_segments):
            m = jax.ops.segment_max(alpha, seg, num_segments=num_segments)
            a = jnp.exp(alpha - m[seg])
            z = jax.ops.segment_sum(a, seg, num_segments=num_segments)
            return a / (z[seg] + EPS)
        key = jax.random.key(seed)
        ks = jax.random.split(key, 12)
        s = 1.0 / np.sqrt(D)
        return {'x': jax.random.normal(ks[0], (N, D), jnp.float32), 'edge_index': jax.random.randint(ks[1], (2, E), 0, N, jnp.int64), 'gamma': jnp.ones((D,), jnp.float32), 'beta': jnp.zeros((D,), jnp.float32), 'Wl': jax.random.normal(ks[2], (D, H * D), jnp.float32) * s, 'bl': jnp.zeros((H * D,), jnp.float32), 'Wr': jax.random.normal(ks[3], (D, H * D), jnp.float32) * s, 'br': jnp.zeros((H * D,), jnp.float32), 'att': jax.random.normal(ks[4], (H, D), jnp.float32) * s, 'res_W': jax.random.normal(ks[5], (D, D), jnp.float32) * s, 'bias': jnp.zeros((D,), jnp.float32)}
    _L2_gnn_all = _L2_gnn_setup()
    _L2_gnn_in = {k: v for k, v in _L2_gnn_all.items() if k in ('gamma', 'beta', 'Wl', 'bl', 'Wr', 'br', 'att', 'res_W', 'bias')}
    del _L2_gnn_all

    def _L3_gnn_setup():
        import jax, jax.numpy as jnp
        import numpy as np
        N, P, Fdim, K = (3125, 31250, 128, 64)
        NRI, NRA = (3, 2)

        def ssp(x):
            return jax.nn.softplus(x) - jnp.log(2.0)

        def residual(x, W1, b1, W2, b2):
            return x + ssp(ssp(x) @ W1 + b1) @ W2 + b2
        key = jax.random.key(seed)
        ks = jax.random.split(key, 20)
        s = 1.0 / np.sqrt(Fdim)
        inp = {'x': jax.random.normal(ks[0], (N, Fdim), jnp.float32), 'rbf': jax.random.uniform(ks[1], (P, K), jnp.float32), 'idx_i': jax.random.randint(ks[2], (P,), 0, N), 'idx_j': jax.random.randint(ks[3], (P,), 0, N), 'k2f_W': jax.random.normal(ks[4], (K, Fdim), jnp.float32) / np.sqrt(K), 'Wi': jax.random.normal(ks[5], (Fdim, Fdim), jnp.float32) * s, 'bi': jnp.zeros((Fdim,), jnp.float32), 'Wj': jax.random.normal(ks[6], (Fdim, Fdim), jnp.float32) * s, 'bj': jnp.zeros((Fdim,), jnp.float32), 'res_int_W1': jax.random.normal(ks[7], (NRI, Fdim, Fdim), jnp.float32) * s, 'res_int_b1': jnp.zeros((NRI, Fdim), jnp.float32), 'res_int_W2': jax.random.normal(ks[8], (NRI, Fdim, Fdim), jnp.float32) * s, 'res_int_b2': jnp.zeros((NRI, Fdim), jnp.float32), 'dense_W': jax.random.normal(ks[9], (Fdim, Fdim), jnp.float32) * s, 'dense_b': jnp.zeros((Fdim,), jnp.float32), 'u': jnp.ones((Fdim,), jnp.float32), 'res_at_W1': jax.random.normal(ks[10], (NRA, Fdim, Fdim), jnp.float32) * s, 'res_at_b1': jnp.zeros((NRA, Fdim), jnp.float32), 'res_at_W2': jax.random.normal(ks[11], (NRA, Fdim, Fdim), jnp.float32) * s, 'res_at_b2': jnp.zeros((NRA, Fdim), jnp.float32)}
        return inp
    _L3_gnn_all = _L3_gnn_setup()
    _L3_gnn_in = {k: v for k, v in _L3_gnn_all.items() if k in ('k2f_W', 'Wi', 'bi', 'Wj', 'bj', 'res_int_W1', 'res_int_b1', 'res_int_W2', 'res_int_b2', 'dense_W', 'dense_b', 'u', 'res_at_W1', 'res_at_b1', 'res_at_W2', 'res_at_b2')}
    del _L3_gnn_all
    return {'x': x, 'src': src, 'dst': dst, 'edge_attr_64': edge_attr_64, 'L0_gnn_W1': _L0_gnn_in['W1'], 'L0_gnn_b1': _L0_gnn_in['b1'], 'L0_gnn_W2': _L0_gnn_in['W2'], 'L0_gnn_b2': _L0_gnn_in['b2'], 'L1_gnn_W': _L1_gnn_in['W'], 'L1_gnn_att': _L1_gnn_in['att'], 'L2_gnn_gamma': _L2_gnn_in['gamma'], 'L2_gnn_beta': _L2_gnn_in['beta'], 'L2_gnn_Wl': _L2_gnn_in['Wl'], 'L2_gnn_bl': _L2_gnn_in['bl'], 'L2_gnn_Wr': _L2_gnn_in['Wr'], 'L2_gnn_br': _L2_gnn_in['br'], 'L2_gnn_att': _L2_gnn_in['att'], 'L2_gnn_res_W': _L2_gnn_in['res_W'], 'L2_gnn_bias': _L2_gnn_in['bias'], 'L3_gnn_k2f_W': _L3_gnn_in['k2f_W'], 'L3_gnn_Wi': _L3_gnn_in['Wi'], 'L3_gnn_bi': _L3_gnn_in['bi'], 'L3_gnn_Wj': _L3_gnn_in['Wj'], 'L3_gnn_bj': _L3_gnn_in['bj'], 'L3_gnn_res_int_W1': _L3_gnn_in['res_int_W1'], 'L3_gnn_res_int_b1': _L3_gnn_in['res_int_b1'], 'L3_gnn_res_int_W2': _L3_gnn_in['res_int_W2'], 'L3_gnn_res_int_b2': _L3_gnn_in['res_int_b2'], 'L3_gnn_dense_W': _L3_gnn_in['dense_W'], 'L3_gnn_dense_b': _L3_gnn_in['dense_b'], 'L3_gnn_u': _L3_gnn_in['u'], 'L3_gnn_res_at_W1': _L3_gnn_in['res_at_W1'], 'L3_gnn_res_at_b1': _L3_gnn_in['res_at_b1'], 'L3_gnn_res_at_W2': _L3_gnn_in['res_at_W2'], 'L3_gnn_res_at_b2': _L3_gnn_in['res_at_b2']}

def reference(x, src, dst, edge_attr_64, L0_gnn_W1, L0_gnn_b1, L0_gnn_W2, L0_gnn_b2, L1_gnn_W, L1_gnn_att, L2_gnn_gamma, L2_gnn_beta, L2_gnn_Wl, L2_gnn_bl, L2_gnn_Wr, L2_gnn_br, L2_gnn_att, L2_gnn_res_W, L2_gnn_bias, L3_gnn_k2f_W, L3_gnn_Wi, L3_gnn_bi, L3_gnn_Wj, L3_gnn_bj, L3_gnn_res_int_W1, L3_gnn_res_int_b1, L3_gnn_res_int_W2, L3_gnn_res_int_b2, L3_gnn_dense_W, L3_gnn_dense_b, L3_gnn_u, L3_gnn_res_at_W1, L3_gnn_res_at_b1, L3_gnn_res_at_W2, L3_gnn_res_at_b2):
    import jax
    import jax.numpy as jnp

    def _L0_gnn_ref(x, edge_index, W1, b1, W2, b2):
        import jax, jax.numpy as jnp
        import numpy as np
        N_NODES = 3125
        N_EDGES = 50000
        F_IN = 128
        H1 = 128
        H2 = 128

        def _gcn_norm(edge_index, num_nodes):
            loop = jnp.arange(num_nodes, dtype=edge_index.dtype)
            row = jnp.concatenate([edge_index[0], loop])
            col = jnp.concatenate([edge_index[1], loop])
            ones = jnp.ones_like(col, dtype=jnp.float32)
            deg = jax.ops.segment_sum(ones, col, num_segments=num_nodes)
            dinv = jnp.where(deg > 0, 1.0 / jnp.sqrt(deg), 0.0)
            norm = dinv[row] * dinv[col]
            return (row, col, norm)

        def _gcn_conv(x, W, b, row, col, norm, num_nodes):
            h = x @ W
            msg = h[row] * norm[:, None]
            out = jax.ops.segment_sum(msg, col, num_segments=num_nodes)
            return out + b
        N = x.shape[0]
        row, col, norm = _gcn_norm(edge_index, N)
        h = jax.nn.relu(_gcn_conv(x, W1, b1, row, col, norm, N))
        h = _gcn_conv(h, W2, b2, row, col, norm, N)
        return jax.nn.softmax(h, axis=1)

    def _L1_gnn_ref(x, edge_index, W, att):
        import jax, jax.numpy as jnp
        import numpy as np
        N_NODES = 3125
        N_EDGES = 50000
        IN_CH = 128
        HEADS = 4
        OUT_CH = 32
        N = x.shape[0]
        row, col = (edge_index[0], edge_index[1])
        projected = (x @ W).reshape(N, HEADS, OUT_CH)
        src = projected[row]
        dst = projected[col]
        scores = jnp.tanh(src + dst)
        scores = jnp.einsum('ehc,hc->eh', scores, att)
        scores = jnp.exp(scores - jnp.max(scores, axis=0, keepdims=True))
        out = jax.ops.segment_sum(src * scores[:, :, None], col, num_segments=N)
        normalizer = jax.ops.segment_sum(scores, col, num_segments=N)
        out = out / jnp.maximum(normalizer, 1e-12)[:, :, None]
        return out.reshape(N, HEADS * OUT_CH)

    def _L2_gnn_ref(x, edge_index, gamma, beta, Wl, bl, Wr, br, att, res_W, bias):
        import jax, jax.numpy as jnp
        import numpy as np
        N, E, D, H = (3125, 50000, 128, 2)
        NEG_SLOPE = 0.2
        EPS = 1e-16

        def _segment_softmax(alpha, seg, num_segments):
            m = jax.ops.segment_max(alpha, seg, num_segments=num_segments)
            a = jnp.exp(alpha - m[seg])
            z = jax.ops.segment_sum(a, seg, num_segments=num_segments)
            return a / (z[seg] + EPS)
        n = x.shape[0]
        residual = x
        mu = x.mean(-1, keepdims=True)
        var = ((x - mu) ** 2).mean(-1, keepdims=True)
        h = (x - mu) * jax.lax.rsqrt(var + 1e-05) * gamma + beta
        h = jax.nn.relu(h)
        xl = (h @ Wl + bl).reshape(n, H, D)
        xr = (h @ Wr + br).reshape(n, H, D)
        src, dst = (edge_index[0], edge_index[1])
        e = jax.nn.leaky_relu(xl[src] + xr[dst], NEG_SLOPE)
        alpha = jnp.einsum('ehd,hd->eh', e, att)
        alpha = _segment_softmax(alpha, dst, n)
        msg = xl[src] * alpha[..., None]
        out = jax.ops.segment_sum(msg, dst, num_segments=n)
        out = out.mean(axis=1)
        out = out + h @ res_W + bias
        return residual + out

    def _L3_gnn_ref(x, rbf, idx_i, idx_j, k2f_W, Wi, bi, Wj, bj, res_int_W1, res_int_b1, res_int_W2, res_int_b2, dense_W, dense_b, u, res_at_W1, res_at_b1, res_at_W2, res_at_b2):
        import jax, jax.numpy as jnp
        import numpy as np
        N, P, Fdim, K = (3125, 31250, 128, 64)
        NRI, NRA = (3, 2)

        def ssp(x):
            return jax.nn.softplus(x) - jnp.log(2.0)

        def residual(x, W1, b1, W2, b2):
            return x + ssp(ssp(x) @ W1 + b1) @ W2 + b2
        n = x.shape[0]
        xa = ssp(x)
        g = rbf @ k2f_W
        xi = xa @ Wi + bi
        msg = g * (xa @ Wj + bj)[idx_j]
        xj = jax.ops.segment_sum(msg, idx_i, num_segments=n)
        m = xi + xj
        for l in range(NRI):
            m = residual(m, res_int_W1[l], res_int_b1[l], res_int_W2[l], res_int_b2[l])
        m = ssp(m)
        out = u * x + m @ dense_W + dense_b
        for l in range(NRA):
            out = residual(out, res_at_W1[l], res_at_b1[l], res_at_W2[l], res_at_b2[l])
        return out
    edge_index = jnp.stack([src, dst])
    h = jnp.maximum(_layernorm(x, axis=-1), 0.0)
    x = x + _L0_gnn_ref(h, edge_index, L0_gnn_W1, L0_gnn_b1, L0_gnn_W2, L0_gnn_b2)
    h = jnp.maximum(_layernorm(x, axis=-1), 0.0)
    x = x + _L1_gnn_ref(h, edge_index, L1_gnn_W, L1_gnn_att)
    h = jnp.maximum(_layernorm(x, axis=-1), 0.0)
    x = x + _L2_gnn_ref(h, edge_index, L2_gnn_gamma, L2_gnn_beta, L2_gnn_Wl, L2_gnn_bl, L2_gnn_Wr, L2_gnn_br, L2_gnn_att, L2_gnn_res_W, L2_gnn_bias)
    h = jnp.maximum(_layernorm(x, axis=-1), 0.0)
    x = x + _L3_gnn_ref(h, edge_attr_64, src, dst, L3_gnn_k2f_W, L3_gnn_Wi, L3_gnn_bi, L3_gnn_Wj, L3_gnn_bj, L3_gnn_res_int_W1, L3_gnn_res_int_b1, L3_gnn_res_int_W2, L3_gnn_res_int_b2, L3_gnn_dense_W, L3_gnn_dense_b, L3_gnn_u, L3_gnn_res_at_W1, L3_gnn_res_at_b1, L3_gnn_res_at_W2, L3_gnn_res_at_b2)
    return x

_drawn_inputs = setup_inputs


def setup_inputs(seed=0):
    import zlib

    import numpy as np

    out = dict(_drawn_inputs(seed))
    spreads = {'L0_gnn_b1': (0.0, 0.8),
     'L0_gnn_b2': (0.0, 0.8),
     'L2_gnn_gamma': (1.0, 0.2),
     'L2_gnn_beta': (0.0, 0.1),
     'L2_gnn_bl': (0.0, 0.1),
     'L2_gnn_br': (0.0, 0.8),
     'L2_gnn_bias': (0.0, 0.1),
     'L3_gnn_bi': (0.0, 0.487),
     'L3_gnn_bj': (0.0, 0.1),
     'L3_gnn_res_int_b1': (0.0, 0.54),
     'L3_gnn_res_int_b2': (0.0, 0.276),
     'L3_gnn_dense_b': (0.0, 0.416),
     'L3_gnn_u': (1.0, 0.2),
     'L3_gnn_res_at_b1': (0.0, 0.55),
     'L3_gnn_res_at_b2': (0.0, 0.335)}
    factors = {'L0_gnn_W1': 8.0, 'L0_gnn_W2': 8.0, 'L2_gnn_Wr': 7.302}
    for name, (base, spread) in spreads.items():
        noise = np.random.default_rng([zlib.crc32(name.encode()), seed]).standard_normal(out[name].shape)
        drawn = base * np.exp(spread * noise) if base else spread * noise
        out[name] = jnp.asarray(drawn.astype(out[name].dtype))
    for name, factor in factors.items():
        out[name] = (out[name] * factor).astype(out[name].dtype)
    return out
```

```python
from contextlib import ExitStack

import numpy as np

import concourse.bass as bass
from concourse import mybir

ALU = mybir.AluOpType
ACT = mybir.ActivationFunctionType
AX = mybir.AxisListType
F32 = mybir.dt.float32
I32 = mybir.dt.int32

P = 128
F = 128
WIN = 32
SUB = 4
TILE = P * SUB
RING = 4
BIG = 1e30
CHUNK = 512
BANKS = 8
LN_EPS = 1e-5
HEADS1 = 4
HEADS2 = 2


def ceil_div(a, b):
    return -(-a // b)


class Tile:

    def __init__(self, t, slot, rounds):
        self.t, self.slot, self.rounds = t, slot, rounds
        self.two = slot % 2


def over_tiles(eng, tiles, stages):
    full = tiles // RING

    def step(s_round, s_slot, static):
        for lag, stage in stages:
            slot = (s_slot - lag) % RING
            rounds = s_round if s_slot >= lag else s_round - 1
            t = rounds * RING + slot
            if not static or 0 <= t < tiles:
                stage(Tile(t, slot, rounds))

    for s in range(RING):
        step(0, s, True)
    with eng.Fori(1, full) as i:
        for s in range(RING):
            step(i, s, False)
    for s in range(full * RING, tiles + max(lag for lag, _ in stages)):
        step(s // RING, s % RING, True)


def wait_count(eng, sem, count):
    if not isinstance(count, int) or count > 0:
        eng.wait_ge(sem, count)


class Kernel:

    def __init__(self, nc, ctx, ins, out):
        self.nc, self.ctx, self.ins, self.out = nc, ctx, ins, out
        self.n_nodes = ins["x"].shape[1] * P
        self.blocks = ins["x"].shape[1]
        self.tiles = ins["src_rows"].shape[0]

    def sb(self, name, shape, dt=F32):
        return self.ctx.enter_context(self.nc.sbuf_tensor(name, shape, dt))


class Stage:

    def __init__(self, k, name):
        self.k, self.nc, self.name = k, k.nc, name
        self.ctx, self.sems, self.pool_dma = ExitStack(), [], []

    def sem(self, name):
        s = self.ctx.enter_context(self.nc.semaphore(f"{self.name}_{name}"))
        self.sems.append(s)
        return s

    def pool_dma_sem(self, name):
        s = self.sem(name)
        self.pool_dma.append(s)
        return s

    def __enter__(self):
        return self

    def block(self):
        return self.nc.Block(f"{self.name}_{self.nc.next_id()}", no_gpsimd_drain=not self.pool_dma)

    def clear(self):
        for s in self.pool_dma:
            self.nc.gpsimd.dma_reset(range(s.num, s.num + 1))
        for s in self.sems:
            self.nc.gpsimd.sem_clear(s)
        self.nc.all_engine_barrier()

    def __exit__(self, *exc):
        if exc[0] is None:
            self.clear()
        self.ctx.close()
        return False



def load_everything(k):
    nc, ins = k.nc, k.ins
    B, T, N = k.blocks, k.tiles, k.n_nodes
    k.bank = [k.ctx.enter_context(nc.psum_tensor(f"bank{i}", [P, CHUNK], F32)) for i in range(BANKS)]
    k.x = k.sb("x_nm", [P, B, F])
    k.h = k.sb("h_nm", [P, B, F])
    k.fa = k.sb("fm_a", [P, N])
    k.fb = k.sb("fm_b", [P, N])
    k.acc = k.sb("acc", [P, 2, N])
    k.inv_sqrt_deg = k.sb("inv_sqrt_deg_fm", [P, N])
    k.inv_sqrt_deg_nm = k.sb("inv_sqrt_deg_nm", [P, B])
    k.scores = k.sb("scores", [P, T * SUB * HEADS1])
    k.stat = k.sb("stat", [P, B])
    k.stat2 = k.sb("stat2", [P, B])
    k.wide = k.sb("wide", [P, 2, N])
    k.dst_i = k.scores[:, 0:T * SUB].bitcast(I32)
    k.dst_f = k.sb("dst_f", [P, T * SUB])
    k.pad = k.sb("pad", [P, T * SUB])
    k.local = k.sb("local", [P, T * SUB])
    k.member = k.sb("member", [P, T * SUB])
    k.first = k.sb("first", [P, T])
    k.base = k.sb("base", [P, T])
    k.base_i = k.sb("base_i", [P, T], I32)
    k.first_i = k.base_i
    k.win_off = k.sb("win_off", [P, 1])
    k.win_step = k.sb("win_step", [P, 1])
    k.passes_i = k.sb("passes_i", [P, 1], I32)
    k.spare = k.sb("spare", [P, 1])
    k.small = k.sb("small", [P, 16])
    k.picked = k.sb("picked", [P, SUB * HEADS1])
    k.tops = k.sb("tops", [P, 2, HEADS2])
    k.tile_top = k.sb("tile_top", [HEADS2, WIN])
    k.node_top = k.inv_sqrt_deg[0:HEADS2, :]
    k.node_sum = k.fa[0:HEADS2, :]
    k.node_sum1 = k.inv_sqrt_deg[0:HEADS1, :]
    k.shifted = [k.sb(f"shifted{i}", [P, SUB * HEADS2]) for i in range(2)]
    k.weight = [k.sb(f"weight{i}", [P, SUB * HEADS1]) for i in range(2)]
    k.scaled = [k.sb(f"scaled{i}", [P, HEADS2, SUB, WIN]) for i in range(2)]
    k.iota_i = k.sb("iota_i", [P, WIN], I32)
    k.iota_n = k.sb("iota_n", [P, WIN])
    k.iota_pi = k.sb("iota_pi", [P, 1], I32)
    k.iota_p = k.sb("iota_p", [P, 1])
    k.ident = k.sb("ident", [P, P])
    k.ones = k.sb("ones", [P, P])
    k.lower = k.sb("lower", [P, P])
    k.eps = k.sb("eps", [P, 1])
    k.half = k.sb("half", [P, 1])
    k.head_row = k.sb("head_row", [HEADS2, HEADS2 * P])
    k.head_block = k.sb("head_block", [HEADS1, F])
    k.idx = [k.sb(f"idx{i}", [P, SUB], I32) for i in range(RING)]
    k.g = [k.sb(f"gathered{i}", [P, SUB, 2 * F]) for i in range(RING)]
    k.onehot = [k.sb(f"onehot{i}", [P, SUB, WIN]) for i in range(2)]
    k.msg = [k.sb(f"msg{i}", [P, SUB, F]) for i in range(2)]
    k.dst_row = [k.sb(f"dst_row{i}", [WIN, TILE], I32) for i in range(2)]
    k.onehot_t = [k.sb(f"onehot_t{i}", [WIN, TILE]) for i in range(2)]
    k.window = [k.sb(f"window{i}", [WIN, 2 * F]) for i in range(2)]
    k.zact = [k.sb(f"zact{i}", [P, 2, TILE]) for i in range(2)]
    k.src_row = [k.zact[i][:, 1, :].bitcast(I32) for i in range(2)]
    k.attr = [k.sb(f"attr{i}", [64, TILE]) for i in range(2)]
    k.table1 = nc.dram_tensor("table1", [N, F], F32).ap()
    k.table2 = nc.dram_tensor("table2", [N, 2 * F], F32).ap()
    k.table2r = nc.dram_tensor("table2r", [N, 2 * F], F32).ap()
    k.sums = [[nc.dram_tensor(f"sums{i}_{j}", [N + P, F], F32).ap() for j in range(SUB)] for i in range(2)]
    k.kept1 = nc.dram_tensor("kept1", [T, P, SUB * F], F32).ap()
    k.kept2 = nc.dram_tensor("kept2", [T, P, SUB * 2 * F], F32).ap()

    k.w = {}
    loads = []

    def weight(name, src, shape):
        k.w[name] = k.sb("w_" + name, shape)
        loads.append((k.w[name], src))

    for name in ("L0_gnn_W1", "L0_gnn_W2", "L1_gnn_W", "L2_gnn_Wl", "L2_gnn_Wr", "L2_gnn_res_W",
                 "L3_gnn_k2f_W", "L3_gnn_Wi", "L3_gnn_Wj", "L3_gnn_dense_W"):
        weight(name, ins[name], list(ins[name].shape))
    for name in ("L3_gnn_res_int_W1", "L3_gnn_res_int_W2", "L3_gnn_res_at_W1", "L3_gnn_res_at_W2"):
        for l in range(ins[name].shape[0]):
            weight(f"{name}{l}", ins[name][l], [F, F])
    for name in ("L0_gnn_b1", "L2_gnn_gamma", "L2_gnn_beta", "L2_gnn_bias", "L3_gnn_bi", "L3_gnn_dense_b",
                 "L3_gnn_u"):
        weight(name, ins[name].rearrange("(f o) -> f o", o=1), [F, 1])
    for name in ("L3_gnn_res_int_b1", "L3_gnn_res_int_b2", "L3_gnn_res_at_b1", "L3_gnn_res_at_b2"):
        for l in range(ins[name].shape[0]):
            weight(f"{name}{l}", ins[name][l].rearrange("(f o) -> f o", o=1), [F, 1])
    for name in ("L0_gnn_b2", "L2_gnn_bl", "L2_gnn_br", "L3_gnn_bj"):
        n = ins[name].shape[0]
        weight(name, ins[name].rearrange("(o f) -> o f", o=1).to_broadcast([P, n]), [P, n])
    k.att1 = k.sb("att1", [F, HEADS1])
    k.att1_col = k.sb("att1_col", [F, 1])
    loads.append((k.att1_col, ins["L1_gnn_att"].rearrange("h (c o) -> (h c) o", o=1)))
    k.att2_rows = k.sb("att2_rows", [HEADS2, F])
    k.att2 = k.sb("att2", [F, HEADS2])
    loads.append((k.att2_rows, ins["L2_gnn_att"]))
    loads.append((k.x, ins["x"]))
    loads.append((k.dst_i, ins["dst_edges"]))
    loads.append((k.first_i, ins["dst_first"].to_broadcast([P, T])))

    per_head = F // HEADS1
    with Stage(k, "setup") as st:
        loaded, made, done, flat = st.sem("loaded"), st.sem("made"), st.sem("done"), st.sem("flat")
        cast = st.sem("cast")
        with st.block() as block:
            @block.sync
            def _(sp):
                with nc.allow_non_contiguous_dma(reason="bias and attention columns, first destinations"):
                    for dst, src in loads:
                        full = dst[:, :, :] if len(dst.shape) == 3 else dst[:, :]
                        sp.dma_start(full, src).then_inc(loaded, 16)
                sp.wait_ge(loaded, 16 * len(loads))

            @block.gpsimd
            def _(pool):
                pool.iota(k.iota_i[:, :], pattern=[[1, WIN]], base=0, channel_multiplier=0).then_inc(made, 1)
                pool.iota(k.iota_pi[:, :], pattern=[[0, 1]], base=0, channel_multiplier=1).then_inc(made, 1)
                pool.memset(k.ident[:, :], 0.0).then_inc(flat, 1)
                pool.memset(k.ones[:, :], 1.0)
                pool.memset(k.lower[:, :], 1.0)
                pool.memset(k.eps[:, :], LN_EPS)
                pool.memset(k.half[:, :], 0.5)
                pool.memset(k.head_block[:, :], 1.0)
                pool.memset(k.head_row[:, :], 1.0).then_inc(flat, 1)
                pool.memset(k.att1[:, :], 1.0).then_inc(flat, 1)
                pool.wait_ge(flat, 3)
                pool.affine_select(out=k.ident[:, :], in_=k.ident[:, :], compare_op=ALU.not_equal, fill=1.0,
                                   base=0, pattern=[[-1, P]], channel_multiplier=1)
                pool.affine_select(out=k.lower[:, :], in_=k.lower[:, :], compare_op=ALU.is_ge, fill=0.0,
                                   base=-1, pattern=[[-1, P]], channel_multiplier=1)
                pool.affine_select(out=k.head_row[:, :], in_=k.head_row[:, :], compare_op=ALU.is_ge, fill=0.0,
                                   base=0, pattern=[[1, HEADS2 * P]], channel_multiplier=-P).then_inc(flat, 1)
                pool.affine_select(out=k.head_block[:, :], in_=k.head_block[:, :], compare_op=ALU.is_ge, fill=0.0,
                                   base=0, pattern=[[1, F]], channel_multiplier=-per_head).then_inc(flat, 1)
                pool.affine_select(out=k.att1[:, :], in_=k.att1[:, :], compare_op=ALU.is_ge, fill=0.0,
                                   base=0, pattern=[[-per_head, HEADS1]], channel_multiplier=1).then_inc(flat, 1)
                pool.wait_ge(flat, 6)
                pool.affine_select(out=k.head_block[:, :], in_=k.head_block[:, :], compare_op=ALU.is_ge, fill=0.0,
                                   base=per_head - 1, pattern=[[-1, F]], channel_multiplier=per_head)
                pool.affine_select(out=k.head_row[:, :], in_=k.head_row[:, :], compare_op=ALU.is_ge, fill=0.0,
                                   base=P - 1, pattern=[[-1, HEADS2 * P]], channel_multiplier=P)
                pool.affine_select(out=k.att1[:, :], in_=k.att1[:, :], compare_op=ALU.is_ge, fill=0.0,
                                   base=per_head - 1, pattern=[[per_head, HEADS1]],
                                   channel_multiplier=-1).then_inc(made, 1)

            @block.tensor
            def _(pe):
                pe.wait_ge(loaded, 16 * len(loads))
                pe.wait_ge(made, 3)
                pe.transpose(k.bank[1][:, 0:HEADS2], k.att2_rows[:, :],
                             k.ident[0:HEADS2, 0:HEADS2]).then_inc(done, 1)

            @block.vector
            def _(dve):
                dve.wait_ge(made, 3)
                dve.tensor_copy(k.iota_n[:, :], k.iota_i[:, :])
                dve.tensor_copy(k.iota_p[:, :], k.iota_pi[:, :])
                dve.wait_ge(loaded, 16 * len(loads))
                dve.tensor_scalar(k.att1[:, :], k.att1[:, :], k.att1_col[:, 0:1], None, ALU.mult)
                dve.tensor_copy(k.first[:, :], k.first_i[:, :])
                dve.tensor_copy(k.dst_f[:, :], k.dst_i[:, :]).then_inc(cast, 1)
                dve.memset(k.win_off[:, :], 0.0)
                dve.memset(k.win_step[:, :], 0.0)
                dve.wait_ge(done, 1)
                dve.tensor_copy(k.att2[:, :], k.bank[1][:, 0:HEADS2])
                dve.wait_ge(cast, 1)
                dve.tensor_scalar(k.pad[:, :], k.dst_f[:, :], 0.0, -BIG, ALU.is_lt, ALU.mult)


def place_windows(k):
    nc, T = k.nc, k.tiles
    with Stage(k, "windows") as st:
        placed, local = st.sem("placed"), st.sem("local")
        with st.block() as block:
            @block.vector
            def _(dve):
                dve.tensor_scalar(k.base[:, :], k.first[:, :], k.win_off[:, 0:1], None, ALU.add).then_inc(placed, 1)
                dve.wait_ge(placed, 1)
                dve.tensor_tensor(k.local[:, :].rearrange("p (t j) -> p t j", j=SUB),
                                  k.dst_f[:, :].rearrange("p (t j) -> p t j", j=SUB),
                                  k.base[:, :].unsqueeze(2).to_broadcast([P, T, SUB]),
                                  ALU.subtract).then_inc(local, 1)
                dve.tensor_scalar(k.base_i[:, :], k.base[:, :], 0.0, float(k.n_nodes - WIN), ALU.max, ALU.min)
                dve.tensor_scalar(k.win_off[:, :], k.win_off[:, :], k.win_step[:, 0:1], None, ALU.add)
                dve.wait_ge(local, 1)
                dve.tensor_scalar(k.member[:, :], k.local[:, :], 0.0, None, ALU.is_ge).then_inc(placed, 1)
                dve.wait_ge(placed, 2)
                dve.scalar_tensor_tensor(out=k.member[:, :], in0=k.local[:, :], scalar=float(WIN),
                                         in1=k.member[:, :], op0=ALU.is_lt, op1=ALU.mult)


def choose_passes(k, n_edges):
    nc = k.nc
    passes = ceil_div(k.n_nodes, WIN)
    place_windows(k)
    with Stage(k, "choice") as st:
        counted, summed, step = st.sem("counted"), st.sem("summed"), st.sem("step")
        with st.block() as block:
            @block.vector
            def _(dve):
                dve.tensor_reduce(k.small[:, 0:1], k.member[:, :], AX.X, ALU.add).then_inc(counted, 1)
                dve.wait_ge(summed, 1)
                dve.tensor_scalar(k.small[:, 1:2], k.bank[0][:, 0:1], float(n_edges), None,
                                  ALU.is_equal).then_inc(step, 1)
                dve.wait_ge(step, 1)
                dve.tensor_scalar(k.passes_i[:, :], k.small[:, 1:2], float(1 - passes), float(passes),
                                  ALU.mult, ALU.add)
                dve.tensor_scalar(k.win_step[:, :], k.small[:, 1:2], float(-WIN), float(WIN), ALU.mult, ALU.add)
                dve.tensor_scalar(k.first[:, :], k.first[:, :], k.small[:, 1:2], None, ALU.mult)

            @block.tensor
            def _(pe):
                pe.wait_ge(counted, 1)
                pe.matmul(k.bank[0][:, 0:1], k.ones[:, :], k.small[:, 0:1], start=True,
                          stop=True).then_inc(summed, 1)
    k.passes = nc.values_load(k.passes_i[0:1, 0:1], min_val=1, max_val=passes,
                              skip_runtime_bounds_check_because="it is 1 or the number of windows")


def reset_windows(k):
    with Stage(k, "rewind") as st:
        with st.block() as block:
            @block.vector
            def _(dve):
                dve.memset(k.win_off[:, :], 0.0)



def chunks(n):
    return [(c, min(c + CHUNK, n)) for c in range(0, n, CHUNK)]


def product_stage(k, name, count, product, engine, take):
    with Stage(k, name) as st:
        ready, taken = st.sem("product_ready"), st.sem("product_taken")

        with st.block() as block:
            @block.tensor
            def _(pe):
                for c in range(count):
                    wait_count(pe, taken, c + 1 - BANKS)
                    product(pe, c, k.bank[c % BANKS]).then_inc(ready, 1)

            def taker(eng):
                for c in range(count):
                    eng.wait_ge(ready, c + 1)
                    take(eng, c, k.bank[c % BANKS]).then_inc(taken, 1)

            if engine == "scalar":
                @block.scalar
                def _(act):
                    taker(act)
            else:
                @block.vector
                def _(dve):
                    taker(dve)


def to_feature_major(k, name, src, dst, func=None, scale=1.0, bias=0.0):
    def product(pe, c, bank):
        lo, hi = chunks(k.n_nodes)[c]
        for b in range(lo // P, hi // P):
            mm = pe.transpose(bank[:, b * P - lo:(b + 1) * P - lo], src[:, b, :], k.ident[:, :])
        return mm

    def take(act, c, bank):
        lo, hi = chunks(k.n_nodes)[c]
        if func is None:
            return act.copy(dst[:, lo:hi], bank[:, 0:hi - lo])
        return act.activation(dst[:, lo:hi], bank[:, 0:hi - lo], func, bias=bias, scale=scale)

    product_stage(k, name, len(chunks(k.n_nodes)), product, "scalar", take)


def add_to_nodes(k, name, src, dst):
    def product(pe, c, bank):
        lo, hi = chunks(k.n_nodes)[c]
        for b in range(lo // P, hi // P):
            mm = pe.transpose(bank[:, b * P - lo:(b + 1) * P - lo], src[:, b * P:(b + 1) * P], k.ident[:, :])
        return mm

    def take(dve, c, bank):
        lo, hi = chunks(k.n_nodes)[c]
        d = dst[:, lo // P:hi // P, :]
        return dve.tensor_tensor(d, d, bank[:, 0:hi - lo].rearrange("p (b f) -> p b f", f=F), ALU.add)

    product_stage(k, name, len(chunks(k.n_nodes)), product, "vector", take)


def linear(k, name, weight, src, take, engine="vector"):
    def product(pe, c, bank):
        lo, hi = chunks(k.n_nodes)[c]
        return pe.matmul(bank[:, 0:hi - lo], weight, src[:, lo:hi], start=True, stop=True)

    product_stage(k, name, len(chunks(k.n_nodes)), product, engine,
                  lambda eng, c, bank: take(eng, chunks(k.n_nodes)[c], bank[:, 0:chunks(k.n_nodes)[c][1] - chunks(k.n_nodes)[c][0]]))


def table_rows(k, name, src, weight, bias, table):
    width = weight.shape[1]
    rows = k.wide[:, :, :].rearrange("p a n -> p (a n)")[:, 0:k.blocks * width]
    def product(pe, c, bank):
        return pe.matmul(bank[:, 0:width], src[:, c * P:(c + 1) * P], weight, start=True, stop=True)

    def take(dve, c, bank):
        d = rows[:, c * width:(c + 1) * width]
        if bias is None:
            return dve.tensor_copy(d, bank[:, 0:width])
        return dve.tensor_tensor(d, bank[:, 0:width], bias, ALU.add)

    product_stage(k, name, k.blocks, product, "vector", take)
    store_table(k, name, rows.rearrange("p (b f) -> p b f", f=width), table)


def store_table(k, name, rows, table):
    with Stage(k, name + "_store") as st:
        stored = st.sem("stored")
        with st.block() as block:
            @block.sync
            def _(sp):
                sp.dma_start(table.rearrange("(b p) f -> p b f", p=P), rows).then_inc(stored, 16)
                sp.wait_ge(stored, 16)


def layer_norm(k, name, src, dst, relu):
    B = k.blocks
    sq = k.wide[:, 0, :].rearrange("p (b f) -> p b f", f=F)
    cen = k.wide[:, 1, :].rearrange("p (b f) -> p b f", f=F)

    def wide(stat):
        return stat[:, :].unsqueeze(2).to_broadcast([P, B, F])

    with Stage(k, name) as st:
        step, squared, rooted = st.sem("step"), st.sem("squared"), st.sem("rooted")
        with st.block() as block:
            @block.vector
            def _(dve):
                dve.tensor_reduce(k.stat[:, :], src[:, :, :], AX.X, ALU.add).then_inc(step, 1)
                dve.wait_ge(step, 1)
                dve.tensor_scalar(k.stat[:, :], k.stat[:, :], 1.0 / F, None, ALU.mult).then_inc(step, 1)
                dve.wait_ge(step, 2)
                dve.tensor_tensor(cen, src[:, :, :], wide(k.stat), ALU.subtract).then_inc(step, 1)
                dve.wait_ge(squared, 1)
                dve.tensor_reduce(k.stat[:, :], sq, AX.X, ALU.add).then_inc(step, 1)
                dve.wait_ge(rooted, 1)
                dve.reciprocal(k.stat2[:, :], k.stat2[:, :]).then_inc(step, 1)
                dve.wait_ge(step, 5)
                if relu:
                    dve.scalar_tensor_tensor(out=dst[:, :, :], in0=cen, scalar=0.0, in1=wide(k.stat2),
                                             op0=ALU.max, op1=ALU.mult)
                else:
                    dve.tensor_tensor(dst[:, :, :], cen, wide(k.stat2), ALU.mult)

            @block.scalar
            def _(act):
                act.wait_ge(step, 3)
                act.square(sq, cen).then_inc(squared, 1)
                act.wait_ge(step, 4)
                act.activation(k.stat2[:, :], k.stat[:, :], ACT.Sqrt, bias=k.eps[:, 0:1],
                               scale=1.0 / F).then_inc(rooted, 1)


def vector_stage(k, name, *ops):
    with Stage(k, name) as st:
        step = st.sem("step")
        with st.block() as block:
            @block.vector
            def _(dve):
                for n, op in enumerate(ops):
                    wait_count(dve, step, n)
                    op(dve).then_inc(step, 1)



def gathered(k, slot, width):
    return k.g[slot][:, :, :].rearrange("p j f -> p (j f)")[:, 0:SUB * width].rearrange(
        "p (j f) -> p j f", f=width)


def load_indices(k, sp, idx_loaded, t):
    sp.dma_start(k.idx[t.slot][:, :],
                 k.ins["src_rows"][bass.ds(t.t, 1), :, :].rearrange("o p j -> (o p) j")).then_inc(
                     idx_loaded[t.slot], 16)


def gather(k, pool, table, width, idx_loaded, gathers_begun, rows_loaded, t):
    pool.wait_ge(idx_loaded[t.slot], (t.rounds + 1) * 16)
    pool.sem_inc(gathers_begun, 1)
    g = gathered(k, t.slot, width)
    for j in range(SUB):
        pool.indirect_dma_start(out=g[:, j, :], out_offset=None, in_=table,
                                in_offset=bass.IndirectOffsetOnAxis(ap=k.idx[t.slot][:, j:j + 1], axis=0)
                                ).then_inc(rows_loaded[t.slot][j], 16)


def gather_sems(st):
    idx_loaded = [st.sem(f"idx_loaded{i}") for i in range(RING)]
    rows_loaded = [[st.pool_dma_sem(f"rows_loaded{i}_{j}") for j in range(SUB)] for i in range(RING)]
    return idx_loaded, st.sem("gathers_begun"), rows_loaded


def make_onehot(k, dve, t):
    return dve.tensor_tensor(k.onehot[t.two][:, :, :],
                             k.local[:, bass.ds(t.t * SUB, SUB)].unsqueeze(2).to_broadcast([P, SUB, WIN]),
                             k.iota_n[:, :].unsqueeze(1).to_broadcast([P, SUB, WIN]), ALU.is_equal)


def window_base(k, eng, t):
    return eng.value_load(k.base_i[0:1, bass.ds(t.t, 1)], min_val=0, max_val=k.n_nodes - WIN)


def repeated(k, one_pass):
    reset_windows(k)
    with k.nc.Fori(0, k.passes):
        place_windows(k)
        one_pass()


def count_degrees(k):
    def one_pass():
        with Stage(k, "deg") as st:
            onehot_ready, sums_ready, added = st.sem("onehot_ready"), st.sem("sums_ready"), st.sem("added")
            with st.block() as block:
                @block.tensor
                def _(pe):
                    def sums(t):
                        pe.wait_ge(onehot_ready, t.t + 1)
                        wait_count(pe, added, t.t - 1)
                        for j in range(SUB):
                            mm = pe.matmul(k.bank[t.two][:, 0:WIN], k.ones[:, :], k.onehot[t.two][:, j, :],
                                           start=(j == 0), stop=(j == SUB - 1))
                        mm.then_inc(sums_ready, 1)
                    over_tiles(pe, k.tiles, [(0, sums)])

                @block.vector
                def _(dve):
                    def onehot(t):
                        wait_count(dve, sums_ready, t.t - 1)
                        make_onehot(k, dve, t).then_inc(onehot_ready, 1)

                    def add(t):
                        at = window_base(k, dve, t)
                        dve.wait_ge(sums_ready, t.t + 1)
                        wait_count(dve, added, t.t)
                        a = k.acc[:, 0, bass.ds(at, WIN)]
                        dve.tensor_tensor(a, a, k.bank[t.two][:, 0:WIN], ALU.add).then_inc(added, 1)
                    over_tiles(dve, k.tiles, [(0, onehot), (1, add)])
    repeated(k, one_pass)


def sum_neighbours(k, name, table):
    def one_pass():
        with Stage(k, name) as st:
            idx_loaded, gathers_begun, rows_loaded = gather_sems(st)
            onehot_ready, sums_ready, added = st.sem("onehot_ready"), st.sem("sums_ready"), st.sem("added")
            with st.block() as block:
                @block.sync
                def _(sp):
                    def indices(t):
                        wait_count(sp, sums_ready, t.t + 1 - RING)
                        load_indices(k, sp, idx_loaded, t)
                    over_tiles(sp, k.tiles, [(0, indices)])

                @block.gpsimd
                def _(pool):
                    def rows(t):
                        wait_count(pool, sums_ready, t.t + 1 - RING)
                        gather(k, pool, table, F, idx_loaded, gathers_begun, rows_loaded, t)
                    over_tiles(pool, k.tiles, [(0, rows)])

                @block.tensor
                def _(pe):
                    def sums(t):
                        pe.wait_ge(onehot_ready, t.t + 1)
                        wait_count(pe, added, t.t - 1)
                        g = gathered(k, t.slot, F)
                        for j in range(SUB):
                            pe.wait_ge(rows_loaded[t.slot][j], (t.rounds + 1) * 16)
                            mm = pe.matmul(k.bank[t.two][:, 0:WIN], g[:, j, :], k.onehot[t.two][:, j, :],
                                           start=(j == 0), stop=(j == SUB - 1))
                        mm.then_inc(sums_ready, 1)
                    over_tiles(pe, k.tiles, [(0, sums)])

                @block.vector
                def _(dve):
                    def onehot(t):
                        wait_count(dve, sums_ready, t.t - 1)
                        make_onehot(k, dve, t).then_inc(onehot_ready, 1)

                    def add(t):
                        at = window_base(k, dve, t)
                        dve.wait_ge(sums_ready, t.t + 1)
                        wait_count(dve, added, t.t)
                        a = k.acc[:, 0, bass.ds(at, WIN)]
                        dve.tensor_tensor(a, a, k.bank[t.two][:, 0:WIN], ALU.add).then_inc(added, 1)
                    over_tiles(dve, k.tiles, [(0, onehot), (1, add)])
    repeated(k, one_pass)


def half_rounds(t):
    return t.rounds * 2 + (1 if t.slot >= 2 else 0)


def scatter_filtered(k, table):
    attr = k.ins["attr_rows"]
    depth = attr.shape[1]

    def one_pass():
        with Stage(k, "filt") as st:
            dst_loaded = [st.sem(f"dst_loaded{i}") for i in range(2)]
            win_loaded = [st.sem(f"win_loaded{i}") for i in range(2)]
            attr_loaded = [st.sem(f"attr_loaded{i}") for i in range(2)]
            src_loaded = [st.sem(f"src_loaded{i}") for i in range(2)]
            scattered = [[st.pool_dma_sem(f"scattered{i}_{j}") for j in range(SUB)] for i in range(2)]
            onehot_t_ready, filter_ready, rows_ready = (st.sem("onehot_t_ready"), st.sem("filter_ready"),
                                                        st.sem("rows_ready"))
            copied, msg_ready, same_ready = st.sem("copied"), st.sem("msg_ready"), st.sem("same_ready")
            before_ready, row_picked, row_ready = st.sem("before_ready"), st.sem("row_picked"), st.sem("row_ready")
            joined, out_ready, begun = st.sem("joined"), st.sem("out_ready"), st.sem("scatters_begun")

            def same(t):
                return gathered(k, t.two, F)

            def out_rows(t):
                return k.g[t.slot][:, :, :].rearrange("p j f -> p (j f)")[:, SUB * F:].rearrange(
                    "p (j f) -> p j f", f=F)

            with st.block() as block:
                @block.sync
                def _(sp):
                    def loads(t):
                        at = window_base(k, sp, t)
                        wait_count(sp, onehot_t_ready, t.t - 1)
                        sp.dma_start(k.dst_row[t.two][:, :],
                                     k.ins["dst_rows"][bass.ds(t.t, 1), :].to_broadcast([WIN, TILE])).then_inc(
                                         dst_loaded[t.two], 16)
                        wait_count(sp, rows_ready, t.t - 1)
                        sp.dma_start(k.window[t.two][:, 0:F], table[bass.ds(at, WIN), :]).then_inc(
                            win_loaded[t.two], 16)
                        wait_count(sp, filter_ready, t.t - 1)
                        sp.dma_start(k.attr[t.two][:, :],
                                     attr[bass.ds(t.t, 1), :, :].rearrange("o c e -> (o c) e")).then_inc(
                                         attr_loaded[t.two], 16)
                        wait_count(sp, before_ready, t.t - 1)
                        sp.dma_start(k.src_row[t.two][:, :],
                                     k.ins["src_flat"][bass.ds(t.t, 1), :].to_broadcast([P, TILE])).then_inc(
                                         src_loaded[t.two], 16)
                    over_tiles(sp, k.tiles, [(0, loads)])

                @block.tensor
                def _(pe):
                    def filters(t):
                        pe.wait_ge(attr_loaded[t.two], (half_rounds(t) + 1) * 16)
                        wait_count(pe, msg_ready, t.t - 1)
                        for j in range(SUB):
                            mm = pe.matmul(k.bank[t.two][:, j * F:(j + 1) * F],
                                           k.attr[t.two][0:depth, j * P:(j + 1) * P],
                                           k.w["L3_gnn_k2f_W"][:, :], start=True, stop=True)
                        mm.then_inc(filter_ready, 1)
                        pe.wait_ge(onehot_t_ready, t.t + 1)
                        pe.wait_ge(win_loaded[t.two], (half_rounds(t) + 1) * 16)
                        wait_count(pe, copied, t.t - 1)
                        for j in range(SUB):
                            mm = pe.matmul(k.bank[2 + t.two][:, j * F:(j + 1) * F],
                                           k.onehot_t[t.two][:, j * P:(j + 1) * P], k.window[t.two][:, 0:F],
                                           start=True, stop=True)
                        mm.then_inc(rows_ready, 1)

                    def join(t):
                        pe.wait_ge(msg_ready, t.t + 1)
                        pe.wait_ge(same_ready, t.t + 1)
                        wait_count(pe, out_ready, t.t - 1)
                        for j in range(SUB):
                            mm = pe.matmul(k.bank[4 + t.two][:, j * F:(j + 1) * F], same(t)[:, j, :],
                                           k.msg[t.two][:, j, :], start=True, stop=True)
                        mm.then_inc(joined, 1)
                    over_tiles(pe, k.tiles, [(0, filters), (1, join)])

                @block.scalar
                def _(act):
                    def copy_rows(t):
                        act.wait_ge(rows_ready, t.t + 1)
                        wait_count(act, msg_ready, t.t - 1)
                        act.copy(k.zact[t.two][:, 0, :], k.bank[2 + t.two][:, :]).then_inc(copied, 1)

                    def copy_out(t):
                        act.wait_ge(joined, t.t + 1)
                        for j in range(SUB):
                            wait_count(act, scattered[t.two][j], (half_rounds(t) - 1) * 16)
                        act.copy(out_rows(t).rearrange("p j f -> p (j f)"),
                                 k.bank[4 + t.two][:, :]).then_inc(out_ready, 1)
                    over_tiles(act, k.tiles, [(0, copy_rows), (1, copy_out)])

                @block.vector
                def _(dve):
                    def onehots(t):
                        wait_count(dve, rows_ready, t.t - 1)
                        dve.wait_ge(dst_loaded[t.two], (half_rounds(t) + 1) * 16)
                        dve.tensor_scalar(k.onehot_t[t.two][:, :], k.dst_row[t.two][:, :],
                                          k.base[0:WIN, bass.ds(t.t, 1)], k.iota_p[0:WIN, 0:1],
                                          ALU.subtract, ALU.is_equal).then_inc(onehot_t_ready, 1)

                    def messages(t):
                        mine = k.src_f[:, bass.ds(t.t * SUB, SUB)]
                        row = k.src_row[t.two][:, :].rearrange("p (j e) -> p j e", e=P)
                        wait_count(dve, joined, t.t - 1)
                        dve.wait_ge(src_loaded[t.two], (half_rounds(t) + 1) * 16)
                        dve.tensor_tensor(same(t), row, mine.unsqueeze(2).to_broadcast([P, SUB, P]),
                                          ALU.is_equal).then_inc(same_ready, 1)
                        dve.wait_ge(same_ready, t.t + 1)
                        wait_count(dve, row_picked, t.t)
                        dve.tensor_tensor(k.earlier[:, :, :], same(t), k.lower[:, :].unsqueeze(1).to_broadcast(
                            [P, SUB, P]), ALU.mult).then_inc(row_picked_in, 1)
                        dve.wait_ge(copied, t.t + 1)
                        dve.wait_ge(filter_ready, t.t + 1)
                        dve.tensor_tensor(k.msg[t.two][:, :, :],
                                          k.zact[t.two][:, 0, :].rearrange("p (j f) -> p j f", f=F),
                                          k.bank[t.two][:, :].rearrange("p (j f) -> p j f", f=F),
                                          ALU.mult).then_inc(msg_ready, 1)
                        dve.wait_ge(row_picked_in, t.t + 1)
                        dve.tensor_reduce(k.picked[:, 0:SUB], k.earlier[:, :, :], AX.X, ALU.add).then_inc(
                            before_ready, 1)
                        dve.tensor_scalar(k.picked[:, SUB:2 * SUB], mine, -1.0, k.spare[:, 0:1],
                                          ALU.mult, ALU.add).then_inc(away_ready, 1)
                        dve.wait_ge(away_ready, t.t + 1)
                        dve.scalar_tensor_tensor(out=k.picked[:, 2 * SUB:3 * SUB], in0=k.picked[:, 0:SUB], scalar=0.5,
                                                 in1=k.picked[:, SUB:2 * SUB], op0=ALU.is_gt,
                                                 op1=ALU.mult).then_inc(row_picked, 1)
                        dve.wait_ge(row_picked, t.t + 1)
                        for j in range(SUB):
                            wait_count(dve, scattered[t.two][j], (half_rounds(t) - 1) * 16)
                        dve.tensor_tensor(k.idx[t.slot][:, :], k.picked[:, 2 * SUB:3 * SUB], mine,
                                          ALU.add).then_inc(row_ready, 1)
                    row_picked_in, away_ready = st.sem("earlier_ready"), st.sem("away_ready")
                    over_tiles(dve, k.tiles, [(0, onehots), (1, messages)])

                @block.gpsimd
                def _(pool):
                    def scatter(t):
                        pool.wait_ge(out_ready, t.t + 1)
                        pool.wait_ge(row_ready, t.t + 1)
                        for j in range(SUB):
                            wait_count(pool, scattered[t.two][j], half_rounds(t) * 16)
                        pool.sem_inc(begun, 1)
                        for j in range(SUB):
                            pool.indirect_dma_start(
                                out=k.sums[t.two][j], out_offset=bass.IndirectOffsetOnAxis(
                                    ap=k.idx[t.slot][:, j:j + 1], axis=0),
                                in_=out_rows(t)[:, j, :], in_offset=None,
                                compute_op=ALU.add).then_inc(scattered[t.two][j], 16)
                    over_tiles(pool, k.tiles, [(1, scatter)])
                    for two in range(2):
                        for j in range(SUB):
                            pool.wait_ge(scattered[two][j], 16 * ceil_div(k.tiles - two, 2))
    repeated(k, one_pass)


def score_edges(k, name, heads, table, table_dst, kept):
    nc = k.nc
    gat = name == "gat"
    width = F * (2 if gat else 1)
    zs = width // F
    att = k.att2 if gat else k.att1
    cols = SUB * heads

    def z_bank(t, h):
        return k.bank[h * 2 + t.two]

    def one_pass():
        with Stage(k, name) as st:
            idx_loaded, gathers_begun, rows_loaded = gather_sems(st)
            dst_loaded = [st.sem(f"dst_loaded{i}") for i in range(2)]
            win_loaded = [st.sem(f"win_loaded{i}") for i in range(2)]
            stored = [st.sem(f"stored{i}") for i in range(RING)]
            onehot_t_ready, z_ready, act_ready = st.sem("onehot_t_ready"), st.sem("z_ready"), st.sem("act_ready")
            slope_ready, score_ready = st.sem("slope_ready"), st.sem("score_ready")
            masked, added = st.sem("masked"), st.sem("added")
            onehot_ready, spread, turned = st.sem("onehot_ready"), st.sem("spread"), st.sem("turned")
            tops, tops_turned, tops_merged, best = (st.sem("tops"), st.sem("tops_turned"),
                                                    st.sem("tops_merged"), st.sem("best"))
            outside_ready, exclusive = st.sem("outside_ready"), st.sem("exclusive")
            with st.block() as block:
                @block.sync
                def _(sp):
                    def loads(t):
                        at = window_base(k, sp, t)
                        wait_count(sp, onehot_t_ready, t.t - 1)
                        sp.dma_start(k.dst_row[t.two][:, :],
                                     k.ins["dst_rows"][bass.ds(t.t, 1), :].to_broadcast([WIN, TILE])).then_inc(
                                         dst_loaded[t.two], 16)
                        wait_count(sp, z_ready, t.t - 1)
                        sp.dma_start(k.window[t.two][:, 0:width], table_dst[bass.ds(at, WIN), :]).then_inc(
                            win_loaded[t.two], 16)
                        wait_count(sp, z_ready, t.t + 1 - RING)
                        load_indices(k, sp, idx_loaded, t)

                    def keep(t):
                        for j in range(SUB):
                            sp.wait_ge(rows_loaded[t.slot][j], (t.rounds + 1) * 16)
                        sp.dma_start(kept[bass.ds(t.t, 1), :, :].rearrange("o p f -> (o p) f"),
                                     gathered(k, t.slot, width).rearrange("p j f -> p (j f)")).then_inc(
                                         stored[t.slot], 16)
                    over_tiles(sp, k.tiles, [(0, loads), (2, keep)])
                    for slot in range(RING):
                        sp.wait_ge(stored[slot], 16 * ceil_div(k.tiles - slot, RING))

                @block.gpsimd
                def _(pool):
                    def rows(t):
                        wait_count(pool, z_ready, t.t + 1 - RING)
                        wait_count(pool, stored[t.slot], t.rounds * 16)
                        gather(k, pool, table, width, idx_loaded, gathers_begun, rows_loaded, t)
                    over_tiles(pool, k.tiles, [(0, rows)])

                @block.tensor
                def _(pe):
                    def sums(t):
                        pe.wait_ge(win_loaded[t.two], (half_rounds(t) + 1) * 16)
                        pe.wait_ge(onehot_t_ready, t.t + 1)
                        wait_count(pe, act_ready, t.t - 1)
                        g = gathered(k, t.slot, width)
                        for j in range(SUB):
                            pe.wait_ge(rows_loaded[t.slot][j], (t.rounds + 1) * 16)
                            for h in range(zs):
                                pe.matmul(z_bank(t, h)[:, j * P:(j + 1) * P], g[:, j, h * F:(h + 1) * F],
                                          k.ident[:, :], is_transpose=True, start=(j == 0), stop=False,
                                          skip_group_check=True)
                        for h in range(zs):
                            mm = pe.matmul(z_bank(t, h)[:, :], k.window[t.two][:, h * F:(h + 1) * F],
                                           k.onehot_t[t.two][:, :], start=False, stop=True,
                                           skip_group_check=True)
                        mm.then_inc(z_ready, 1)

                    def scores(t):
                        pe.wait_ge(act_ready, t.t + 1)
                        wait_count(pe, spread if gat else masked, t.t - 1)
                        for h in range(zs):
                            for j in range(SUB):
                                lhs = k.zact[t.two][:, h, j * P:(j + 1) * P]
                                if gat:
                                    mm = pe.matmul(k.bank[4 + t.two][:, h * SUB + j:h * SUB + j + 1], lhs,
                                                   att[:, h:h + 1], start=True, stop=True)
                                else:
                                    mm = pe.matmul(k.bank[4 + t.two][:, j * heads:(j + 1) * heads], lhs,
                                                   att[:, :], start=True, stop=True)
                        mm.then_inc(score_ready, 1)

                    def turn(t):
                        pe.wait_ge(exclusive, t.t + 1)
                        wait_count(pe, tops, t.t)
                        for h in range(heads):
                            mm = pe.transpose(k.bank[6][:, h * P:(h + 1) * P],
                                              k.msg[t.two][:, h, :], k.ident[:, :])
                        mm.then_inc(turned, 1)

                    def turn_tops(t):
                        pe.wait_ge(tops, t.t + 1)
                        wait_count(pe, best, t.t)
                        pe.transpose(k.bank[7][0:heads, 0:P], k.tops[:, t.two, :],
                                     k.ident[:, :]).then_inc(tops_turned, 1)
                    stages = [(0, sums), (2 if gat else 1, scores)]
                    if gat:
                        stages += [(3, turn), (4, turn_tops)]
                    over_tiles(pe, k.tiles, stages)

                @block.scalar
                def _(act):
                    def activate(t):
                        act.wait_ge(z_ready, t.t + 1)
                        wait_count(act, score_ready, t.t - 1)
                        if gat:
                            for h in range(zs):
                                a = act.mul(k.zact[t.two][:, h, :], z_bank(t, h)[:, :], 0.2)
                            a.then_inc(slope_ready, 1)
                        else:
                            act.activation(k.zact[t.two][:, 0, :], z_bank(t, 0)[:, :],
                                           ACT.Tanh).then_inc(act_ready, 1)
                    over_tiles(act, k.tiles, [(0, activate)])

                @block.vector
                def _(dve):
                    def onehots(t):
                        wait_count(dve, z_ready, t.t - 1)
                        dve.wait_ge(dst_loaded[t.two], (half_rounds(t) + 1) * 16)
                        dve.tensor_scalar(k.onehot_t[t.two][:, :], k.dst_row[t.two][:, :],
                                          k.base[0:WIN, bass.ds(t.t, 1)], k.iota_p[0:WIN, 0:1],
                                          ALU.subtract, ALU.is_equal).then_inc(onehot_t_ready, 1)

                    def leaky(t):
                        dve.wait_ge(slope_ready, t.t + 1)
                        for h in range(zs):
                            za = k.zact[t.two][:, h, :]
                            m = dve.tensor_tensor(za, za, z_bank(t, h)[:, :], ALU.max)
                        m.then_inc(act_ready, 1)

                    def pick(t):
                        dve.wait_ge(score_ready, t.t + 1)
                        s = k.bank[4 + t.two][:, 0:cols]
                        m = k.member[:, bass.ds(t.t * SUB, SUB)]
                        mine = k.scores[:, bass.ds(t.t * cols, cols)]
                        picked_s = k.picked[:, 0:cols]
                        if gat:
                            s = s.rearrange("p (h j) -> p h j", j=SUB)
                            m = m.unsqueeze(1).to_broadcast([P, heads, SUB])
                            ps = picked_s.rearrange("p (h j) -> p h j", j=SUB)
                        else:
                            s = s.rearrange("p (j h) -> p j h", h=heads)
                            m = m.unsqueeze(2).to_broadcast([P, SUB, heads])
                            ps = picked_s.rearrange("p (j h) -> p j h", h=heads)
                        wait_count(dve, added, t.t)
                        dve.tensor_tensor(ps, s, m, ALU.mult).then_inc(masked, 1)
                        if gat:
                            one = k.onehot[t.two]
                            make_onehot(k, dve, t).then_inc(onehot_ready, 1)
                            dve.wait_ge(onehot_ready, t.t + 1)
                            dve.tensor_scalar(k.msg[t.two][:, 2, :], one[:, :, :].rearrange("p j n -> p (j n)"),
                                              BIG, -BIG, ALU.mult, ALU.add).then_inc(outside_ready, 1)
                            wait_count(dve, turned, t.t - 1)
                            ms = k.msg[t.two][:, 0:heads, :].rearrange("p h (j n) -> p h j n", n=WIN)
                            dve.tensor_tensor(ms, one[:, :, :].unsqueeze(1).to_broadcast([P, heads, SUB, WIN]),
                                              s.unsqueeze(3).to_broadcast([P, heads, SUB, WIN]),
                                              ALU.mult).then_inc(spread, 1)
                            dve.wait_ge(spread, t.t + 1)
                            dve.wait_ge(outside_ready, t.t + 1)
                            dve.tensor_tensor(k.msg[t.two][:, 0:heads, :], k.msg[t.two][:, 0:heads, :],
                                              k.msg[t.two][:, 2, :].unsqueeze(1).to_broadcast([P, heads, P]),
                                              ALU.add).then_inc(exclusive, 1)
                        dve.wait_ge(masked, t.t + 1)
                        dve.tensor_tensor(mine, mine, picked_s, ALU.add).then_inc(added, 1)

                    def top(t):
                        dve.wait_ge(turned, t.t + 1)
                        wait_count(dve, tops_turned, t.t - 1)
                        dve.tensor_reduce(k.tops[:, t.two, :],
                                          k.bank[6][:, 0:heads * P].rearrange("p (h e) -> p h e", e=P),
                                          AX.X, ALU.max).then_inc(tops, 1)

                    def best_of_nodes(t):
                        at = window_base(k, dve, t)
                        dve.wait_ge(tops_turned, t.t + 1)
                        wait_count(dve, best, t.t)
                        dve.tensor_reduce(k.tile_top[:, :], k.bank[7][0:heads, 0:P].rearrange(
                            "h (j n) -> h n j", n=WIN), AX.X, ALU.max).then_inc(tops_merged, 1)
                        dve.wait_ge(tops_merged, t.t + 1)
                        m = k.node_top[:, bass.ds(at, WIN)]
                        dve.tensor_tensor(m, m, k.tile_top[:, :], ALU.max).then_inc(best, 1)
                    if gat:
                        over_tiles(dve, k.tiles, [(0, onehots), (1, leaky), (2, pick), (3, top),
                                                  (4, best_of_nodes)])
                    else:
                        over_tiles(dve, k.tiles, [(0, onehots), (1, pick)])
    repeated(k, one_pass)


def kept_rows(k, sp, kept, width, rows_loaded, t):
    sp.dma_start(gathered(k, t.slot, width).rearrange("p j f -> p (j f)"),
                 kept[bass.ds(t.t, 1), :, :].rearrange("o p f -> (o p) f")).then_inc(rows_loaded[t.slot], 16)


def weigh_additive(k):
    heads, per_head = HEADS1, F // HEADS1

    def one_pass():
        with Stage(k, "addw") as st:
            rows_loaded = [st.sem(f"rows_loaded{i}") for i in range(RING)]
            weight_ready, onehot_ready, msg_ready = st.sem("weight_ready"), st.sem("onehot_ready"), st.sem("msg_ready")
            sums_ready, added = st.sem("sums_ready"), st.sem("added")
            with st.block() as block:
                @block.sync
                def _(sp):
                    def loads(t):
                        wait_count(sp, msg_ready, t.t + 1 - RING)
                        kept_rows(k, sp, k.kept1, F, rows_loaded, t)
                    over_tiles(sp, k.tiles, [(0, loads)])

                @block.scalar
                def _(act):
                    def weights(t):
                        wait_count(act, sums_ready, t.t - 1)
                        act.activation(k.weight[t.two][:, :],
                                       k.scores[:, bass.ds(t.t * SUB * heads, SUB * heads)],
                                       ACT.Exp).then_inc(weight_ready, 1)
                    over_tiles(act, k.tiles, [(0, weights)])

                @block.tensor
                def _(pe):
                    def sums(t):
                        pe.wait_ge(msg_ready, t.t + 1)
                        pe.wait_ge(onehot_ready, t.t + 1)
                        pe.wait_ge(weight_ready, t.t + 1)
                        wait_count(pe, added, t.t - 1)
                        for j in range(SUB):
                            pe.matmul(k.bank[t.two][:, 0:WIN], k.msg[t.two][:, j, :],
                                      k.onehot[t.two][:, j, :], start=(j == 0), stop=(j == SUB - 1))
                        for j in range(SUB):
                            mm = pe.matmul(k.bank[t.two][0:heads, WIN:2 * WIN],
                                           k.weight[t.two][:, j * heads:(j + 1) * heads], k.onehot[t.two][:, j, :], start=(j == 0), stop=(j == SUB - 1))
                        mm.then_inc(sums_ready, 1)
                    over_tiles(pe, k.tiles, [(0, sums)])

                @block.vector
                def _(dve):
                    def messages(t):
                        wait_count(dve, sums_ready, t.t - 1)
                        make_onehot(k, dve, t).then_inc(onehot_ready, 1)
                        dve.wait_ge(weight_ready, t.t + 1)
                        dve.wait_ge(rows_loaded[t.slot], (t.rounds + 1) * 16)
                        g = gathered(k, t.slot, F).rearrange("p j (h c) -> p (j h) c", h=heads)
                        dve.tensor_tensor(k.msg[t.two][:, :, :].rearrange("p j (h c) -> p (j h) c", h=heads), g,
                                          k.weight[t.two][:, :].unsqueeze(2).to_broadcast([P, SUB * heads, per_head]),
                                          ALU.mult).then_inc(msg_ready, 1)

                    def add(t):
                        at = window_base(k, dve, t)
                        dve.wait_ge(sums_ready, t.t + 1)
                        wait_count(dve, added, t.t)
                        a = k.acc[:, 0, bass.ds(at, WIN)]
                        dve.tensor_tensor(a, a, k.bank[t.two][:, 0:WIN], ALU.add)
                        z = k.node_sum1[:, bass.ds(at, WIN)]
                        dve.tensor_tensor(z, z, k.bank[t.two][0:heads, WIN:2 * WIN], ALU.add).then_inc(added, 1)
                    over_tiles(dve, k.tiles, [(0, messages), (1, add)])
    repeated(k, one_pass)


def weigh_gat(k):
    heads = HEADS2
    cols = heads * SUB

    def one_pass():
        with Stage(k, "gatw") as st:
            rows_loaded = [st.sem(f"rows_loaded{i}") for i in range(RING)]
            onehot_ready, spread, shift, arg = (st.sem("onehot_ready"), st.sem("spread"), st.sem("shift"),
                                                st.sem("arg"))
            arg_ready, weight_ready, scaled_ready = st.sem("arg_ready"), st.sem("weight_ready"), st.sem("scaled_ready")
            sums_ready, added = st.sem("sums_ready"), st.sem("added")
            with st.block() as block:
                @block.sync
                def _(sp):
                    def loads(t):
                        wait_count(sp, sums_ready, t.t + 1 - RING)
                        kept_rows(k, sp, k.kept2, 2 * F, rows_loaded, t)
                    over_tiles(sp, k.tiles, [(0, loads)])

                @block.scalar
                def _(act):
                    def weights(t):
                        act.wait_ge(arg_ready, t.t + 1)
                        act.activation(k.weight[t.two][:, 0:cols], k.shifted[t.two][:, :],
                                       ACT.Exp).then_inc(weight_ready, 1)
                    over_tiles(act, k.tiles, [(0, weights)])

                @block.tensor
                def _(pe):
                    def sums(t):
                        pe.wait_ge(scaled_ready, t.t + 1)
                        pe.wait_ge(onehot_ready, t.t + 1)
                        pe.wait_ge(weight_ready, t.t + 1)
                        pe.wait_ge(rows_loaded[t.slot], (t.rounds + 1) * 16)
                        wait_count(pe, added, t.t - 1)
                        g = gathered(k, t.slot, 2 * F)
                        for h in range(heads):
                            for j in range(SUB):
                                pe.matmul(k.bank[t.two][:, h * WIN:(h + 1) * WIN], g[:, j, h * F:(h + 1) * F],
                                          k.scaled[t.two][:, h, j, :], start=(j == 0), stop=(j == SUB - 1))
                        w = k.weight[t.two][:, 0:cols].rearrange("p (h j) -> p h j", j=SUB)
                        for j in range(SUB):
                            mm = pe.matmul(k.bank[t.two][0:heads, heads * WIN:(heads + 1) * WIN], w[:, :, j],
                                           k.onehot[t.two][:, j, :], start=(j == 0), stop=(j == SUB - 1))
                        mm.then_inc(sums_ready, 1)
                    over_tiles(pe, k.tiles, [(1, sums)])

                @block.vector
                def _(dve):
                    def arguments(t):
                        at = window_base(k, dve, t)
                        wait_count(dve, sums_ready, t.t - 1)
                        make_onehot(k, dve, t).then_inc(onehot_ready, 1)
                        dve.wait_ge(onehot_ready, t.t + 1)
                        sc = k.scaled[t.two][:, :, :, :]
                        dve.tensor_tensor(sc, k.onehot[t.two][:, :, :].unsqueeze(1).to_broadcast([P, heads, SUB, WIN]),
                                          k.wide[:, :, bass.ds(at, WIN)].unsqueeze(2).to_broadcast([P, heads, SUB, WIN]),
                                          ALU.mult).then_inc(spread, 1)
                        dve.wait_ge(spread, t.t + 1)
                        wait_count(dve, arg_ready, t.t)
                        dve.tensor_reduce(k.picked[:, 0:cols], sc.rearrange("p h j n -> p (h j) n"), AX.X,
                                          ALU.add).then_inc(shift, 1)
                        dve.wait_ge(shift, t.t + 1)
                        dve.tensor_tensor(k.shifted[t.two][:, :], k.scores[:, bass.ds(t.t * cols, cols)],
                                          k.picked[:, 0:cols], ALU.subtract).then_inc(arg, 1)
                        dve.wait_ge(arg, t.t + 1)
                        dve.tensor_scalar(k.shifted[t.two][:, :], k.shifted[t.two][:, :], 1.0, None,
                                          ALU.min).then_inc(arg_ready, 1)

                    def scale(t):
                        dve.wait_ge(weight_ready, t.t + 1)
                        w = k.weight[t.two][:, 0:cols].rearrange("p (h j) -> p h j", j=SUB)
                        dve.tensor_tensor(k.scaled[t.two][:, :, :, :],
                                          k.onehot[t.two][:, :, :].unsqueeze(1).to_broadcast([P, heads, SUB, WIN]),
                                          w.unsqueeze(3).to_broadcast([P, heads, SUB, WIN]),
                                          ALU.mult).then_inc(scaled_ready, 1)

                    def add(t):
                        at = window_base(k, dve, t)
                        dve.wait_ge(sums_ready, t.t + 1)
                        wait_count(dve, added, t.t)
                        a = k.acc[:, :, bass.ds(at, WIN)]
                        dve.tensor_tensor(a, a, k.bank[t.two][:, 0:heads * WIN].rearrange(
                            "p (a n) -> p a n", n=WIN), ALU.add)
                        z = k.node_sum[:, bass.ds(at, WIN)]
                        dve.tensor_tensor(z, z, k.bank[t.two][0:heads, heads * WIN:(heads + 1) * WIN],
                                          ALU.add).then_inc(added, 1)
                    over_tiles(dve, k.tiles, [(0, arguments), (1, scale), (2, add)])
    repeated(k, one_pass)



def gcn_layer(k):
    nc, B, N = k.nc, k.blocks, k.n_nodes
    layer_norm(k, "n0", k.x, k.h, relu=True)
    vector_stage(k, "deg0", lambda dve: dve.memset(k.acc[:, 0, :], 1.0))
    count_degrees(k)
    with Stage(k, "root") as st:
        rooted, inverted, turned = st.sem("rooted"), st.sem("inverted"), st.sem("turned")
        with st.block() as block:
            @block.scalar
            def _(act):
                act.sqrt(k.inv_sqrt_deg[:, :], k.acc[:, 0, :]).then_inc(rooted, 1)

            @block.vector
            def _(dve):
                dve.wait_ge(rooted, 1)
                dve.reciprocal(k.inv_sqrt_deg[:, :], k.inv_sqrt_deg[:, :]).then_inc(inverted, 1)
                dve.wait_ge(turned, 1)
                dve.tensor_copy(k.inv_sqrt_deg_nm[:, :], k.bank[0][:, 0:B])

            @block.tensor
            def _(pe):
                pe.wait_ge(inverted, 1)
                for b in range(B):
                    mm = pe.matmul(k.bank[0][:, b:b + 1], k.inv_sqrt_deg[0:1, b * P:(b + 1) * P],
                                   k.ones[0:1, 0:1], start=True, stop=True)
                mm.then_inc(turned, 1)
    own = k.wide[:, 0, :].rearrange("p (b f) -> p b f", f=F)
    vector_stage(k, "rows0", lambda dve: dve.tensor_tensor(
        own, k.h[:, :, :], k.inv_sqrt_deg_nm[:, :].unsqueeze(2).to_broadcast([P, B, F]), ALU.mult))
    store_table(k, "rows0", own, k.table1)
    to_feature_major(k, "own0", own, k.acc[:, 0, :])
    sum_neighbours(k, "agg0", k.table1)
    vector_stage(k, "deg1", lambda dve: dve.tensor_tensor(k.fa[:, :], k.acc[:, 0, :], k.inv_sqrt_deg[:, :], ALU.mult))
    linear(k, "gcn1", k.w["L0_gnn_W1"][:, :], k.fa,
           lambda act, lh, bank: act.activation(k.fb[:, lh[0]:lh[1]], bank, ACT.Relu,
                                                bias=k.w["L0_gnn_b1"][:, 0:1]), engine="scalar")
    vector_stage(k, "rows1", lambda dve: dve.tensor_tensor(k.acc[:, 0, :], k.fb[:, :], k.inv_sqrt_deg[:, :], ALU.mult))
    rows = k.wide[:, 0, :].rearrange("p (b f) -> p b f", f=F)
    turn_to_nodes(k, "turn1", k.acc[:, 0, :], rows)
    store_table(k, "rows1", rows, k.table1)
    sum_neighbours(k, "agg1", k.table1)
    vector_stage(k, "deg2", lambda dve: dve.tensor_tensor(k.fa[:, :], k.acc[:, 0, :], k.inv_sqrt_deg[:, :], ALU.mult))
    logits = k.wide[:, 0, :].rearrange("p (b f) -> p b f", f=F)
    product_stage(k, "gcn2", B,
                  lambda pe, b, bank: pe.matmul(bank[:, 0:F], k.fa[:, b * P:(b + 1) * P], k.w["L0_gnn_W2"][:, :],
                                                start=True, stop=True),
                  "vector",
                  lambda dve, b, bank: dve.tensor_tensor(logits[:, b, :], bank[:, 0:F], k.w["L0_gnn_b2"][:, :],
                                                         ALU.add))

    def wide(stat):
        return stat[:, :].unsqueeze(2).to_broadcast([P, B, F])

    with Stage(k, "soft") as st:
        step, raised = st.sem("step"), st.sem("raised")
        with st.block() as block:
            @block.vector
            def _(dve):
                dve.tensor_reduce(k.stat[:, :], logits, AX.X, ALU.max).then_inc(step, 1)
                dve.wait_ge(step, 1)
                dve.tensor_tensor(logits, logits, wide(k.stat), ALU.subtract).then_inc(step, 1)
                dve.wait_ge(raised, 1)
                dve.tensor_reduce(k.stat[:, :], logits, AX.X, ALU.add).then_inc(step, 1)
                dve.wait_ge(step, 3)
                dve.reciprocal(k.stat2[:, :], k.stat[:, :]).then_inc(step, 1)
                dve.wait_ge(step, 4)
                dve.tensor_tensor(logits, logits, wide(k.stat2), ALU.mult).then_inc(step, 1)
                dve.wait_ge(step, 5)
                dve.tensor_tensor(k.x[:, :, :], k.x[:, :, :], logits, ALU.add)

            @block.scalar
            def _(act):
                act.wait_ge(step, 2)
                act.activation(logits, logits, ACT.Exp).then_inc(raised, 1)


def turn_to_nodes(k, name, src, dst):
    def product(pe, c, bank):
        lo, hi = chunks(k.n_nodes)[c]
        for b in range(lo // P, hi // P):
            mm = pe.transpose(bank[:, b * P - lo:(b + 1) * P - lo], src[:, b * P:(b + 1) * P], k.ident[:, :])
        return mm

    def take(act, c, bank):
        lo, hi = chunks(k.n_nodes)[c]
        return act.copy(dst[:, lo // P:hi // P, :], bank[:, 0:hi - lo].rearrange("p (b f) -> p b f", f=F))

    product_stage(k, name, len(chunks(k.n_nodes)), product, "scalar", take)


def additive_layer(k):
    layer_norm(k, "n1", k.x, k.h, relu=True)
    to_feature_major(k, "turn2", k.h, k.fa)
    table_rows(k, "proj", k.fa, k.w["L1_gnn_W"][:, :], None, k.table1)
    per_edge = k.tiles * SUB
    scores = k.scores[:, :].rearrange("p (e h) -> p e h", h=HEADS1)
    vector_stage(k, "pad1", lambda dve: dve.tensor_copy(
        scores, k.pad[:, :].unsqueeze(2).to_broadcast([P, per_edge, HEADS1])))
    score_edges(k, "add", HEADS1, k.table1, k.table1, k.kept1)
    with Stage(k, "max1") as st:
        step, turned, spread = st.sem("step"), st.sem("turned"), st.sem("spread")
        top = k.small[:, 0:HEADS1]
        with st.block() as block:
            @block.vector
            def _(dve):
                dve.memset(k.small[:, :], 0.0)
                dve.memset(k.node_sum1[:, :], 0.0)
                dve.memset(k.acc[:, 0, :], 0.0).then_inc(step, 1)
                dve.wait_ge(step, 1)
                dve.tensor_reduce(top, scores.rearrange("p e h -> p h e"), AX.X, ALU.max).then_inc(step, 1)
                dve.wait_ge(turned, 1)
                dve.tensor_reduce(k.small[0:HEADS1, 8:9], k.bank[0][0:HEADS1, 0:P], AX.X, ALU.max).then_inc(step, 1)
                dve.wait_ge(step, 3)
                dve.tensor_scalar(k.small[0:HEADS1, 12:12 + HEADS1], k.ident[0:HEADS1, 0:HEADS1],
                                  k.small[0:HEADS1, 8:9], None, ALU.mult).then_inc(step, 1)
                dve.wait_ge(spread, 1)
                dve.tensor_copy(top, k.bank[1][:, 0:HEADS1]).then_inc(step, 1)
                dve.wait_ge(step, 5)
                dve.tensor_tensor(scores, scores, top.unsqueeze(1).to_broadcast([P, per_edge, HEADS1]), ALU.subtract)

            @block.tensor
            def _(pe):
                pe.wait_ge(step, 2)
                pe.transpose(k.bank[0][0:HEADS1, 0:P], top, k.ident[:, :]).then_inc(turned, 1)
                pe.wait_ge(step, 4)
                pe.matmul(k.bank[1][:, 0:HEADS1], k.ones[0:HEADS1, :], k.small[0:HEADS1, 12:12 + HEADS1],
                          start=True, stop=True).then_inc(spread, 1)
    weigh_additive(k)
    vector_stage(k, "norm1",
                 lambda dve: dve.tensor_scalar(k.node_sum1[:, :], k.node_sum1[:, :], 1e-12, None, ALU.max),
                 lambda dve: dve.reciprocal(k.node_sum1[:, :], k.node_sum1[:, :]))
    linear(k, "div1", k.head_block[:, :], k.node_sum1,
           lambda dve, lh, bank: dve.tensor_tensor(k.fa[:, lh[0]:lh[1]], k.acc[:, 0, lh[0]:lh[1]], bank, ALU.mult))
    add_to_nodes(k, "sum1", k.fa, k.x)


def gat_layer(k):
    N = k.n_nodes
    w = k.w
    layer_norm(k, "n2", k.x, k.h, relu=True)
    inner = k.acc[:, 0, :].rearrange("p (b f) -> p b f", f=F)
    layer_norm(k, "n2i", k.h, inner, relu=False)
    vector_stage(k, "res2", lambda dve: dve.tensor_tensor(k.x[:, :, :], k.x[:, :, :], k.h[:, :, :], ALU.add))
    to_feature_major(k, "turn3", inner, k.fa, func=ACT.Relu, scale=w["L2_gnn_gamma"][:, 0:1],
                     bias=w["L2_gnn_beta"][:, 0:1])
    table_rows(k, "left", k.fa, w["L2_gnn_Wl"][:, :], w["L2_gnn_bl"][:, :], k.table2)
    table_rows(k, "right", k.fa, w["L2_gnn_Wr"][:, :], w["L2_gnn_br"][:, :], k.table2r)
    linear(k, "resw", w["L2_gnn_res_W"][:, :], k.fa,
           lambda act, lh, bank: act.activation(k.fb[:, lh[0]:lh[1]], bank, ACT.Identity,
                                                bias=w["L2_gnn_bias"][:, 0:1]), engine="scalar")
    scores = k.scores[:, 0:k.tiles * SUB * HEADS2].rearrange("p (t h j) -> p t h j", h=HEADS2, j=SUB)
    vector_stage(k, "pad2",
                 lambda dve: dve.tensor_copy(scores[:, :, 0, :], k.pad[:, :].rearrange("p (t j) -> p t j", j=SUB)),
                 lambda dve: dve.tensor_copy(scores[:, :, 1, :], k.pad[:, :].rearrange("p (t j) -> p t j", j=SUB)),
                 lambda dve: dve.memset(k.node_top[:, :], -BIG),
                 lambda dve: dve.memset(k.node_sum[:, :], 0.0))
    score_edges(k, "gat", HEADS2, k.table2, k.table2r, k.kept2)
    cs = chunks(N)

    def spread_rows(name, rows, dst):
        def product(pe, c, bank):
            h, (lo, hi) = c // len(cs), cs[c % len(cs)]
            return pe.matmul(bank[:, 0:hi - lo], k.head_row[:, h * P:(h + 1) * P], rows[:, lo:hi],
                             start=True, stop=True)

        def take(act, c, bank):
            h, (lo, hi) = c // len(cs), cs[c % len(cs)]
            return act.copy(dst[:, h, lo:hi], bank[:, 0:hi - lo])
        product_stage(k, name, HEADS2 * len(cs), product, "scalar", take)

    spread_rows("tops2", k.node_top, k.wide)
    vector_stage(k, "zero2", lambda dve: dve.memset(k.acc[:, :, :], 0.0))
    weigh_gat(k)
    vector_stage(k, "norm2",
                 lambda dve: dve.tensor_scalar(k.node_sum[:, :], k.node_sum[:, :], 1e-16, None, ALU.add),
                 lambda dve: dve.reciprocal(k.node_sum[:, :], k.node_sum[:, :]),
                 lambda dve: dve.tensor_scalar(k.node_sum[:, :], k.node_sum[:, :], 1.0 / HEADS2, None, ALU.mult))
    spread_rows("sums2", k.node_sum, k.wide)
    vector_stage(k, "mean2",
                 lambda dve: dve.tensor_tensor(k.acc[:, :, :], k.acc[:, :, :], k.wide[:, :, :], ALU.mult),
                 lambda dve: dve.tensor_tensor(k.acc[:, 0, :], k.acc[:, 0, :], k.acc[:, 1, :], ALU.add),
                 lambda dve: dve.tensor_tensor(k.fb[:, :], k.fb[:, :], k.acc[:, 0, :], ALU.add))
    add_to_nodes(k, "sum2", k.fb, k.x)


def ssp_linear(k, name, src, weight, bias, dst, residual, scratch, keep=None):
    cs = chunks(k.n_nodes)
    low, soft = scratch
    soft = keep if keep is not None else soft
    with Stage(k, name) as st:
        folded, raised, logged, soft_ready = st.sem("folded"), st.sem("raised"), st.sem("logged"), st.sem("soft_ready")
        ready, taken = st.sem("ready"), st.sem("taken")
        with st.block() as block:
            @block.scalar
            def _(act):
                for c, (lo, hi) in enumerate(cs):
                    act.wait_ge(folded, c + 1)
                    act.activation(low[:, lo:hi], low[:, lo:hi], ACT.Exp).then_inc(raised, 1)
                    act.wait_ge(raised, c + 1)
                    act.activation(low[:, lo:hi], low[:, lo:hi], ACT.Ln, bias=k.half[:, 0:1],
                                   scale=0.5).then_inc(logged, 1)

            @block.tensor
            def _(pe):
                for c, (lo, hi) in enumerate(cs):
                    pe.wait_ge(soft_ready, c + 1)
                    pe.matmul(k.bank[c][:, 0:hi - lo], weight, soft[:, lo:hi], start=True,
                              stop=True).then_inc(ready, 1)

            @block.vector
            def _(dve):
                for lo, hi in cs:
                    dve.scalar_tensor_tensor(out=low[:, lo:hi], in0=src[:, lo:hi], scalar=-1.0, in1=src[:, lo:hi],
                                             op0=ALU.mult, op1=ALU.min).then_inc(folded, 1)
                for c in range(len(cs) + 1):
                    if c < len(cs):
                        lo, hi = cs[c]
                        dve.wait_ge(logged, c + 1)
                        dve.scalar_tensor_tensor(out=soft[:, lo:hi], in0=src[:, lo:hi], scalar=0.0,
                                                 in1=low[:, lo:hi], op0=ALU.max, op1=ALU.add).then_inc(soft_ready, 1)
                    if c > 0:
                        lo, hi = cs[c - 1]
                        dve.wait_ge(ready, c)
                        if residual is None:
                            dve.tensor_scalar(dst[:, lo:hi], k.bank[c - 1][:, 0:hi - lo], bias, None,
                                              ALU.add).then_inc(taken, 1)
                        else:
                            dve.scalar_tensor_tensor(out=dst[:, lo:hi], in0=k.bank[c - 1][:, 0:hi - lo],
                                                     scalar=bias, in1=residual[:, lo:hi], op0=ALU.add,
                                                     op1=ALU.add).then_inc(taken, 1)


def load_sources(k):
    B, nq = k.blocks, k.tiles * SUB
    raw = k.scores[:, 0:nq].bitcast(I32)
    k.src_f = k.scores[:, nq:2 * nq]
    k.earlier = k.scores[:, 2 * nq:2 * nq + SUB * P].rearrange("p (j e) -> p j e", e=P)
    zeros = k.wide[:, 0, :]
    with Stage(k, "srcs") as st:
        loaded, cleared, zeroed = st.sem("loaded"), st.sem("cleared"), st.sem("zeroed")
        with st.block() as block:
            @block.vector
            def _(dve):
                dve.memset(zeros, 0.0).then_inc(cleared, 1)
                dve.tensor_scalar(k.spare[:, :], k.iota_p[:, :], float(k.n_nodes), None, ALU.add)
                dve.wait_ge(loaded, 16)
                dve.tensor_copy(k.src_f, raw)

            @block.sync
            def _(sp):
                sp.dma_start(raw, k.ins["src_edges"]).then_inc(loaded, 16)
                sp.wait_ge(cleared, 1)
                for two in k.sums:
                    for table in two:
                        sp.dma_start(table[0:k.n_nodes, :].rearrange("(b p) f -> p b f", p=P),
                                     zeros.rearrange("p (b f) -> p b f", f=F)).then_inc(zeroed, 16)
                        sp.dma_start(table[k.n_nodes:k.n_nodes + P, :], zeros[:, 0:F]).then_inc(zeroed, 16)
                sp.wait_ge(loaded, 16)
                sp.wait_ge(zeroed, 32 * 2 * SUB)


def collect_sums(k):
    tables = [table for two in k.sums for table in two]
    total = k.h
    with Stage(k, "coll") as st:
        loaded = [st.sem(f"loaded{i}") for i in range(3)]
        added = st.sem("added")
        bufs = [k.wide[:, 0, :], k.wide[:, 1, :], k.acc[:, 1, :]]
        with st.block() as block:
            @block.sync
            def _(sp):
                for n, table in enumerate(tables):
                    wait_count(sp, added, n - 2)
                    sp.dma_start(bufs[n % 3].rearrange("p (b f) -> p b f", f=F),
                                 table[0:k.n_nodes, :].rearrange("(b p) f -> p b f", p=P)).then_inc(loaded[n % 3], 16)

            @block.vector
            def _(dve):
                for n in range(len(tables)):
                    dve.wait_ge(loaded[n % 3], 16 * (n // 3 + 1))
                    wait_count(dve, added, n)
                    buf = bufs[n % 3].rearrange("p (b f) -> p b f", f=F)
                    if n == 0:
                        dve.tensor_copy(total[:, :, :], buf).then_inc(added, 1)
                    else:
                        dve.tensor_tensor(total[:, :, :], total[:, :, :], buf, ALU.add).then_inc(added, 1)

    def product(pe, c, bank):
        lo, hi = chunks(k.n_nodes)[c]
        for b in range(lo // P, hi // P):
            mm = pe.transpose(bank[:, b * P - lo:(b + 1) * P - lo], total[:, b, :], k.ident[:, :])
        return mm

    def take(dve, c, bank):
        lo, hi = chunks(k.n_nodes)[c]
        a = k.acc[:, 0, lo:hi]
        return dve.tensor_tensor(a, a, bank[:, 0:hi - lo], ALU.add)

    product_stage(k, "collt", len(chunks(k.n_nodes)), product, "vector", take)


def interaction_layer(k):
    w = k.w
    layer_norm(k, "n3", k.x, k.h, relu=True)
    to_feature_major(k, "turn4", k.h, k.fa)
    scratch = (k.wide[:, 0, :], k.wide[:, 1, :])
    m = k.acc[:, 0, :]
    ssp_linear(k, "xi", k.fa, w["L3_gnn_Wi"][:, :], w["L3_gnn_bi"][:, 0:1], m, None, scratch, keep=k.fb)
    table_rows(k, "xj", k.fb, w["L3_gnn_Wj"][:, :], w["L3_gnn_bj"][:, :], k.table1)
    load_sources(k)
    scatter_filtered(k, k.table1)
    collect_sums(k)
    mid = k.acc[:, 1, :]
    for l in range(k.ins["L3_gnn_res_int_W1"].shape[0]):
        ssp_linear(k, f"ri{l}a", m, w[f"L3_gnn_res_int_W1{l}"][:, :], w[f"L3_gnn_res_int_b1{l}"][:, 0:1], mid,
                   None, scratch)
        ssp_linear(k, f"ri{l}b", mid, w[f"L3_gnn_res_int_W2{l}"][:, :], w[f"L3_gnn_res_int_b2{l}"][:, 0:1], m,
                   m, scratch)
    vector_stage(k, "gate", lambda dve: dve.tensor_scalar(k.fa[:, :], k.fa[:, :], w["L3_gnn_u"][:, 0:1], None,
                                                          ALU.mult))
    ssp_linear(k, "dense", m, w["L3_gnn_dense_W"][:, :], w["L3_gnn_dense_b"][:, 0:1], k.fa, k.fa, scratch)
    for l in range(k.ins["L3_gnn_res_at_W1"].shape[0]):
        ssp_linear(k, f"ra{l}a", k.fa, w[f"L3_gnn_res_at_W1{l}"][:, :], w[f"L3_gnn_res_at_b1{l}"][:, 0:1], mid,
                   None, scratch)
        ssp_linear(k, f"ra{l}b", mid, w[f"L3_gnn_res_at_W2{l}"][:, :], w[f"L3_gnn_res_at_b2{l}"][:, 0:1], k.fa,
                   k.fa, scratch)
    add_to_nodes(k, "sum3", k.fa, k.x)


def store_nodes(k):
    n = k.out.shape[0]
    full = n // P
    with Stage(k, "out") as st:
        stored = st.sem("stored")
        with st.block() as block:
            @block.sync
            def _(sp):
                sp.dma_start(k.out[0:full * P, :].rearrange("(b p) f -> p b f", p=P),
                             k.x[:, 0:full, :]).then_inc(stored, 16)
                sp.dma_start(k.out[full * P:n, :], k.x[0:n - full * P, full, :]).then_inc(stored, 16)
                sp.wait_ge(stored, 32)


def gnn_kernel(nc, ins, out, n_edges):
    with ExitStack() as ctx:
        k = Kernel(nc, ctx, ins, out)
        load_everything(k)
        choose_passes(k, n_edges)
        gcn_layer(k)
        additive_layer(k)
        gat_layer(k)
        interaction_layer(k)
        store_nodes(k)


def kernel(**inputs):
    import numpy as _np
    import concourse.bacc as _bacc
    from concourse import mybir as _mybir
    from concourse.bass_utils import run_bass_kernel_spmd as _run

    arrays = {name: _np.ascontiguousarray(a) for name, a in inputs.items()}
    x, src, dst, attr = (arrays.pop(name) for name in ("x", "src", "dst", "edge_attr_64"))
    n, f = x.shape
    n_edges, depth = attr.shape
    blocks, tiles = ceil_div(n, P), ceil_div(n_edges, TILE)

    x_rows = _np.zeros((blocks * P, f), x.dtype)
    x_rows[:n] = x
    arrays["x"] = _np.ascontiguousarray(x_rows.reshape(blocks, P, f).transpose(1, 0, 2))
    src_rows, dst_rows = _np.zeros(tiles * TILE, src.dtype), _np.full(tiles * TILE, -1, dst.dtype)
    src_rows[:n_edges], dst_rows[:n_edges] = src, dst
    arrays["src_rows"] = _np.ascontiguousarray(src_rows.reshape(tiles, SUB, P).transpose(0, 2, 1))
    arrays["src_flat"] = src_rows.reshape(tiles, TILE)
    arrays["src_edges"] = _np.ascontiguousarray(
        src_rows.reshape(tiles, SUB, P).transpose(2, 0, 1).reshape(P, tiles * SUB))
    arrays["dst_rows"] = dst_rows.reshape(tiles, TILE)
    arrays["dst_first"] = _np.ascontiguousarray(dst_rows[::TILE].reshape(1, tiles))
    arrays["dst_edges"] = _np.ascontiguousarray(
        dst_rows.reshape(tiles, SUB, P).transpose(2, 0, 1).reshape(P, tiles * SUB))
    attr_rows = _np.zeros((tiles * TILE, depth), attr.dtype)
    attr_rows[:n_edges] = attr
    arrays["attr_rows"] = _np.ascontiguousarray(attr_rows.reshape(tiles, TILE, depth).transpose(0, 2, 1))

    nc = _bacc.Bacc("TRN2", target_bir_lowering=False, num_devices=1)
    ins = {name: nc.dram_tensor(f"in_{name}", a.shape, _mybir.dt.from_np(a.dtype), kind="ExternalInput").ap()
           for name, a in arrays.items()}
    out = nc.dram_tensor("out_nodes", (n, f), _mybir.dt.from_np(x.dtype), kind="ExternalOutput").ap()
    gnn_kernel(nc, ins, out, n_edges)
    r = _run(nc, [{f"in_{name}": a for name, a in arrays.items()}], core_ids=[0])
    return r.results[0]["out_nodes"]
```

```python
from contextlib import ExitStack

import numpy as np

import concourse.bass as bass
from concourse import mybir

ALU = mybir.AluOpType
ACT = mybir.ActivationFunctionType
AX = mybir.AxisListType
F32 = mybir.dt.float32
I32 = mybir.dt.int32
BF16 = mybir.dt.bfloat16

P = 128
F = 128
WIN = 32
PARTS = 3
WROWS = WIN * PARTS
SUB = 4
TILE = P * SUB
RING = 4
ROUND = 1.5 * 2 ** 23
BIG = 1e30
CHUNK = 512
BANKS = 8
LN_EPS = 1e-5
HEADS1 = 4
HEADS2 = 2


def ceil_div(a, b):
    return -(-a // b)


class Tile:

    def __init__(self, t, slot, rounds):
        self.t, self.slot, self.rounds = t, slot, rounds
        self.two = slot % 2


def over_tiles(eng, tiles, stages):
    full = tiles // RING

    def step(s_round, s_slot, static):
        for lag, stage in stages:
            slot = (s_slot - lag) % RING
            rounds = s_round if s_slot >= lag else s_round - 1
            t = rounds * RING + slot
            if not static or 0 <= t < tiles:
                stage(Tile(t, slot, rounds))

    for s in range(RING):
        step(0, s, True)
    with eng.Fori(1, full) as i:
        for s in range(RING):
            step(i, s, False)
    for s in range(full * RING, tiles + max(lag for lag, _ in stages)):
        step(s // RING, s % RING, True)


def wait_count(eng, sem, count):
    if not isinstance(count, int) or count > 0:
        eng.wait_ge(sem, count)


class Kernel:

    def __init__(self, nc, ctx, ins, out):
        self.nc, self.ctx, self.ins, self.out = nc, ctx, ins, out
        self.n_nodes = ins["x"].shape[1] * P
        self.blocks = ins["x"].shape[1]
        self.tiles = ins["src_rows"].shape[0]

    def sb(self, name, shape, dt=F32):
        return self.ctx.enter_context(self.nc.sbuf_tensor(name, shape, dt))


class Stage:

    def __init__(self, k, name):
        self.k, self.nc, self.name = k, k.nc, name
        self.ctx, self.sems, self.pool_dma = ExitStack(), [], []

    def sem(self, name):
        s = self.ctx.enter_context(self.nc.semaphore(f"{self.name}_{name}"))
        self.sems.append(s)
        return s

    def pool_dma_sem(self, name):
        s = self.sem(name)
        self.pool_dma.append(s)
        return s

    def __enter__(self):
        return self

    def block(self):
        return self.nc.Block(f"{self.name}_{self.nc.next_id()}", no_gpsimd_drain=not self.pool_dma)

    def clear(self):
        for s in self.pool_dma:
            self.nc.gpsimd.dma_reset(range(s.num, s.num + 1))
        for s in self.sems:
            self.nc.gpsimd.sem_clear(s)
        self.nc.all_engine_barrier()

    def __exit__(self, *exc):
        if exc[0] is None:
            self.clear()
        self.ctx.close()
        return False



def load_everything(k):
    nc, ins = k.nc, k.ins
    B, T, N = k.blocks, k.tiles, k.n_nodes
    k.bank = [k.ctx.enter_context(nc.psum_tensor(f"bank{i}", [P, CHUNK], F32)) for i in range(BANKS)]
    k.x = k.sb("x_nm", [P, B, F])
    k.h = k.sb("h_nm", [P, B, F])
    k.fa = k.sb("fm_a", [P, N])
    k.fb = k.sb("fm_b", [P, N])
    k.acc = k.sb("acc", [P, 2, N])
    k.inv_sqrt_deg = k.sb("inv_sqrt_deg_fm", [P, N])
    k.inv_sqrt_deg_nm = k.sb("inv_sqrt_deg_nm", [P, B])
    k.scores = k.sb("scores", [P, T * SUB * HEADS1])
    k.stat = k.sb("stat", [P, B])
    k.stat2 = k.sb("stat2", [P, B])
    k.wide = k.sb("wide", [P, 2, N])
    k.dst_i = k.scores[:, 0:T * SUB].bitcast(I32)
    k.dst_f = k.sb("dst_f", [P, T * SUB])
    k.pad = k.sb("pad", [P, T * SUB])
    k.local = k.sb("local", [P, T * SUB])
    k.member = k.sb("member", [P, T * SUB])
    k.first = k.sb("first", [P, T])
    k.base = k.sb("base", [P, T])
    k.base_i = k.sb("base_i", [P, T], I32)
    k.first_i = k.base_i
    k.win_off = k.sb("win_off", [P, 1])
    k.win_step = k.sb("win_step", [P, 1])
    k.passes_i = k.sb("passes_i", [P, 1], I32)
    k.spare = k.sb("spare", [P, 1])
    k.small = k.sb("small", [P, 16])
    k.picked = k.sb("picked", [P, SUB * HEADS1])
    k.tops = k.sb("tops", [P, 2, HEADS2])
    k.tile_top = k.sb("tile_top", [HEADS2, WIN])
    k.node_top = k.inv_sqrt_deg[0:HEADS2, :]
    k.node_sum = [k.fa[:, :], k.inv_sqrt_deg[:, :]]
    k.tile_sum = k.sb("tile_sum", [P, HEADS2, WIN])
    k.node_sum1 = k.inv_sqrt_deg[0:HEADS1, :]
    k.shifted = [k.sb(f"shifted{i}", [P, SUB * HEADS2]) for i in range(2)]
    k.weight = [k.sb(f"weight{i}", [P, SUB * HEADS1]) for i in range(2)]
    k.scaled = [k.sb(f"scaled{i}", [P, HEADS2, SUB, WIN]) for i in range(RING)]
    k.iota_i = k.sb("iota_i", [P, WIN], I32)
    k.iota_n = k.sb("iota_n", [P, WIN])
    k.iota_pi = k.sb("iota_pi", [P, 1], I32)
    k.iota_p = k.sb("iota_p", [P, 1])
    k.iota_w = k.sb("iota_w", [P, 1])
    k.ident = k.sb("ident", [P, P])
    k.ones = k.sb("ones", [P, P])
    k.lower = k.sb("lower", [P, P])
    k.eps = k.sb("eps", [P, 1])
    k.half = k.sb("half", [P, 1])
    k.head_row = k.sb("head_row", [HEADS2, HEADS2 * P])
    k.head_block = k.sb("head_block", [HEADS1, F])
    k.idx = [k.sb(f"idx{i}", [P, SUB], I32) for i in range(RING)]
    k.g = [k.sb(f"gathered{i}", [P, SUB, 2 * F]) for i in range(RING)]
    k.onehot = [k.sb(f"onehot{i}", [P, SUB, WIN]) for i in range(RING)]
    k.ones16 = k.sb("ones16", [P, P], BF16)
    k.msg = [k.sb(f"msg{i}", [P, SUB, F]) for i in range(2)]
    k.dst_row = [k.sb(f"dst_row{i}", [WROWS, TILE], BF16) for i in range(RING)]
    k.onehot_t = [k.sb(f"onehot_t{i}", [WROWS, TILE], BF16) for i in range(2)]
    k.window = [k.sb(f"window{i}", [WROWS, 2 * F], BF16) for i in range(RING)]
    k.zact = [k.sb(f"zact{i}", [P, 2, TILE]) for i in range(2)]
    k.src_row = [k.zact[i][:, 1, :].bitcast(I32) for i in range(2)]
    k.attr = [k.sb(f"attr{i}", [64, TILE]) for i in range(2)]
    k.table1 = nc.dram_tensor("table1", [N, F], F32).ap()
    k.table2 = nc.dram_tensor("table2", [N, 2 * F], F32).ap()
    k.parts1 = nc.dram_tensor("parts1", [N, PARTS, F], BF16).ap()
    k.parts2 = nc.dram_tensor("parts2", [N, PARTS, 2 * F], BF16).ap()
    k.local_rows = nc.dram_tensor("local_rows", [T, TILE], BF16).ap()
    k.sums = [[nc.dram_tensor(f"sums{i}_{j}", [N + P, F], F32).ap() for j in range(SUB)] for i in range(2)]
    k.kept1 = nc.dram_tensor("kept1", [T, P, SUB * F], F32).ap()
    k.kept2 = nc.dram_tensor("kept2", [T, P, SUB * 2 * F], F32).ap()

    k.w = {}
    loads = []

    def weight(name, src, shape):
        k.w[name] = k.sb("w_" + name, shape)
        loads.append((k.w[name], src))

    for name in ("L0_gnn_W1", "L0_gnn_W2", "L1_gnn_W", "L2_gnn_Wl", "L2_gnn_Wr", "L2_gnn_res_W",
                 "L3_gnn_k2f_W", "L3_gnn_Wi", "L3_gnn_Wj", "L3_gnn_dense_W"):
        weight(name, ins[name], list(ins[name].shape))
    for name in ("L3_gnn_res_int_W1", "L3_gnn_res_int_W2", "L3_gnn_res_at_W1", "L3_gnn_res_at_W2"):
        for l in range(ins[name].shape[0]):
            weight(f"{name}{l}", ins[name][l], [F, F])
    for name in ("L0_gnn_b1", "L2_gnn_gamma", "L2_gnn_beta", "L2_gnn_bias", "L3_gnn_bi", "L3_gnn_dense_b",
                 "L3_gnn_u"):
        weight(name, ins[name].rearrange("(f o) -> f o", o=1), [F, 1])
    for name in ("L3_gnn_res_int_b1", "L3_gnn_res_int_b2", "L3_gnn_res_at_b1", "L3_gnn_res_at_b2"):
        for l in range(ins[name].shape[0]):
            weight(f"{name}{l}", ins[name][l].rearrange("(f o) -> f o", o=1), [F, 1])
    for name in ("L0_gnn_b2", "L2_gnn_bl", "L2_gnn_br", "L3_gnn_bj"):
        n = ins[name].shape[0]
        weight(name, ins[name].rearrange("(o f) -> o f", o=1).to_broadcast([P, n]), [P, n])
    k.att1 = k.sb("att1", [F, HEADS1])
    k.att1_col = k.sb("att1_col", [F, 1])
    loads.append((k.att1_col, ins["L1_gnn_att"].rearrange("h (c o) -> (h c) o", o=1)))
    k.att2_rows = k.sb("att2_rows", [HEADS2, F])
    k.att2 = k.sb("att2", [F, HEADS2])
    loads.append((k.att2_rows, ins["L2_gnn_att"]))
    loads.append((k.x, ins["x"]))
    loads.append((k.dst_i, ins["dst_edges"]))
    loads.append((k.first_i, ins["dst_first"].to_broadcast([P, T])))

    per_head = F // HEADS1
    with Stage(k, "setup") as st:
        loaded, made, done, flat = st.sem("loaded"), st.sem("made"), st.sem("done"), st.sem("flat")
        cast = st.sem("cast")
        with st.block() as block:
            @block.sync
            def _(sp):
                with nc.allow_non_contiguous_dma(reason="bias and attention columns, first destinations"):
                    for dst, src in loads:
                        full = dst[:, :, :] if len(dst.shape) == 3 else dst[:, :]
                        sp.dma_start(full, src).then_inc(loaded, 16)
                sp.wait_ge(loaded, 16 * len(loads))

            @block.gpsimd
            def _(pool):
                pool.iota(k.iota_i[:, :], pattern=[[1, WIN]], base=0, channel_multiplier=0).then_inc(made, 1)
                pool.iota(k.iota_pi[:, :], pattern=[[0, 1]], base=0, channel_multiplier=1).then_inc(made, 1)
                pool.memset(k.ident[:, :], 0.0).then_inc(flat, 1)
                pool.memset(k.ones[:, :], 1.0)
                pool.memset(k.ones16[:, :], 1.0)
                pool.memset(k.lower[:, :], 1.0)
                pool.memset(k.eps[:, :], LN_EPS)
                pool.memset(k.half[:, :], 0.5)
                pool.memset(k.head_block[:, :], 1.0)
                pool.memset(k.head_row[:, :], 1.0).then_inc(flat, 1)
                pool.memset(k.att1[:, :], 1.0).then_inc(flat, 1)
                pool.wait_ge(flat, 3)
                pool.affine_select(out=k.ident[:, :], in_=k.ident[:, :], compare_op=ALU.not_equal, fill=1.0,
                                   base=0, pattern=[[-1, P]], channel_multiplier=1)
                pool.affine_select(out=k.lower[:, :], in_=k.lower[:, :], compare_op=ALU.is_ge, fill=0.0,
                                   base=-1, pattern=[[-1, P]], channel_multiplier=1)
                pool.affine_select(out=k.head_row[:, :], in_=k.head_row[:, :], compare_op=ALU.is_ge, fill=0.0,
                                   base=0, pattern=[[1, HEADS2 * P]], channel_multiplier=-P).then_inc(flat, 1)
                pool.affine_select(out=k.head_block[:, :], in_=k.head_block[:, :], compare_op=ALU.is_ge, fill=0.0,
                                   base=0, pattern=[[1, F]], channel_multiplier=-per_head).then_inc(flat, 1)
                pool.affine_select(out=k.att1[:, :], in_=k.att1[:, :], compare_op=ALU.is_ge, fill=0.0,
                                   base=0, pattern=[[-per_head, HEADS1]], channel_multiplier=1).then_inc(flat, 1)
                pool.wait_ge(flat, 6)
                pool.affine_select(out=k.head_block[:, :], in_=k.head_block[:, :], compare_op=ALU.is_ge, fill=0.0,
                                   base=per_head - 1, pattern=[[-1, F]], channel_multiplier=per_head)
                pool.affine_select(out=k.head_row[:, :], in_=k.head_row[:, :], compare_op=ALU.is_ge, fill=0.0,
                                   base=P - 1, pattern=[[-1, HEADS2 * P]], channel_multiplier=P)
                pool.affine_select(out=k.att1[:, :], in_=k.att1[:, :], compare_op=ALU.is_ge, fill=0.0,
                                   base=per_head - 1, pattern=[[per_head, HEADS1]],
                                   channel_multiplier=-1).then_inc(made, 1)

            @block.tensor
            def _(pe):
                pe.wait_ge(loaded, 16 * len(loads))
                pe.wait_ge(made, 3)
                pe.transpose(k.bank[1][:, 0:HEADS2], k.att2_rows[:, :],
                             k.ident[0:HEADS2, 0:HEADS2]).then_inc(done, 1)

            @block.vector
            def _(dve):
                dve.wait_ge(made, 3)
                dve.tensor_copy(k.iota_n[:, :], k.iota_i[:, :])
                dve.tensor_copy(k.iota_p[:, :], k.iota_pi[:, :]).then_inc(cast, 1)
                dve.wait_ge(cast, 1)
                dve.tensor_scalar(k.iota_w[:, :], k.iota_p[:, :], -1.0, 1.0 / PARTS, ALU.add,
                                  ALU.mult).then_inc(cast, 1)
                dve.wait_ge(cast, 2)
                dve.tensor_scalar(k.iota_w[:, :], k.iota_w[:, :], ROUND, None, ALU.add).then_inc(cast, 1)
                dve.wait_ge(cast, 3)
                dve.tensor_scalar(k.iota_w[:, :], k.iota_w[:, :], -ROUND, None, ALU.add)
                dve.wait_ge(loaded, 16 * len(loads))
                dve.tensor_scalar(k.att1[:, :], k.att1[:, :], k.att1_col[:, 0:1], None, ALU.mult)
                dve.tensor_copy(k.first[:, :], k.first_i[:, :])
                dve.tensor_copy(k.dst_f[:, :], k.dst_i[:, :]).then_inc(cast, 1)
                dve.memset(k.win_off[:, :], 0.0)
                dve.memset(k.win_step[:, :], 0.0)
                dve.wait_ge(done, 1)
                dve.tensor_copy(k.att2[:, :], k.bank[1][:, 0:HEADS2])
                dve.wait_ge(cast, 4)
                dve.tensor_scalar(k.pad[:, :], k.dst_f[:, :], 0.0, -BIG, ALU.is_lt, ALU.mult)


def place_windows(k):
    nc, T = k.nc, k.tiles
    with Stage(k, "windows") as st:
        placed, local = st.sem("placed"), st.sem("local")
        with st.block() as block:
            @block.vector
            def _(dve):
                dve.tensor_scalar(k.base[:, :], k.first[:, :], k.win_off[:, 0:1], None, ALU.add).then_inc(placed, 1)
                dve.wait_ge(placed, 1)
                dve.tensor_tensor(k.local[:, :].rearrange("p (t j) -> p t j", j=SUB),
                                  k.dst_f[:, :].rearrange("p (t j) -> p t j", j=SUB),
                                  k.base[:, :].unsqueeze(2).to_broadcast([P, T, SUB]),
                                  ALU.subtract).then_inc(local, 1)
                dve.tensor_scalar(k.base_i[:, :], k.base[:, :], 0.0, float(k.n_nodes - WIN), ALU.max, ALU.min)
                dve.tensor_scalar(k.win_off[:, :], k.win_off[:, :], k.win_step[:, 0:1], None, ALU.add)
                dve.wait_ge(local, 1)
                dve.tensor_scalar(k.member[:, :], k.local[:, :], 0.0, None, ALU.is_ge).then_inc(placed, 1)
                dve.wait_ge(placed, 2)
                dve.scalar_tensor_tensor(out=k.member[:, :], in0=k.local[:, :], scalar=float(WIN),
                                         in1=k.member[:, :], op0=ALU.is_lt, op1=ALU.mult)


def store_local_rows(k):
    nc, cols = k.nc, k.tiles * SUB
    blocks = ceil_div(cols, P)
    rows = k.wide[:, 0, :].bitcast(BF16)[:, 0:blocks * P]
    with Stage(k, "locals") as st:
        turned, copied, stored = st.sem("turned"), st.sem("copied"), st.sem("stored")
        with st.block() as block:
            @block.tensor
            def _(pe):
                for b in range(blocks):
                    n = min(P, cols - b * P)
                    pe.transpose(k.bank[b][0:n, 0:P], k.local[:, b * P:b * P + n], k.ident[:, :]).then_inc(turned, 1)

            @block.scalar
            def _(act):
                for b in range(blocks):
                    n = min(P, cols - b * P)
                    act.wait_ge(turned, b + 1)
                    act.copy(rows[0:n, b * P:(b + 1) * P], k.bank[b][0:n, 0:P]).then_inc(copied, 1)

            @block.sync
            def _(sp):
                flat = k.local_rows.rearrange("t (j e) -> (t j) e", e=P)
                for b in range(blocks):
                    n = min(P, cols - b * P)
                    sp.wait_ge(copied, b + 1)
                    sp.dma_start(flat[b * P:b * P + n, :], rows[0:n, b * P:(b + 1) * P]).then_inc(stored, 16)
                sp.wait_ge(stored, 16 * blocks)


def choose_passes(k, n_edges):
    nc = k.nc
    passes = ceil_div(k.n_nodes, WIN)
    place_windows(k)
    with Stage(k, "choice") as st:
        counted, summed, step = st.sem("counted"), st.sem("summed"), st.sem("step")
        with st.block() as block:
            @block.vector
            def _(dve):
                dve.tensor_reduce(k.small[:, 0:1], k.member[:, :], AX.X, ALU.add).then_inc(counted, 1)
                dve.wait_ge(summed, 1)
                dve.tensor_scalar(k.small[:, 1:2], k.bank[0][:, 0:1], float(n_edges), None,
                                  ALU.is_equal).then_inc(step, 1)
                dve.wait_ge(step, 1)
                dve.tensor_scalar(k.passes_i[:, :], k.small[:, 1:2], float(1 - passes), float(passes),
                                  ALU.mult, ALU.add)
                dve.tensor_scalar(k.win_step[:, :], k.small[:, 1:2], float(-WIN), float(WIN), ALU.mult, ALU.add)
                dve.tensor_scalar(k.first[:, :], k.first[:, :], k.small[:, 1:2], None, ALU.mult)

            @block.tensor
            def _(pe):
                pe.wait_ge(counted, 1)
                pe.matmul(k.bank[0][:, 0:1], k.ones[:, :], k.small[:, 0:1], start=True,
                          stop=True).then_inc(summed, 1)
    k.passes = nc.values_load(k.passes_i[0:1, 0:1], min_val=1, max_val=passes,
                              skip_runtime_bounds_check_because="it is 1 or the number of windows")


def reset_windows(k):
    with Stage(k, "rewind") as st:
        with st.block() as block:
            @block.vector
            def _(dve):
                dve.memset(k.win_off[:, :], 0.0)



def chunks(n):
    return [(c, min(c + CHUNK, n)) for c in range(0, n, CHUNK)]


def product_stage(k, name, count, product, engine, take):
    with Stage(k, name) as st:
        ready, taken = st.sem("product_ready"), st.sem("product_taken")

        with st.block() as block:
            @block.tensor
            def _(pe):
                for c in range(count):
                    wait_count(pe, taken, c + 1 - BANKS)
                    product(pe, c, k.bank[c % BANKS]).then_inc(ready, 1)

            def taker(eng):
                for c in range(count):
                    eng.wait_ge(ready, c + 1)
                    take(eng, c, k.bank[c % BANKS]).then_inc(taken, 1)

            if engine == "scalar":
                @block.scalar
                def _(act):
                    taker(act)
            else:
                @block.vector
                def _(dve):
                    taker(dve)


def to_feature_major(k, name, src, dst, func=None, scale=1.0, bias=0.0):
    def product(pe, c, bank):
        lo, hi = chunks(k.n_nodes)[c]
        for b in range(lo // P, hi // P):
            mm = pe.transpose(bank[:, b * P - lo:(b + 1) * P - lo], src[:, b, :], k.ident[:, :])
        return mm

    def take(act, c, bank):
        lo, hi = chunks(k.n_nodes)[c]
        if func is None:
            return act.copy(dst[:, lo:hi], bank[:, 0:hi - lo])
        return act.activation(dst[:, lo:hi], bank[:, 0:hi - lo], func, bias=bias, scale=scale)

    product_stage(k, name, len(chunks(k.n_nodes)), product, "scalar", take)


def add_to_nodes(k, name, src, dst):
    def product(pe, c, bank):
        lo, hi = chunks(k.n_nodes)[c]
        for b in range(lo // P, hi // P):
            mm = pe.transpose(bank[:, b * P - lo:(b + 1) * P - lo], src[:, b * P:(b + 1) * P], k.ident[:, :])
        return mm

    def take(dve, c, bank):
        lo, hi = chunks(k.n_nodes)[c]
        d = dst[:, lo // P:hi // P, :]
        return dve.tensor_tensor(d, d, bank[:, 0:hi - lo].rearrange("p (b f) -> p b f", f=F), ALU.add)

    product_stage(k, name, len(chunks(k.n_nodes)), product, "vector", take)


def linear(k, name, weight, src, take, engine="vector"):
    def product(pe, c, bank):
        lo, hi = chunks(k.n_nodes)[c]
        return pe.matmul(bank[:, 0:hi - lo], weight, src[:, lo:hi], start=True, stop=True)

    product_stage(k, name, len(chunks(k.n_nodes)), product, engine,
                  lambda eng, c, bank: take(eng, chunks(k.n_nodes)[c], bank[:, 0:chunks(k.n_nodes)[c][1] - chunks(k.n_nodes)[c][0]]))


def table_rows(k, name, src, weight, bias, table):
    width = weight.shape[1]
    rows = k.wide[:, :, :].rearrange("p a n -> p (a n)")[:, 0:k.blocks * width]
    def product(pe, c, bank):
        return pe.matmul(bank[:, 0:width], src[:, c * P:(c + 1) * P], weight, start=True, stop=True)

    def take(dve, c, bank):
        d = rows[:, c * width:(c + 1) * width]
        if bias is None:
            return dve.tensor_copy(d, bank[:, 0:width])
        return dve.tensor_tensor(d, bank[:, 0:width], bias, ALU.add)

    product_stage(k, name, k.blocks, product, "vector", take)
    if table is not None:
        store_table(k, name, rows.rearrange("p (b f) -> p b f", f=width), table)


def store_table(k, name, rows, table):
    with Stage(k, name + "_store") as st:
        stored = st.sem("stored")
        with st.block() as block:
            @block.sync
            def _(sp):
                sp.dma_start(table.rearrange("(b p) f -> p b f", p=P), rows).then_inc(stored, 16)
                sp.wait_ge(stored, 16)


def store_parts(k, name, rows, rest, parts, table):
    width = table.shape[2]
    groups = [(b, min(b + 5, k.blocks)) for b in range(0, k.blocks, 5)]
    G = len(groups)

    def cut(a, g):
        return a[:, groups[g][0] * width:groups[g][1] * width]

    with Stage(k, name) as st:
        rounded, left, stored = ([st.sem(f"rounded{c}") for c in range(PARTS)],
                                 [st.sem(f"left{c}") for c in range(PARTS - 1)], st.sem("stored"))
        with st.block() as block:
            @block.scalar
            def _(act):
                for g in range(G):
                    act.copy(cut(parts[0], g), cut(rows, g)).then_inc(rounded[0], 1)
                for c in range(1, PARTS):
                    for g in range(G):
                        act.wait_ge(left[c - 1], g + 1)
                        act.copy(cut(parts[c], g), cut(rest, g)).then_inc(rounded[c], 1)

            @block.vector
            def _(dve):
                for c in range(PARTS - 1):
                    for g in range(G):
                        dve.wait_ge(rounded[c], g + 1)
                        if c > 0:
                            dve.wait_ge(left[c - 1], g + 1)
                        dve.tensor_tensor(cut(rest, g), cut(rows if c == 0 else rest, g), cut(parts[c], g),
                                          ALU.subtract).then_inc(left[c], 1)

            @block.sync
            def _(sp):
                to = table.rearrange("(b p) c f -> p b c f", p=P)
                for c in range(PARTS):
                    sp.wait_ge(rounded[c], G)
                    sp.dma_start(to[:, :, c, :], parts[c].rearrange("p (b f) -> p b f", f=width)).then_inc(stored, 16)
                sp.wait_ge(stored, 16 * PARTS)


def layer_norm(k, name, src, dst, relu):
    B = k.blocks
    sq = k.wide[:, 0, :].rearrange("p (b f) -> p b f", f=F)
    cen = k.wide[:, 1, :].rearrange("p (b f) -> p b f", f=F)

    def wide(stat):
        return stat[:, :].unsqueeze(2).to_broadcast([P, B, F])

    with Stage(k, name) as st:
        step, squared, rooted = st.sem("step"), st.sem("squared"), st.sem("rooted")
        with st.block() as block:
            @block.vector
            def _(dve):
                dve.tensor_reduce(k.stat[:, :], src[:, :, :], AX.X, ALU.add).then_inc(step, 1)
                dve.wait_ge(step, 1)
                dve.tensor_scalar(k.stat[:, :], k.stat[:, :], 1.0 / F, None, ALU.mult).then_inc(step, 1)
                dve.wait_ge(step, 2)
                dve.tensor_tensor(cen, src[:, :, :], wide(k.stat), ALU.subtract).then_inc(step, 1)
                dve.wait_ge(squared, 1)
                dve.tensor_reduce(k.stat[:, :], sq, AX.X, ALU.add).then_inc(step, 1)
                dve.wait_ge(rooted, 1)
                dve.reciprocal(k.stat2[:, :], k.stat2[:, :]).then_inc(step, 1)
                dve.wait_ge(step, 5)
                if relu:
                    dve.scalar_tensor_tensor(out=dst[:, :, :], in0=cen, scalar=0.0, in1=wide(k.stat2),
                                             op0=ALU.max, op1=ALU.mult)
                else:
                    dve.tensor_tensor(dst[:, :, :], cen, wide(k.stat2), ALU.mult)

            @block.scalar
            def _(act):
                act.wait_ge(step, 3)
                act.square(sq, cen).then_inc(squared, 1)
                act.wait_ge(step, 4)
                act.activation(k.stat2[:, :], k.stat[:, :], ACT.Sqrt, bias=k.eps[:, 0:1],
                               scale=1.0 / F).then_inc(rooted, 1)


def vector_stage(k, name, *ops):
    with Stage(k, name) as st:
        step = st.sem("step")
        with st.block() as block:
            @block.vector
            def _(dve):
                for n, op in enumerate(ops):
                    wait_count(dve, step, n)
                    op(dve).then_inc(step, 1)



def gathered(k, slot, width):
    return k.g[slot][:, :, :].rearrange("p j f -> p (j f)")[:, 0:SUB * width].rearrange(
        "p (j f) -> p j f", f=width)


def load_indices(k, sp, idx_loaded, t):
    sp.dma_start(k.idx[t.slot][:, :],
                 k.ins["src_rows"][bass.ds(t.t, 1), :, :].rearrange("o p j -> (o p) j")).then_inc(
                     idx_loaded[t.slot], 16)


def gather(k, pool, table, width, idx_loaded, gathers_begun, rows_loaded, t):
    pool.wait_ge(idx_loaded[t.slot], (t.rounds + 1) * 16)
    pool.sem_inc(gathers_begun, 1)
    g = gathered(k, t.slot, width)
    for j in range(SUB):
        pool.indirect_dma_start(out=g[:, j, :], out_offset=None, in_=table,
                                in_offset=bass.IndirectOffsetOnAxis(ap=k.idx[t.slot][:, j:j + 1], axis=0)
                                ).then_inc(rows_loaded[t.slot][j], 16)


def gather_sems(st):
    idx_loaded = [st.sem(f"idx_loaded{i}") for i in range(RING)]
    rows_loaded = [[st.pool_dma_sem(f"rows_loaded{i}_{j}") for j in range(SUB)] for i in range(RING)]
    return idx_loaded, st.sem("gathers_begun"), rows_loaded


def make_onehot(k, dve, t, onehot=None):
    return dve.tensor_tensor(k.onehot[t.slot][:, :, :] if onehot is None else onehot,
                             k.local[:, bass.ds(t.t * SUB, SUB)].unsqueeze(2).to_broadcast([P, SUB, WIN]),
                             k.iota_n[:, :].unsqueeze(1).to_broadcast([P, SUB, WIN]), ALU.is_equal)


def window_base(k, eng, t):
    return eng.value_load(k.base_i[0:1, bass.ds(t.t, 1)], min_val=0, max_val=k.n_nodes - WIN)


def repeated(k, one_pass, rows=False):
    reset_windows(k)
    with k.nc.Fori(0, k.passes):
        place_windows(k)
        if rows:
            store_local_rows(k)
        one_pass()


def count_degrees(k):
    def onehot16(t):
        return k.onehot[t.slot][:, :, :].rearrange("p j n -> p (j n)").bitcast(BF16)[:, 0:SUB * WIN].rearrange(
            "p (j n) -> p j n", n=WIN)

    def one_pass():
        with Stage(k, "deg") as st:
            onehot_ready, sums_ready, added = st.sem("onehot_ready"), st.sem("sums_ready"), st.sem("added")
            with st.block() as block:
                @block.tensor
                def _(pe):
                    def sums(t):
                        pe.wait_ge(onehot_ready, t.t + 1)
                        wait_count(pe, added, t.t + 1 - RING)
                        for j in range(SUB):
                            mm = pe.matmul(k.bank[t.slot][:, 0:WIN], k.ones16[:, :], onehot16(t)[:, j, :],
                                           start=(j == 0), stop=(j == SUB - 1))
                        mm.then_inc(sums_ready, 1)
                    over_tiles(pe, k.tiles, [(0, sums)])

                @block.vector
                def _(dve):
                    def onehot(t):
                        wait_count(dve, sums_ready, t.t + 1 - RING)
                        make_onehot(k, dve, t, onehot16(t)).then_inc(onehot_ready, 1)

                    def add(t):
                        at = window_base(k, dve, t)
                        dve.wait_ge(sums_ready, t.t + 1)
                        wait_count(dve, added, t.t)
                        a = k.acc[:, 0, bass.ds(at, WIN)]
                        dve.tensor_tensor(a, a, k.bank[t.slot][:, 0:WIN], ALU.add).then_inc(added, 1)
                    over_tiles(dve, k.tiles, [(0, onehot), (3, add)])
    repeated(k, one_pass)


def sum_neighbours(k, name, table):
    def one_pass():
        with Stage(k, name) as st:
            idx_loaded, gathers_begun, rows_loaded = gather_sems(st)
            onehot_ready, sums_ready, added = st.sem("onehot_ready"), st.sem("sums_ready"), st.sem("added")
            with st.block() as block:
                @block.sync
                def _(sp):
                    def indices(t):
                        wait_count(sp, sums_ready, t.t + 1 - RING)
                        load_indices(k, sp, idx_loaded, t)
                    over_tiles(sp, k.tiles, [(0, indices)])

                @block.gpsimd
                def _(pool):
                    def rows(t):
                        wait_count(pool, sums_ready, t.t + 1 - RING)
                        gather(k, pool, table, F, idx_loaded, gathers_begun, rows_loaded, t)
                    over_tiles(pool, k.tiles, [(0, rows)])

                @block.tensor
                def _(pe):
                    def sums(t):
                        pe.wait_ge(onehot_ready, t.t + 1)
                        wait_count(pe, added, t.t - 1)
                        g = gathered(k, t.slot, F)
                        for j in range(SUB):
                            pe.wait_ge(rows_loaded[t.slot][j], (t.rounds + 1) * 16)
                            mm = pe.matmul(k.bank[t.two][:, 0:WIN], g[:, j, :], k.onehot[t.slot][:, j, :],
                                           start=(j == 0), stop=(j == SUB - 1))
                        mm.then_inc(sums_ready, 1)
                    over_tiles(pe, k.tiles, [(0, sums)])

                @block.vector
                def _(dve):
                    def onehot(t):
                        wait_count(dve, sums_ready, t.t - 1)
                        make_onehot(k, dve, t).then_inc(onehot_ready, 1)

                    def add(t):
                        at = window_base(k, dve, t)
                        dve.wait_ge(sums_ready, t.t + 1)
                        wait_count(dve, added, t.t)
                        a = k.acc[:, 0, bass.ds(at, WIN)]
                        dve.tensor_tensor(a, a, k.bank[t.two][:, 0:WIN], ALU.add).then_inc(added, 1)
                    over_tiles(dve, k.tiles, [(0, onehot), (1, add)])
    repeated(k, one_pass)


def half_rounds(t):
    return t.rounds * 2 + (1 if t.slot >= 2 else 0)


def load_window(k, sp, table, at, dst_loaded, win_loaded, t):
    width = table.shape[2]
    sp.dma_start(k.dst_row[t.slot][:, :],
                 k.local_rows[bass.ds(t.t, 1), :].to_broadcast([WROWS, TILE])).then_inc(dst_loaded[t.slot], 16)
    sp.dma_start(k.window[t.slot][:, 0:width],
                 table[bass.ds(at, WIN), :, :].rearrange("n c f -> (n c) f")).then_inc(win_loaded[t.slot], 16)


def make_onehot_t(k, dve, t):
    return dve.tensor_scalar(k.onehot_t[t.two][:, :], k.dst_row[t.slot][:, :], k.iota_w[0:WROWS, 0:1], None,
                             ALU.is_equal)


def scatter_filtered(k, table):
    attr = k.ins["attr_rows"]
    depth = attr.shape[1]

    def one_pass():
        with Stage(k, "filt") as st:
            loads_begun = st.sem("loads_begun")
            dst_loaded = [st.sem(f"dst_loaded{i}") for i in range(RING)]
            win_loaded = [st.sem(f"win_loaded{i}") for i in range(RING)]
            attr_loaded = [st.sem(f"attr_loaded{i}") for i in range(2)]
            src_loaded = [st.sem(f"src_loaded{i}") for i in range(2)]
            scattered = [[st.pool_dma_sem(f"scattered{i}_{j}") for j in range(SUB)] for i in range(2)]
            onehot_t_ready, filter_ready, rows_ready = (st.sem("onehot_t_ready"), st.sem("filter_ready"),
                                                        st.sem("rows_ready"))
            copied, msg_ready, same_ready = st.sem("copied"), st.sem("msg_ready"), st.sem("same_ready")
            before_ready, row_picked, row_ready = st.sem("before_ready"), st.sem("row_picked"), st.sem("row_ready")
            joined, out_ready, begun = st.sem("joined"), st.sem("out_ready"), st.sem("scatters_begun")

            def same(t):
                return gathered(k, t.two, F)

            def out_rows(t):
                return k.g[t.slot][:, :, :].rearrange("p j f -> p (j f)")[:, SUB * F:].rearrange(
                    "p (j f) -> p j f", f=F)

            with st.block() as block:
                @block.sync
                def _(sp):
                    def loads(t):
                        at = window_base(k, sp, t)
                        wait_count(sp, rows_ready, t.t + 1 - RING)
                        sp.sem_inc(loads_begun, 1)
                        load_window(k, sp, table, at, dst_loaded, win_loaded, t)
                        wait_count(sp, filter_ready, t.t - 1)
                        sp.dma_start(k.attr[t.two][:, :],
                                     attr[bass.ds(t.t, 1), :, :].rearrange("o c e -> (o c) e")).then_inc(
                                         attr_loaded[t.two], 16)
                        wait_count(sp, before_ready, t.t - 1)
                        sp.sem_inc(loads_begun, 1)
                        sp.dma_start(k.src_row[t.two][:, :],
                                     k.ins["src_flat"][bass.ds(t.t, 1), :].to_broadcast([P, TILE])).then_inc(
                                         src_loaded[t.two], 16)
                    over_tiles(sp, k.tiles, [(0, loads)])

                @block.tensor
                def _(pe):
                    def filters(t):
                        pe.wait_ge(attr_loaded[t.two], (half_rounds(t) + 1) * 16)
                        wait_count(pe, msg_ready, t.t - 1)
                        for j in range(SUB):
                            mm = pe.matmul(k.bank[t.two][:, j * F:(j + 1) * F],
                                           k.attr[t.two][0:depth, j * P:(j + 1) * P],
                                           k.w["L3_gnn_k2f_W"][:, :], start=True, stop=True)
                        mm.then_inc(filter_ready, 1)
                        pe.wait_ge(onehot_t_ready, t.t + 1)
                        pe.wait_ge(win_loaded[t.slot], (t.rounds + 1) * 16)
                        wait_count(pe, copied, t.t - 1)
                        for j in range(SUB):
                            mm = pe.matmul(k.bank[2 + t.two][:, j * F:(j + 1) * F],
                                           k.onehot_t[t.two][:, j * P:(j + 1) * P], k.window[t.slot][:, 0:F],
                                           start=True, stop=True)
                        mm.then_inc(rows_ready, 1)

                    def join(t):
                        pe.wait_ge(msg_ready, t.t + 1)
                        pe.wait_ge(same_ready, t.t + 1)
                        wait_count(pe, out_ready, t.t - 1)
                        for j in range(SUB):
                            mm = pe.matmul(k.bank[4 + t.two][:, j * F:(j + 1) * F], same(t)[:, j, :],
                                           k.msg[t.two][:, j, :], start=True, stop=True)
                        mm.then_inc(joined, 1)
                    over_tiles(pe, k.tiles, [(2, join), (0, filters)])

                @block.scalar
                def _(act):
                    def copy_rows(t):
                        act.wait_ge(rows_ready, t.t + 1)
                        wait_count(act, msg_ready, t.t - 1)
                        act.copy(k.zact[t.two][:, 0, :], k.bank[2 + t.two][:, :]).then_inc(copied, 1)

                    def copy_out(t):
                        act.wait_ge(joined, t.t + 1)
                        for j in range(SUB):
                            wait_count(act, scattered[t.two][j], (half_rounds(t) - 1) * 16)
                        act.copy(out_rows(t).rearrange("p j f -> p (j f)"),
                                 k.bank[4 + t.two][:, :]).then_inc(out_ready, 1)
                    over_tiles(act, k.tiles, [(2, copy_out), (0, copy_rows)])

                @block.vector
                def _(dve):
                    def onehots(t):
                        wait_count(dve, rows_ready, t.t - 1)
                        dve.wait_ge(dst_loaded[t.slot], (t.rounds + 1) * 16)
                        make_onehot_t(k, dve, t).then_inc(onehot_t_ready, 1)

                    def messages(t):
                        mine = k.src_f[:, bass.ds(t.t * SUB, SUB)]
                        row = k.src_row[t.two][:, :].rearrange("p (j e) -> p j e", e=P)
                        wait_count(dve, joined, t.t - 1)
                        dve.wait_ge(src_loaded[t.two], (half_rounds(t) + 1) * 16)
                        dve.tensor_tensor(same(t), row, mine.unsqueeze(2).to_broadcast([P, SUB, P]),
                                          ALU.is_equal).then_inc(same_ready, 1)
                        dve.wait_ge(same_ready, t.t + 1)
                        wait_count(dve, row_picked, t.t)
                        dve.tensor_tensor(k.earlier[:, :, :], same(t), k.lower[:, :].unsqueeze(1).to_broadcast(
                            [P, SUB, P]), ALU.mult).then_inc(row_picked_in, 1)
                        dve.wait_ge(copied, t.t + 1)
                        dve.wait_ge(filter_ready, t.t + 1)
                        dve.tensor_tensor(k.msg[t.two][:, :, :],
                                          k.zact[t.two][:, 0, :].rearrange("p (j f) -> p j f", f=F),
                                          k.bank[t.two][:, :].rearrange("p (j f) -> p j f", f=F),
                                          ALU.mult).then_inc(msg_ready, 1)
                        dve.wait_ge(row_picked_in, t.t + 1)
                        dve.tensor_reduce(k.picked[:, 0:SUB], k.earlier[:, :, :], AX.X, ALU.add).then_inc(
                            before_ready, 1)
                        dve.tensor_scalar(k.picked[:, SUB:2 * SUB], mine, -1.0, k.spare[:, 0:1],
                                          ALU.mult, ALU.add).then_inc(away_ready, 1)
                        dve.wait_ge(away_ready, t.t + 1)
                        dve.scalar_tensor_tensor(out=k.picked[:, 2 * SUB:3 * SUB], in0=k.picked[:, 0:SUB], scalar=0.5,
                                                 in1=k.picked[:, SUB:2 * SUB], op0=ALU.is_gt,
                                                 op1=ALU.mult).then_inc(row_picked, 1)
                        dve.wait_ge(row_picked, t.t + 1)
                        for j in range(SUB):
                            wait_count(dve, scattered[t.two][j], (half_rounds(t) - 1) * 16)
                        dve.tensor_tensor(k.idx[t.slot][:, :], k.picked[:, 2 * SUB:3 * SUB], mine,
                                          ALU.add).then_inc(row_ready, 1)
                    row_picked_in, away_ready = st.sem("earlier_ready"), st.sem("away_ready")
                    over_tiles(dve, k.tiles, [(0, onehots), (1, messages)])

                @block.gpsimd
                def _(pool):
                    def scatter(t):
                        pool.wait_ge(out_ready, t.t + 1)
                        pool.wait_ge(row_ready, t.t + 1)
                        for j in range(SUB):
                            wait_count(pool, scattered[t.two][j], half_rounds(t) * 16)
                        pool.sem_inc(begun, 1)
                        for j in range(SUB):
                            pool.indirect_dma_start(
                                out=k.sums[t.two][j], out_offset=bass.IndirectOffsetOnAxis(
                                    ap=k.idx[t.slot][:, j:j + 1], axis=0),
                                in_=out_rows(t)[:, j, :], in_offset=None,
                                compute_op=ALU.add).then_inc(scattered[t.two][j], 16)
                    over_tiles(pool, k.tiles, [(1, scatter)])
                    for two in range(2):
                        for j in range(SUB):
                            pool.wait_ge(scattered[two][j], 16 * ceil_div(k.tiles - two, 2))
    repeated(k, one_pass, rows=True)


def score_edges(k, name, heads, table, table_dst, kept):
    nc = k.nc
    gat = name == "gat"
    width = F * (2 if gat else 1)
    zs = width // F
    att = k.att2 if gat else k.att1
    cols = SUB * heads

    def z_bank(t, h):
        return k.bank[h * 2 + t.two]

    def outside(t):
        return k.msg[t.two][:, heads + t.slot // 2, :]

    def one_pass():
        with Stage(k, name) as st:
            idx_loaded, gathers_begun, rows_loaded = gather_sems(st)
            loads_begun = st.sem("loads_begun")
            dst_loaded = [st.sem(f"dst_loaded{i}") for i in range(RING)]
            win_loaded = [st.sem(f"win_loaded{i}") for i in range(RING)]
            stored = [st.sem(f"stored{i}") for i in range(RING)]
            onehot_t_ready, z_ready, act_ready = st.sem("onehot_t_ready"), st.sem("z_ready"), st.sem("act_ready")
            slope_ready, score_ready = st.sem("slope_ready"), st.sem("score_ready")
            masked, added = st.sem("masked"), st.sem("added")
            onehot_ready, turned = st.sem("onehot_ready"), st.sem("turned")
            tops, tops_turned, tops_merged, best = (st.sem("tops"), st.sem("tops_turned"),
                                                    st.sem("tops_merged"), st.sem("best"))
            outside_ready, exclusive = st.sem("outside_ready"), st.sem("exclusive")
            with st.block() as block:
                @block.sync
                def _(sp):
                    def loads(t):
                        at = window_base(k, sp, t)
                        wait_count(sp, z_ready, t.t + 1 - RING)
                        sp.sem_inc(loads_begun, 1)
                        load_indices(k, sp, idx_loaded, t)
                        load_window(k, sp, table_dst, at, dst_loaded, win_loaded, t)

                    def keep(t):
                        for j in range(SUB):
                            sp.wait_ge(rows_loaded[t.slot][j], (t.rounds + 1) * 16)
                        sp.dma_start(kept[bass.ds(t.t, 1), :, :].rearrange("o p f -> (o p) f"),
                                     gathered(k, t.slot, width).rearrange("p j f -> p (j f)")).then_inc(
                                         stored[t.slot], 16)
                    over_tiles(sp, k.tiles, [(0, loads), (2, keep)])
                    for slot in range(RING):
                        sp.wait_ge(stored[slot], 16 * ceil_div(k.tiles - slot, RING))

                @block.gpsimd
                def _(pool):
                    def rows(t):
                        wait_count(pool, z_ready, t.t + 1 - RING)
                        wait_count(pool, stored[t.slot], t.rounds * 16)
                        gather(k, pool, table, width, idx_loaded, gathers_begun, rows_loaded, t)
                    over_tiles(pool, k.tiles, [(0, rows)])

                @block.tensor
                def _(pe):
                    def sums(t):
                        pe.wait_ge(win_loaded[t.slot], (t.rounds + 1) * 16)
                        pe.wait_ge(onehot_t_ready, t.t + 1)
                        wait_count(pe, act_ready, t.t - 1)
                        g = gathered(k, t.slot, width)
                        for j in range(SUB):
                            pe.wait_ge(rows_loaded[t.slot][j], (t.rounds + 1) * 16)
                            for h in range(zs):
                                pe.matmul(z_bank(t, h)[:, j * P:(j + 1) * P], g[:, j, h * F:(h + 1) * F],
                                          k.ident[:, :], is_transpose=True, start=(j == 0), stop=False,
                                          skip_group_check=True)
                        for h in range(zs):
                            mm = pe.matmul(z_bank(t, h)[:, :], k.window[t.slot][:, h * F:(h + 1) * F],
                                           k.onehot_t[t.two][:, :], start=False, stop=True,
                                           skip_group_check=True)
                        mm.then_inc(z_ready, 1)

                    def scores(t):
                        pe.wait_ge(act_ready, t.t + 1)
                        wait_count(pe, exclusive if gat else masked, t.t - 1)
                        for h in range(zs):
                            for j in range(SUB):
                                lhs = k.zact[t.two][:, h, j * P:(j + 1) * P]
                                if gat:
                                    mm = pe.matmul(k.bank[4 + t.two][:, h * SUB + j:h * SUB + j + 1], lhs,
                                                   att[:, h:h + 1], start=True, stop=True)
                                else:
                                    mm = pe.matmul(k.bank[4 + t.two][:, j * heads:(j + 1) * heads], lhs,
                                                   att[:, :], start=True, stop=True)
                        mm.then_inc(score_ready, 1)

                    def turn(t):
                        pe.wait_ge(exclusive, t.t + 1)
                        wait_count(pe, tops, t.t)
                        for h in range(heads):
                            mm = pe.transpose(k.bank[6][:, h * P:(h + 1) * P],
                                              k.msg[t.two][:, h, :], k.ident[:, :])
                        mm.then_inc(turned, 1)

                    def turn_tops(t):
                        pe.wait_ge(tops, t.t + 1)
                        wait_count(pe, best, t.t)
                        pe.transpose(k.bank[7][0:heads, 0:P], k.tops[:, t.two, :],
                                     k.ident[:, :]).then_inc(tops_turned, 1)
                    if gat:
                        over_tiles(pe, k.tiles, [(2, scores), (3, turn), (4, turn_tops), (0, sums)])
                    else:
                        over_tiles(pe, k.tiles, [(2, scores), (0, sums)])

                @block.scalar
                def _(act):
                    def activate(t):
                        act.wait_ge(z_ready, t.t + 1)
                        wait_count(act, score_ready, t.t - 1)
                        if gat:
                            for h in range(zs):
                                a = act.mul(k.zact[t.two][:, h, :], z_bank(t, h)[:, :], 0.2)
                            a.then_inc(slope_ready, 1)
                        else:
                            act.activation(k.zact[t.two][:, 0, :], z_bank(t, 0)[:, :],
                                           ACT.Tanh).then_inc(act_ready, 1)

                    def penalties(t):
                        act.wait_ge(onehot_ready, t.t + 1)
                        wait_count(act, exclusive, t.t + 1 - RING)
                        act.activation(outside(t), k.onehot[t.slot][:, :, :].rearrange("p j n -> p (j n)"),
                                       ACT.Copy, bias=-BIG, scale=BIG).then_inc(outside_ready, 1)
                    over_tiles(act, k.tiles, [(0, activate), (1, penalties)] if gat else [(0, activate)])

                @block.vector
                def _(dve):
                    def onehots(t):
                        wait_count(dve, z_ready, t.t - 1)
                        dve.wait_ge(dst_loaded[t.slot], (t.rounds + 1) * 16)
                        make_onehot_t(k, dve, t).then_inc(onehot_t_ready, 1)

                    def leaky(t):
                        wait_count(dve, outside_ready, t.t + 1 - RING)
                        make_onehot(k, dve, t).then_inc(onehot_ready, 1)
                        dve.wait_ge(slope_ready, t.t + 1)
                        for h in range(zs):
                            za = k.zact[t.two][:, h, :]
                            m = dve.tensor_tensor(za, za, z_bank(t, h)[:, :], ALU.max)
                        m.then_inc(act_ready, 1)

                    def pick(t):
                        dve.wait_ge(score_ready, t.t + 1)
                        s = k.bank[4 + t.two][:, 0:cols]
                        m = k.member[:, bass.ds(t.t * SUB, SUB)]
                        mine = k.scores[:, bass.ds(t.t * cols, cols)]
                        picked_s = k.picked[:, 0:cols]
                        if gat:
                            s = s.rearrange("p (h j) -> p h j", j=SUB)
                            m = m.unsqueeze(1).to_broadcast([P, heads, SUB])
                            ps = picked_s.rearrange("p (h j) -> p h j", j=SUB)
                        else:
                            s = s.rearrange("p (j h) -> p j h", h=heads)
                            m = m.unsqueeze(2).to_broadcast([P, SUB, heads])
                            ps = picked_s.rearrange("p (j h) -> p j h", h=heads)
                        wait_count(dve, added, t.t)
                        dve.tensor_tensor(ps, s, m, ALU.mult).then_inc(masked, 1)
                        if gat:
                            dve.wait_ge(outside_ready, t.t + 1)
                            wait_count(dve, turned, t.t - 1)
                            dve.tensor_tensor(k.msg[t.two][:, 0:heads, :].rearrange("p h (j n) -> p h j n", n=WIN),
                                              outside(t).rearrange("p (j n) -> p j n", n=WIN).unsqueeze(1)
                                              .to_broadcast([P, heads, SUB, WIN]),
                                              s.unsqueeze(3).to_broadcast([P, heads, SUB, WIN]),
                                              ALU.add).then_inc(exclusive, 1)
                        dve.wait_ge(masked, t.t + 1)
                        dve.tensor_tensor(mine, mine, picked_s, ALU.add).then_inc(added, 1)

                    def top(t):
                        dve.wait_ge(turned, t.t + 1)
                        wait_count(dve, tops_turned, t.t - 1)
                        dve.tensor_reduce(k.tops[:, t.two, :],
                                          k.bank[6][:, 0:heads * P].rearrange("p (h e) -> p h e", e=P),
                                          AX.X, ALU.max).then_inc(tops, 1)

                    def best_of_nodes(t):
                        at = window_base(k, dve, t)
                        dve.wait_ge(tops_turned, t.t + 1)
                        wait_count(dve, best, t.t)
                        dve.tensor_reduce(k.tile_top[:, :], k.bank[7][0:heads, 0:P].rearrange(
                            "h (j n) -> h n j", n=WIN), AX.X, ALU.max).then_inc(tops_merged, 1)
                        dve.wait_ge(tops_merged, t.t + 1)
                        m = k.node_top[:, bass.ds(at, WIN)]
                        dve.tensor_tensor(m, m, k.tile_top[:, :], ALU.max).then_inc(best, 1)
                    if gat:
                        over_tiles(dve, k.tiles, [(0, onehots), (1, leaky), (2, pick), (3, top),
                                                  (4, best_of_nodes)])
                    else:
                        over_tiles(dve, k.tiles, [(0, onehots), (2, pick)])
    repeated(k, one_pass, rows=True)


def kept_rows(k, sp, kept, width, rows_loaded, t):
    sp.dma_start(gathered(k, t.slot, width).rearrange("p j f -> p (j f)"),
                 kept[bass.ds(t.t, 1), :, :].rearrange("o p f -> (o p) f")).then_inc(rows_loaded[t.slot], 16)


def weigh_additive(k):
    heads, per_head = HEADS1, F // HEADS1

    def one_pass():
        with Stage(k, "addw") as st:
            rows_loaded = [st.sem(f"rows_loaded{i}") for i in range(RING)]
            weight_ready, onehot_ready, msg_ready = st.sem("weight_ready"), st.sem("onehot_ready"), st.sem("msg_ready")
            sums_ready, added = st.sem("sums_ready"), st.sem("added")
            with st.block() as block:
                @block.sync
                def _(sp):
                    def loads(t):
                        wait_count(sp, msg_ready, t.t + 1 - RING)
                        kept_rows(k, sp, k.kept1, F, rows_loaded, t)
                    over_tiles(sp, k.tiles, [(0, loads)])

                @block.scalar
                def _(act):
                    def weights(t):
                        wait_count(act, sums_ready, t.t - 1)
                        act.activation(k.weight[t.two][:, :],
                                       k.scores[:, bass.ds(t.t * SUB * heads, SUB * heads)],
                                       ACT.Exp).then_inc(weight_ready, 1)
                    over_tiles(act, k.tiles, [(0, weights)])

                @block.tensor
                def _(pe):
                    def sums(t):
                        pe.wait_ge(msg_ready, t.t + 1)
                        pe.wait_ge(onehot_ready, t.t + 1)
                        pe.wait_ge(weight_ready, t.t + 1)
                        wait_count(pe, added, t.t - 1)
                        for j in range(SUB):
                            pe.matmul(k.bank[t.two][:, 0:WIN], k.msg[t.two][:, j, :],
                                      k.onehot[t.slot][:, j, :], start=(j == 0), stop=(j == SUB - 1))
                        for j in range(SUB):
                            mm = pe.matmul(k.bank[t.two][0:heads, WIN:2 * WIN],
                                           k.weight[t.two][:, j * heads:(j + 1) * heads], k.onehot[t.slot][:, j, :], start=(j == 0), stop=(j == SUB - 1))
                        mm.then_inc(sums_ready, 1)
                    over_tiles(pe, k.tiles, [(0, sums)])

                @block.vector
                def _(dve):
                    def messages(t):
                        wait_count(dve, sums_ready, t.t - 1)
                        make_onehot(k, dve, t).then_inc(onehot_ready, 1)
                        dve.wait_ge(weight_ready, t.t + 1)
                        dve.wait_ge(rows_loaded[t.slot], (t.rounds + 1) * 16)
                        g = gathered(k, t.slot, F).rearrange("p j (h c) -> p (j h) c", h=heads)
                        dve.tensor_tensor(k.msg[t.two][:, :, :].rearrange("p j (h c) -> p (j h) c", h=heads), g,
                                          k.weight[t.two][:, :].unsqueeze(2).to_broadcast([P, SUB * heads, per_head]),
                                          ALU.mult).then_inc(msg_ready, 1)

                    def add(t):
                        at = window_base(k, dve, t)
                        dve.wait_ge(sums_ready, t.t + 1)
                        wait_count(dve, added, t.t)
                        a = k.acc[:, 0, bass.ds(at, WIN)]
                        dve.tensor_tensor(a, a, k.bank[t.two][:, 0:WIN], ALU.add)
                        z = k.node_sum1[:, bass.ds(at, WIN)]
                        dve.tensor_tensor(z, z, k.bank[t.two][0:heads, WIN:2 * WIN], ALU.add).then_inc(added, 1)
                    over_tiles(dve, k.tiles, [(0, messages), (1, add)])
    repeated(k, one_pass)


def weigh_gat(k):
    heads = HEADS2
    cols = heads * SUB

    def one_pass():
        with Stage(k, "gatw") as st:
            rows_loaded = [st.sem(f"rows_loaded{i}") for i in range(RING)]
            onehot_ready, spread, shift, arg = (st.sem("onehot_ready"), st.sem("spread"), st.sem("shift"),
                                                st.sem("arg"))
            arg_ready, weight_ready, scaled_ready = st.sem("arg_ready"), st.sem("weight_ready"), st.sem("scaled_ready")
            sums_ready, merged, added = st.sem("sums_ready"), st.sem("merged"), st.sem("added")
            with st.block() as block:
                @block.sync
                def _(sp):
                    def loads(t):
                        wait_count(sp, sums_ready, t.t + 1 - RING)
                        kept_rows(k, sp, k.kept2, 2 * F, rows_loaded, t)
                    over_tiles(sp, k.tiles, [(0, loads)])

                @block.scalar
                def _(act):
                    def weights(t):
                        act.wait_ge(arg_ready, t.t + 1)
                        wait_count(act, scaled_ready, t.t - 1)
                        act.activation(k.weight[t.two][:, 0:cols], k.shifted[t.two][:, :],
                                       ACT.Exp).then_inc(weight_ready, 1)
                    over_tiles(act, k.tiles, [(0, weights)])

                @block.tensor
                def _(pe):
                    def sums(t):
                        pe.wait_ge(scaled_ready, t.t + 1)
                        pe.wait_ge(rows_loaded[t.slot], (t.rounds + 1) * 16)
                        wait_count(pe, added, t.t - 1)
                        g = gathered(k, t.slot, 2 * F)
                        for h in range(heads):
                            for j in range(SUB):
                                pe.matmul(k.bank[t.two][:, h * WIN:(h + 1) * WIN], g[:, j, h * F:(h + 1) * F],
                                          k.scaled[t.slot][:, h, j, :], start=(j == 0), stop=(j == SUB - 1))
                        pe.matmul(k.bank[2 + t.two][:, 0:cols * WIN], k.ones[:, :],
                                  k.scaled[t.slot][:, :, :, :].rearrange("p h j n -> p (h j n)"),
                                  start=True, stop=True).then_inc(sums_ready, 1)
                    over_tiles(pe, k.tiles, [(1, sums)])

                @block.vector
                def _(dve):
                    def arguments(t):
                        at = window_base(k, dve, t)
                        make_onehot(k, dve, t).then_inc(onehot_ready, 1)
                        dve.wait_ge(onehot_ready, t.t + 1)
                        wait_count(dve, sums_ready, t.t + 1 - RING)
                        sc = k.scaled[t.slot][:, :, :, :]
                        dve.tensor_tensor(sc, k.onehot[t.slot][:, :, :].unsqueeze(1).to_broadcast([P, heads, SUB, WIN]),
                                          k.wide[:, :, bass.ds(at, WIN)].unsqueeze(2).to_broadcast([P, heads, SUB, WIN]),
                                          ALU.mult).then_inc(spread, 1)
                        dve.wait_ge(spread, t.t + 1)
                        wait_count(dve, arg_ready, t.t)
                        dve.tensor_reduce(k.picked[:, 0:cols], sc.rearrange("p h j n -> p (h j) n"), AX.X,
                                          ALU.add).then_inc(shift, 1)
                        dve.wait_ge(shift, t.t + 1)
                        dve.tensor_tensor(k.shifted[t.two][:, :], k.scores[:, bass.ds(t.t * cols, cols)],
                                          k.picked[:, 0:cols], ALU.subtract).then_inc(arg, 1)
                        dve.wait_ge(arg, t.t + 1)
                        dve.tensor_scalar(k.shifted[t.two][:, :], k.shifted[t.two][:, :], 1.0, None,
                                          ALU.min).then_inc(arg_ready, 1)

                    def scale(t):
                        dve.wait_ge(weight_ready, t.t + 1)
                        w = k.weight[t.two][:, 0:cols].rearrange("p (h j) -> p h j", j=SUB)
                        dve.tensor_tensor(k.scaled[t.slot][:, :, :, :],
                                          k.onehot[t.slot][:, :, :].unsqueeze(1).to_broadcast([P, heads, SUB, WIN]),
                                          w.unsqueeze(3).to_broadcast([P, heads, SUB, WIN]),
                                          ALU.mult).then_inc(scaled_ready, 1)

                    def add(t):
                        at = window_base(k, dve, t)
                        dve.wait_ge(sums_ready, t.t + 1)
                        wait_count(dve, added, t.t)
                        a = k.acc[:, :, bass.ds(at, WIN)]
                        dve.tensor_tensor(a, a, k.bank[t.two][:, 0:heads * WIN].rearrange(
                            "p (a n) -> p a n", n=WIN), ALU.add)
                        dve.tensor_reduce(k.tile_sum[:, :, :], k.bank[2 + t.two][:, 0:cols * WIN].rearrange(
                            "p (h j n) -> p h n j", j=SUB, n=WIN), AX.X, ALU.add).then_inc(merged, 1)
                        dve.wait_ge(merged, t.t + 1)
                        for h in range(heads):
                            z = k.node_sum[h][:, bass.ds(at, WIN)]
                            s = dve.tensor_tensor(z, z, k.tile_sum[:, h, :], ALU.add)
                        s.then_inc(added, 1)
                    over_tiles(dve, k.tiles, [(0, arguments), (1, scale), (3, add)])
    repeated(k, one_pass)



def gcn_layer(k):
    nc, B, N = k.nc, k.blocks, k.n_nodes
    layer_norm(k, "n0", k.x, k.h, relu=True)
    vector_stage(k, "deg0", lambda dve: dve.memset(k.acc[:, 0, :], 1.0))
    count_degrees(k)
    with Stage(k, "root") as st:
        rooted, inverted, turned = st.sem("rooted"), st.sem("inverted"), st.sem("turned")
        with st.block() as block:
            @block.scalar
            def _(act):
                act.sqrt(k.inv_sqrt_deg[:, :], k.acc[:, 0, :]).then_inc(rooted, 1)

            @block.vector
            def _(dve):
                dve.wait_ge(rooted, 1)
                dve.reciprocal(k.inv_sqrt_deg[:, :], k.inv_sqrt_deg[:, :]).then_inc(inverted, 1)
                dve.wait_ge(turned, 1)
                dve.tensor_copy(k.inv_sqrt_deg_nm[:, :], k.bank[0][:, 0:B])

            @block.tensor
            def _(pe):
                pe.wait_ge(inverted, 1)
                for b in range(B):
                    mm = pe.matmul(k.bank[0][:, b:b + 1], k.inv_sqrt_deg[0:1, b * P:(b + 1) * P],
                                   k.ones[0:1, 0:1], start=True, stop=True)
                mm.then_inc(turned, 1)
    own = k.wide[:, 0, :].rearrange("p (b f) -> p b f", f=F)
    vector_stage(k, "rows0", lambda dve: dve.tensor_tensor(
        own, k.h[:, :, :], k.inv_sqrt_deg_nm[:, :].unsqueeze(2).to_broadcast([P, B, F]), ALU.mult))
    store_table(k, "rows0", own, k.table1)
    to_feature_major(k, "own0", own, k.acc[:, 0, :])
    sum_neighbours(k, "agg0", k.table1)
    vector_stage(k, "deg1", lambda dve: dve.tensor_tensor(k.fa[:, :], k.acc[:, 0, :], k.inv_sqrt_deg[:, :], ALU.mult))
    linear(k, "gcn1", k.w["L0_gnn_W1"][:, :], k.fa,
           lambda act, lh, bank: act.activation(k.fb[:, lh[0]:lh[1]], bank, ACT.Relu,
                                                bias=k.w["L0_gnn_b1"][:, 0:1]), engine="scalar")
    vector_stage(k, "rows1", lambda dve: dve.tensor_tensor(k.acc[:, 0, :], k.fb[:, :], k.inv_sqrt_deg[:, :], ALU.mult))
    rows = k.wide[:, 0, :].rearrange("p (b f) -> p b f", f=F)
    turn_to_nodes(k, "turn1", k.acc[:, 0, :], rows)
    store_table(k, "rows1", rows, k.table1)
    sum_neighbours(k, "agg1", k.table1)
    vector_stage(k, "deg2", lambda dve: dve.tensor_tensor(k.fa[:, :], k.acc[:, 0, :], k.inv_sqrt_deg[:, :], ALU.mult))
    logits = k.wide[:, 0, :].rearrange("p (b f) -> p b f", f=F)
    product_stage(k, "gcn2", B,
                  lambda pe, b, bank: pe.matmul(bank[:, 0:F], k.fa[:, b * P:(b + 1) * P], k.w["L0_gnn_W2"][:, :],
                                                start=True, stop=True),
                  "vector",
                  lambda dve, b, bank: dve.tensor_tensor(logits[:, b, :], bank[:, 0:F], k.w["L0_gnn_b2"][:, :],
                                                         ALU.add))

    def wide(stat):
        return stat[:, :].unsqueeze(2).to_broadcast([P, B, F])

    with Stage(k, "soft") as st:
        step, raised = st.sem("step"), st.sem("raised")
        with st.block() as block:
            @block.vector
            def _(dve):
                dve.tensor_reduce(k.stat[:, :], logits, AX.X, ALU.max).then_inc(step, 1)
                dve.wait_ge(step, 1)
                dve.tensor_tensor(logits, logits, wide(k.stat), ALU.subtract).then_inc(step, 1)
                dve.wait_ge(raised, 1)
                dve.tensor_reduce(k.stat[:, :], logits, AX.X, ALU.add).then_inc(step, 1)
                dve.wait_ge(step, 3)
                dve.reciprocal(k.stat2[:, :], k.stat[:, :]).then_inc(step, 1)
                dve.wait_ge(step, 4)
                dve.tensor_tensor(logits, logits, wide(k.stat2), ALU.mult).then_inc(step, 1)
                dve.wait_ge(step, 5)
                dve.tensor_tensor(k.x[:, :, :], k.x[:, :, :], logits, ALU.add)

            @block.scalar
            def _(act):
                act.wait_ge(step, 2)
                act.activation(logits, logits, ACT.Exp).then_inc(raised, 1)


def turn_to_nodes(k, name, src, dst):
    def product(pe, c, bank):
        lo, hi = chunks(k.n_nodes)[c]
        for b in range(lo // P, hi // P):
            mm = pe.transpose(bank[:, b * P - lo:(b + 1) * P - lo], src[:, b * P:(b + 1) * P], k.ident[:, :])
        return mm

    def take(act, c, bank):
        lo, hi = chunks(k.n_nodes)[c]
        return act.copy(dst[:, lo // P:hi // P, :], bank[:, 0:hi - lo].rearrange("p (b f) -> p b f", f=F))

    product_stage(k, name, len(chunks(k.n_nodes)), product, "scalar", take)


def node_parts(k):
    h = k.h[:, :, :].rearrange("p b f -> p (b f)").bitcast(BF16)
    return [h[:, 0:k.n_nodes], h[:, k.n_nodes:], k.acc[:, 1, :].bitcast(BF16)[:, 0:k.n_nodes]]


def additive_layer(k):
    layer_norm(k, "n1", k.x, k.h, relu=True)
    to_feature_major(k, "turn2", k.h, k.fa)
    table_rows(k, "proj", k.fa, k.w["L1_gnn_W"][:, :], None, k.table1)
    store_parts(k, "proj_parts", k.wide[:, 0, :], k.wide[:, 1, :], node_parts(k), k.parts1)
    per_edge = k.tiles * SUB
    scores = k.scores[:, :].rearrange("p (e h) -> p e h", h=HEADS1)
    vector_stage(k, "pad1", lambda dve: dve.tensor_copy(
        scores, k.pad[:, :].unsqueeze(2).to_broadcast([P, per_edge, HEADS1])))
    score_edges(k, "add", HEADS1, k.table1, k.parts1, k.kept1)
    with Stage(k, "max1") as st:
        step, turned, spread = st.sem("step"), st.sem("turned"), st.sem("spread")
        top = k.small[:, 0:HEADS1]
        with st.block() as block:
            @block.vector
            def _(dve):
                dve.memset(k.small[:, :], 0.0)
                dve.memset(k.node_sum1[:, :], 0.0)
                dve.memset(k.acc[:, 0, :], 0.0).then_inc(step, 1)
                dve.wait_ge(step, 1)
                dve.tensor_reduce(top, scores.rearrange("p e h -> p h e"), AX.X, ALU.max).then_inc(step, 1)
                dve.wait_ge(turned, 1)
                dve.tensor_reduce(k.small[0:HEADS1, 8:9], k.bank[0][0:HEADS1, 0:P], AX.X, ALU.max).then_inc(step, 1)
                dve.wait_ge(step, 3)
                dve.tensor_scalar(k.small[0:HEADS1, 12:12 + HEADS1], k.ident[0:HEADS1, 0:HEADS1],
                                  k.small[0:HEADS1, 8:9], None, ALU.mult).then_inc(step, 1)
                dve.wait_ge(spread, 1)
                dve.tensor_copy(top, k.bank[1][:, 0:HEADS1]).then_inc(step, 1)
                dve.wait_ge(step, 5)
                dve.tensor_tensor(scores, scores, top.unsqueeze(1).to_broadcast([P, per_edge, HEADS1]), ALU.subtract)

            @block.tensor
            def _(pe):
                pe.wait_ge(step, 2)
                pe.transpose(k.bank[0][0:HEADS1, 0:P], top, k.ident[:, :]).then_inc(turned, 1)
                pe.wait_ge(step, 4)
                pe.matmul(k.bank[1][:, 0:HEADS1], k.ones[0:HEADS1, :], k.small[0:HEADS1, 12:12 + HEADS1],
                          start=True, stop=True).then_inc(spread, 1)
    weigh_additive(k)
    vector_stage(k, "norm1",
                 lambda dve: dve.tensor_scalar(k.node_sum1[:, :], k.node_sum1[:, :], 1e-12, None, ALU.max),
                 lambda dve: dve.reciprocal(k.node_sum1[:, :], k.node_sum1[:, :]))
    linear(k, "div1", k.head_block[:, :], k.node_sum1,
           lambda dve, lh, bank: dve.tensor_tensor(k.fa[:, lh[0]:lh[1]], k.acc[:, 0, lh[0]:lh[1]], bank, ALU.mult))
    add_to_nodes(k, "sum1", k.fa, k.x)


def gat_layer(k):
    N = k.n_nodes
    w = k.w
    layer_norm(k, "n2", k.x, k.h, relu=True)
    inner = k.acc[:, 0, :].rearrange("p (b f) -> p b f", f=F)
    layer_norm(k, "n2i", k.h, inner, relu=False)
    vector_stage(k, "res2", lambda dve: dve.tensor_tensor(k.x[:, :, :], k.x[:, :, :], k.h[:, :, :], ALU.add))
    to_feature_major(k, "turn3", inner, k.fa, func=ACT.Relu, scale=w["L2_gnn_gamma"][:, 0:1],
                     bias=w["L2_gnn_beta"][:, 0:1])
    table_rows(k, "left", k.fa, w["L2_gnn_Wl"][:, :], w["L2_gnn_bl"][:, :], k.table2)
    table_rows(k, "right", k.fa, w["L2_gnn_Wr"][:, :], w["L2_gnn_br"][:, :], None)
    wide = k.wide[:, :, :].rearrange("p a n -> p (a n)")
    store_parts(k, "right_parts", wide, wide,
                [k.acc[:, 0, :].bitcast(BF16), k.acc[:, 1, :].bitcast(BF16),
                 k.h[:, :, :].rearrange("p b f -> p (b f)").bitcast(BF16)], k.parts2)
    linear(k, "resw", w["L2_gnn_res_W"][:, :], k.fa,
           lambda act, lh, bank: act.activation(k.fb[:, lh[0]:lh[1]], bank, ACT.Identity,
                                                bias=w["L2_gnn_bias"][:, 0:1]), engine="scalar")
    scores = k.scores[:, 0:k.tiles * SUB * HEADS2].rearrange("p (t h j) -> p t h j", h=HEADS2, j=SUB)
    vector_stage(k, "pad2",
                 lambda dve: dve.tensor_copy(scores[:, :, 0, :], k.pad[:, :].rearrange("p (t j) -> p t j", j=SUB)),
                 lambda dve: dve.tensor_copy(scores[:, :, 1, :], k.pad[:, :].rearrange("p (t j) -> p t j", j=SUB)),
                 lambda dve: dve.memset(k.node_top[:, :], -BIG))
    score_edges(k, "gat", HEADS2, k.table2, k.parts2, k.kept2)
    cs = chunks(N)

    def spread_rows(name, rows, dst):
        def product(pe, c, bank):
            h, (lo, hi) = c // len(cs), cs[c % len(cs)]
            return pe.matmul(bank[:, 0:hi - lo], k.head_row[:, h * P:(h + 1) * P], rows[:, lo:hi],
                             start=True, stop=True)

        def take(act, c, bank):
            h, (lo, hi) = c // len(cs), cs[c % len(cs)]
            return act.copy(dst[:, h, lo:hi], bank[:, 0:hi - lo])
        product_stage(k, name, HEADS2 * len(cs), product, "scalar", take)

    spread_rows("tops2", k.node_top, k.wide)
    vector_stage(k, "zero2", lambda dve: dve.memset(k.acc[:, :, :], 0.0),
                 lambda dve: dve.memset(k.node_sum[0], 0.0), lambda dve: dve.memset(k.node_sum[1], 0.0))
    weigh_gat(k)
    for h in range(HEADS2):
        vector_stage(k, f"norm2{h}",
                     lambda dve: dve.tensor_scalar(k.node_sum[h], k.node_sum[h], 1e-16, None, ALU.add),
                     lambda dve: dve.reciprocal(k.node_sum[h], k.node_sum[h]),
                     lambda dve: dve.scalar_tensor_tensor(out=k.acc[:, h, :], in0=k.acc[:, h, :],
                                                          scalar=1.0 / HEADS2, in1=k.node_sum[h],
                                                          op0=ALU.mult, op1=ALU.mult))
    vector_stage(k, "mean2",
                 lambda dve: dve.tensor_tensor(k.acc[:, 0, :], k.acc[:, 0, :], k.acc[:, 1, :], ALU.add),
                 lambda dve: dve.tensor_tensor(k.fb[:, :], k.fb[:, :], k.acc[:, 0, :], ALU.add))
    add_to_nodes(k, "sum2", k.fb, k.x)


def ssp_linear(k, name, src, weight, bias, dst, residual, scratch, keep=None):
    cs = chunks(k.n_nodes)
    low, soft = scratch
    soft = keep if keep is not None else soft
    with Stage(k, name) as st:
        folded, raised, logged, soft_ready = st.sem("folded"), st.sem("raised"), st.sem("logged"), st.sem("soft_ready")
        ready, taken = st.sem("ready"), st.sem("taken")
        with st.block() as block:
            @block.scalar
            def _(act):
                for c, (lo, hi) in enumerate(cs):
                    act.wait_ge(folded, c + 1)
                    act.activation(low[:, lo:hi], low[:, lo:hi], ACT.Exp).then_inc(raised, 1)
                    act.wait_ge(raised, c + 1)
                    act.activation(low[:, lo:hi], low[:, lo:hi], ACT.Ln, bias=k.half[:, 0:1],
                                   scale=0.5).then_inc(logged, 1)

            @block.tensor
            def _(pe):
                for c, (lo, hi) in enumerate(cs):
                    pe.wait_ge(soft_ready, c + 1)
                    pe.matmul(k.bank[c][:, 0:hi - lo], weight, soft[:, lo:hi], start=True,
                              stop=True).then_inc(ready, 1)

            @block.vector
            def _(dve):
                for lo, hi in cs:
                    dve.scalar_tensor_tensor(out=low[:, lo:hi], in0=src[:, lo:hi], scalar=-1.0, in1=src[:, lo:hi],
                                             op0=ALU.mult, op1=ALU.min).then_inc(folded, 1)
                for c in range(len(cs) + 1):
                    if c < len(cs):
                        lo, hi = cs[c]
                        dve.wait_ge(logged, c + 1)
                        dve.scalar_tensor_tensor(out=soft[:, lo:hi], in0=src[:, lo:hi], scalar=0.0,
                                                 in1=low[:, lo:hi], op0=ALU.max, op1=ALU.add).then_inc(soft_ready, 1)
                    if c > 0:
                        lo, hi = cs[c - 1]
                        dve.wait_ge(ready, c)
                        if residual is None:
                            dve.tensor_scalar(dst[:, lo:hi], k.bank[c - 1][:, 0:hi - lo], bias, None,
                                              ALU.add).then_inc(taken, 1)
                        else:
                            dve.scalar_tensor_tensor(out=dst[:, lo:hi], in0=k.bank[c - 1][:, 0:hi - lo],
                                                     scalar=bias, in1=residual[:, lo:hi], op0=ALU.add,
                                                     op1=ALU.add).then_inc(taken, 1)


def load_sources(k):
    B, nq = k.blocks, k.tiles * SUB
    raw = k.scores[:, 0:nq].bitcast(I32)
    k.src_f = k.scores[:, nq:2 * nq]
    k.earlier = k.fb[:, 0:SUB * P].rearrange("p (j e) -> p j e", e=P)
    zeros = k.wide[:, 0, :]
    with Stage(k, "srcs") as st:
        loaded, cleared, zeroed = st.sem("loaded"), st.sem("cleared"), st.sem("zeroed")
        with st.block() as block:
            @block.vector
            def _(dve):
                dve.memset(zeros, 0.0).then_inc(cleared, 1)
                dve.tensor_scalar(k.spare[:, :], k.iota_p[:, :], float(k.n_nodes), None, ALU.add)
                dve.wait_ge(loaded, 16)
                dve.tensor_copy(k.src_f, raw)

            @block.sync
            def _(sp):
                sp.dma_start(raw, k.ins["src_edges"]).then_inc(loaded, 16)
                sp.wait_ge(cleared, 1)
                for two in k.sums:
                    for table in two:
                        sp.dma_start(table[0:k.n_nodes, :].rearrange("(b p) f -> p b f", p=P),
                                     zeros.rearrange("p (b f) -> p b f", f=F)).then_inc(zeroed, 16)
                        sp.dma_start(table[k.n_nodes:k.n_nodes + P, :], zeros[:, 0:F]).then_inc(zeroed, 16)
                sp.wait_ge(loaded, 16)
                sp.wait_ge(zeroed, 32 * 2 * SUB)


def collect_sums(k):
    tables = [table for two in k.sums for table in two]
    total = k.h
    with Stage(k, "coll") as st:
        loaded = [st.sem(f"loaded{i}") for i in range(3)]
        added = st.sem("added")
        bufs = [k.wide[:, 0, :], k.wide[:, 1, :], k.acc[:, 1, :]]
        with st.block() as block:
            @block.sync
            def _(sp):
                for n, table in enumerate(tables):
                    wait_count(sp, added, n - 2)
                    sp.dma_start(bufs[n % 3].rearrange("p (b f) -> p b f", f=F),
                                 table[0:k.n_nodes, :].rearrange("(b p) f -> p b f", p=P)).then_inc(loaded[n % 3], 16)

            @block.vector
            def _(dve):
                for n in range(len(tables)):
                    dve.wait_ge(loaded[n % 3], 16 * (n // 3 + 1))
                    wait_count(dve, added, n)
                    buf = bufs[n % 3].rearrange("p (b f) -> p b f", f=F)
                    if n == 0:
                        dve.tensor_copy(total[:, :, :], buf).then_inc(added, 1)
                    else:
                        dve.tensor_tensor(total[:, :, :], total[:, :, :], buf, ALU.add).then_inc(added, 1)

    def product(pe, c, bank):
        lo, hi = chunks(k.n_nodes)[c]
        for b in range(lo // P, hi // P):
            mm = pe.transpose(bank[:, b * P - lo:(b + 1) * P - lo], total[:, b, :], k.ident[:, :])
        return mm

    def take(dve, c, bank):
        lo, hi = chunks(k.n_nodes)[c]
        a = k.acc[:, 0, lo:hi]
        return dve.tensor_tensor(a, a, bank[:, 0:hi - lo], ALU.add)

    product_stage(k, "collt", len(chunks(k.n_nodes)), product, "vector", take)


def interaction_layer(k):
    w = k.w
    layer_norm(k, "n3", k.x, k.h, relu=True)
    to_feature_major(k, "turn4", k.h, k.fa)
    scratch = (k.wide[:, 0, :], k.wide[:, 1, :])
    m = k.acc[:, 0, :]
    ssp_linear(k, "xi", k.fa, w["L3_gnn_Wi"][:, :], w["L3_gnn_bi"][:, 0:1], m, None, scratch, keep=k.fb)
    table_rows(k, "xj", k.fb, w["L3_gnn_Wj"][:, :], w["L3_gnn_bj"][:, :], None)
    store_parts(k, "xj_parts", k.wide[:, 0, :], k.wide[:, 0, :], node_parts(k), k.parts1)
    load_sources(k)
    scatter_filtered(k, k.parts1)
    collect_sums(k)
    mid = k.acc[:, 1, :]
    for l in range(k.ins["L3_gnn_res_int_W1"].shape[0]):
        ssp_linear(k, f"ri{l}a", m, w[f"L3_gnn_res_int_W1{l}"][:, :], w[f"L3_gnn_res_int_b1{l}"][:, 0:1], mid,
                   None, scratch)
        ssp_linear(k, f"ri{l}b", mid, w[f"L3_gnn_res_int_W2{l}"][:, :], w[f"L3_gnn_res_int_b2{l}"][:, 0:1], m,
                   m, scratch)
    vector_stage(k, "gate", lambda dve: dve.tensor_scalar(k.fa[:, :], k.fa[:, :], w["L3_gnn_u"][:, 0:1], None,
                                                          ALU.mult))
    ssp_linear(k, "dense", m, w["L3_gnn_dense_W"][:, :], w["L3_gnn_dense_b"][:, 0:1], k.fa, k.fa, scratch)
    for l in range(k.ins["L3_gnn_res_at_W1"].shape[0]):
        ssp_linear(k, f"ra{l}a", k.fa, w[f"L3_gnn_res_at_W1{l}"][:, :], w[f"L3_gnn_res_at_b1{l}"][:, 0:1], mid,
                   None, scratch)
        ssp_linear(k, f"ra{l}b", mid, w[f"L3_gnn_res_at_W2{l}"][:, :], w[f"L3_gnn_res_at_b2{l}"][:, 0:1], k.fa,
                   k.fa, scratch)
    add_to_nodes(k, "sum3", k.fa, k.x)


def store_nodes(k):
    n = k.out.shape[0]
    full = n // P
    with Stage(k, "out") as st:
        stored = st.sem("stored")
        with st.block() as block:
            @block.sync
            def _(sp):
                sp.dma_start(k.out[0:full * P, :].rearrange("(b p) f -> p b f", p=P),
                             k.x[:, 0:full, :]).then_inc(stored, 16)
                sp.dma_start(k.out[full * P:n, :], k.x[0:n - full * P, full, :]).then_inc(stored, 16)
                sp.wait_ge(stored, 32)


def gnn_kernel(nc, ins, out, n_edges):
    with ExitStack() as ctx:
        k = Kernel(nc, ctx, ins, out)
        load_everything(k)
        choose_passes(k, n_edges)
        gcn_layer(k)
        additive_layer(k)
        gat_layer(k)
        interaction_layer(k)
        store_nodes(k)


def kernel(**inputs):
    import numpy as _np
    import concourse.bacc as _bacc
    from concourse import mybir as _mybir
    from concourse.bass_utils import run_bass_kernel_spmd as _run

    arrays = {name: _np.ascontiguousarray(a) for name, a in inputs.items()}
    x, src, dst, attr = (arrays.pop(name) for name in ("x", "src", "dst", "edge_attr_64"))
    n, f = x.shape
    n_edges, depth = attr.shape
    blocks, tiles = ceil_div(n, P), ceil_div(n_edges, TILE)

    x_rows = _np.zeros((blocks * P, f), x.dtype)
    x_rows[:n] = x
    arrays["x"] = _np.ascontiguousarray(x_rows.reshape(blocks, P, f).transpose(1, 0, 2))
    src_rows, dst_rows = _np.zeros(tiles * TILE, src.dtype), _np.full(tiles * TILE, -1, dst.dtype)
    src_rows[:n_edges], dst_rows[:n_edges] = src, dst
    arrays["src_rows"] = _np.ascontiguousarray(src_rows.reshape(tiles, SUB, P).transpose(0, 2, 1))
    arrays["src_flat"] = src_rows.reshape(tiles, TILE)
    arrays["src_edges"] = _np.ascontiguousarray(
        src_rows.reshape(tiles, SUB, P).transpose(2, 0, 1).reshape(P, tiles * SUB))
    arrays["dst_first"] = _np.ascontiguousarray(dst_rows[::TILE].reshape(1, tiles))
    arrays["dst_edges"] = _np.ascontiguousarray(
        dst_rows.reshape(tiles, SUB, P).transpose(2, 0, 1).reshape(P, tiles * SUB))
    attr_rows = _np.zeros((tiles * TILE, depth), attr.dtype)
    attr_rows[:n_edges] = attr
    arrays["attr_rows"] = _np.ascontiguousarray(attr_rows.reshape(tiles, TILE, depth).transpose(0, 2, 1))

    nc = _bacc.Bacc("TRN2", target_bir_lowering=False, num_devices=1)
    ins = {name: nc.dram_tensor(f"in_{name}", a.shape, _mybir.dt.from_np(a.dtype), kind="ExternalInput").ap()
           for name, a in arrays.items()}
    out = nc.dram_tensor("out_nodes", (n, f), _mybir.dt.from_np(x.dtype), kind="ExternalOutput").ap()
    gnn_kernel(nc, ins, out, n_edges)
    r = _run(nc, [{f"in_{name}": a for name, a in arrays.items()}], core_ids=[0])
    return r.results[0]["out_nodes"]
```

```python
from contextlib import ExitStack

import numpy as np

import concourse.bass as bass
from concourse import mybir

ALU = mybir.AluOpType
ACT = mybir.ActivationFunctionType
AX = mybir.AxisListType
F32 = mybir.dt.float32
I32 = mybir.dt.int32
BF16 = mybir.dt.bfloat16

P = 128
F = 128
WIN = 32
PARTS = 3
WROWS = WIN * PARTS
SUB = 4
TILE = P * SUB
RING = 4
DIGIT = 64
COUNT = 2 * SUB
ROUND = 1.5 * 2 ** 23
BIG = 1e30
CHUNK = 512
BANKS = 8
LN_EPS = 1e-5
HEADS1 = 4
HEADS2 = 2


def ceil_div(a, b):
    return -(-a // b)


class Tile:

    def __init__(self, t, slot, rounds):
        self.t, self.slot, self.rounds = t, slot, rounds
        self.two = slot % 2


def over_tiles(eng, tiles, stages, head=1):
    full = tiles // RING

    def step(s_round, s_slot, static):
        for lag, stage in stages:
            slot = (s_slot - lag) % RING
            rounds = s_round if s_slot >= lag else s_round - 1
            t = rounds * RING + slot
            if not static or 0 <= t < tiles:
                stage(Tile(t, slot, rounds))

    for s in range(head * RING):
        step(s // RING, s % RING, True)
    with eng.Fori(head, full) as i:
        for s in range(RING):
            step(i, s, False)
    for s in range(full * RING, tiles + max(lag for lag, _ in stages)):
        step(s // RING, s % RING, True)


def wait_count(eng, sem, count):
    if not isinstance(count, int) or count > 0:
        eng.wait_ge(sem, count)


class Kernel:

    def __init__(self, nc, ctx, ins, out):
        self.nc, self.ctx, self.ins, self.out = nc, ctx, ins, out
        self.n_nodes = ins["x"].shape[1] * P
        self.blocks = ins["x"].shape[1]
        self.tiles = ins["src_rows"].shape[0]

    def sb(self, name, shape, dt=F32):
        return self.ctx.enter_context(self.nc.sbuf_tensor(name, shape, dt))


class Stage:

    def __init__(self, k, name):
        self.k, self.nc, self.name = k, k.nc, name
        self.ctx, self.sems, self.pool_dma = ExitStack(), [], []

    def sem(self, name):
        s = self.ctx.enter_context(self.nc.semaphore(f"{self.name}_{name}"))
        self.sems.append(s)
        return s

    def pool_dma_sem(self, name):
        s = self.sem(name)
        self.pool_dma.append(s)
        return s

    def __enter__(self):
        return self

    def block(self):
        return self.nc.Block(f"{self.name}_{self.nc.next_id()}", no_gpsimd_drain=not self.pool_dma)

    def clear(self):
        for s in self.pool_dma:
            self.nc.gpsimd.dma_reset(range(s.num, s.num + 1))
        for s in self.sems:
            self.nc.gpsimd.sem_clear(s)
        self.nc.all_engine_barrier()

    def __exit__(self, *exc):
        if exc[0] is None:
            self.clear()
        self.ctx.close()
        return False



def load_everything(k):
    nc, ins = k.nc, k.ins
    B, T, N = k.blocks, k.tiles, k.n_nodes
    k.bank = [k.ctx.enter_context(nc.psum_tensor(f"bank{i}", [P, CHUNK], F32)) for i in range(BANKS)]
    k.x = k.sb("x_nm", [P, B, F])
    k.h = k.sb("h_nm", [P, B, F])
    k.fa = k.sb("fm_a", [P, N])
    k.fb = k.sb("fm_b", [P, N])
    k.acc = k.sb("acc", [P, 2, N])
    k.inv_sqrt_deg = k.sb("inv_sqrt_deg_fm", [P, N])
    k.inv_sqrt_deg_nm = k.sb("inv_sqrt_deg_nm", [P, B])
    k.scores = k.sb("scores", [P, T * SUB * HEADS1])
    k.stat = k.sb("stat", [P, B])
    k.stat2 = k.sb("stat2", [P, B])
    k.wide = k.sb("wide", [P, 2, N])
    k.dst_i = k.scores[:, 0:T * SUB].bitcast(I32)
    k.dst_f = k.sb("dst_f", [P, T * SUB])
    k.pad = k.sb("pad", [P, T * SUB])
    k.local = k.sb("local", [P, T * SUB])
    k.member = k.sb("member", [P, T * SUB])
    k.first = k.sb("first", [P, T])
    k.base = k.sb("base", [P, T])
    k.base_i = k.sb("base_i", [P, T], I32)
    k.first_i = k.base_i
    k.win_off = k.sb("win_off", [P, 1])
    k.win_step = k.sb("win_step", [P, 1])
    k.passes_i = k.sb("passes_i", [P, 1], I32)
    k.spare = k.sb("spare", [P, 1])
    k.small = k.sb("small", [P, 16])
    k.picked = k.sb("picked", [P, SUB * HEADS1])
    k.tops = k.sb("tops", [P, 2, HEADS2])
    k.tile_top = k.sb("tile_top", [HEADS2, WIN])
    k.node_top = k.inv_sqrt_deg[0:HEADS2, :]
    k.node_sum = k.fa[0:HEADS2, :]
    k.top_rows = k.wide[:, 0, 0:2 * B * HEADS2].rearrange("p (a n) -> p a n", a=2)
    k.top_parts = k.wide[:, 1, :].bitcast(BF16)[:, 0:B * PARTS * HEADS2].rearrange(
        "p (b c h) -> p b c h", c=PARTS, h=HEADS2)
    k.node_sum1 = k.inv_sqrt_deg[0:HEADS1, :]
    k.shifted = [k.sb(f"shifted{i}", [P, SUB * HEADS2]) for i in range(2)]
    k.weight = [k.sb(f"weight{i}", [P, SUB * HEADS1]) for i in range(RING)]
    k.iota_i = k.sb("iota_i", [P, DIGIT], I32)
    k.iota_d = k.sb("iota_d", [P, DIGIT], BF16)
    k.iota_n = k.sb("iota_n", [P, WIN])
    k.iota_pi = k.sb("iota_pi", [P, 1], I32)
    k.iota_p = k.sb("iota_p", [P, 1])
    k.iota_w = k.sb("iota_w", [P, 1])
    k.ident = k.sb("ident", [P, P])
    k.ones = k.sb("ones", [P, P])
    k.lower = k.sb("lower", [P, P])
    k.eps = k.sb("eps", [P, 1])
    k.half = k.sb("half", [P, 1])
    k.head_row = k.sb("head_row", [HEADS2, HEADS2 * P])
    k.head_block = k.sb("head_block", [HEADS1, F])
    k.idx = [k.sb(f"idx{i}", [P, SUB], I32) for i in range(RING)]
    k.g = [k.sb(f"gathered{i}", [P, SUB, 2 * F]) for i in range(RING)]
    k.onehot = [k.sb(f"onehot{i}", [P, SUB, WIN]) for i in range(RING)]
    k.msg = [k.sb(f"msg{i}", [P, SUB, F]) for i in range(2)]
    k.dst_row = [k.sb(f"dst_row{i}", [WROWS, TILE], BF16) for i in range(RING)]
    k.onehot_t = [k.sb(f"onehot_t{i}", [WROWS, TILE], BF16) for i in range(2)]
    k.window = [k.sb(f"window{i}", [WROWS, 2 * F], BF16) for i in range(RING)]
    k.zact = [k.sb(f"zact{i}", [P, 2, TILE]) for i in range(2)]
    k.tile_rows = [k.zact[i][0:WIN, 0, 0:HEADS2 * F] for i in range(2)]
    k.scaled = [k.zact[i % 2][:, 1, (i // 2) * TILE // 2:(i // 2 + 1) * TILE // 2].rearrange(
        "p (h j n) -> p h j n", h=HEADS2, j=SUB) for i in range(RING)]
    k.src_row = [k.zact[i][:, 1, :].bitcast(I32) for i in range(2)]
    k.attr = [k.sb(f"attr{i}", [64, TILE]) for i in range(2)]
    k.table1 = nc.dram_tensor("table1", [N, F], F32).ap()
    k.table2 = nc.dram_tensor("table2", [N, 2 * F], F32).ap()
    k.parts1 = nc.dram_tensor("parts1", [N, PARTS, F], BF16).ap()
    k.parts2 = nc.dram_tensor("parts2", [N, PARTS, 2 * F], BF16).ap()
    k.isd = nc.dram_tensor("isd", [N], F32).ap()
    k.parts_top = nc.dram_tensor("parts_top", [N, PARTS, HEADS2], BF16).ap()
    k.local_rows = nc.dram_tensor("local_rows", [T, TILE], BF16).ap()
    k.sums = [[nc.dram_tensor(f"sums{i}_{j}", [N + P, F], F32).ap() for j in range(SUB)] for i in range(2)]
    k.kept1 = nc.dram_tensor("kept1", [T, P, SUB * F], F32).ap()
    k.kept2 = nc.dram_tensor("kept2", [T, P, SUB * 2 * F], F32).ap()

    k.w = {}
    loads = []

    def weight(name, src, shape):
        k.w[name] = k.sb("w_" + name, shape)
        loads.append((k.w[name], src))

    for name in ("L0_gnn_W1", "L0_gnn_W2", "L1_gnn_W", "L2_gnn_Wl", "L2_gnn_Wr", "L2_gnn_res_W",
                 "L3_gnn_k2f_W", "L3_gnn_Wi", "L3_gnn_Wj", "L3_gnn_dense_W"):
        weight(name, ins[name], list(ins[name].shape))
    for name in ("L3_gnn_res_int_W1", "L3_gnn_res_int_W2", "L3_gnn_res_at_W1", "L3_gnn_res_at_W2"):
        for l in range(ins[name].shape[0]):
            weight(f"{name}{l}", ins[name][l], [F, F])
    for name in ("L0_gnn_b1", "L2_gnn_gamma", "L2_gnn_beta", "L2_gnn_bias", "L3_gnn_bi", "L3_gnn_dense_b",
                 "L3_gnn_u"):
        weight(name, ins[name].rearrange("(f o) -> f o", o=1), [F, 1])
    for name in ("L3_gnn_res_int_b1", "L3_gnn_res_int_b2", "L3_gnn_res_at_b1", "L3_gnn_res_at_b2"):
        for l in range(ins[name].shape[0]):
            weight(f"{name}{l}", ins[name][l].rearrange("(f o) -> f o", o=1), [F, 1])
    for name in ("L0_gnn_b2", "L2_gnn_bl", "L2_gnn_br", "L3_gnn_bj"):
        n = ins[name].shape[0]
        weight(name, ins[name].rearrange("(o f) -> o f", o=1).to_broadcast([P, n]), [P, n])
    k.att1 = k.sb("att1", [F, HEADS1])
    k.att1_col = k.sb("att1_col", [F, 1])
    loads.append((k.att1_col, ins["L1_gnn_att"].rearrange("h (c o) -> (h c) o", o=1)))
    k.att2_rows = k.sb("att2_rows", [HEADS2, F])
    k.att2 = k.sb("att2", [F, HEADS2])
    loads.append((k.att2_rows, ins["L2_gnn_att"]))
    loads.append((k.x, ins["x"]))
    loads.append((k.dst_i, ins["dst_edges"]))
    loads.append((k.first_i, ins["dst_first"].to_broadcast([P, T])))

    per_head = F // HEADS1
    with Stage(k, "setup") as st:
        loaded, made, done, flat = st.sem("loaded"), st.sem("made"), st.sem("done"), st.sem("flat")
        cast = st.sem("cast")
        with st.block() as block:
            @block.sync
            def _(sp):
                with nc.allow_non_contiguous_dma(reason="bias and attention columns, first destinations"):
                    for dst, src in loads:
                        full = dst[:, :, :] if len(dst.shape) == 3 else dst[:, :]
                        sp.dma_start(full, src).then_inc(loaded, 16)
                sp.wait_ge(loaded, 16 * len(loads))

            @block.gpsimd
            def _(pool):
                pool.iota(k.iota_i[:, :], pattern=[[1, DIGIT]], base=0, channel_multiplier=0).then_inc(made, 1)
                pool.iota(k.iota_pi[:, :], pattern=[[0, 1]], base=0, channel_multiplier=1).then_inc(made, 1)
                pool.memset(k.ident[:, :], 0.0).then_inc(flat, 1)
                pool.memset(k.ones[:, :], 1.0)
                pool.memset(k.lower[:, :], 1.0)
                pool.memset(k.eps[:, :], LN_EPS)
                pool.memset(k.half[:, :], 0.5)
                pool.memset(k.head_block[:, :], 1.0)
                pool.memset(k.head_row[:, :], 1.0).then_inc(flat, 1)
                pool.memset(k.att1[:, :], 1.0).then_inc(flat, 1)
                pool.wait_ge(flat, 3)
                pool.affine_select(out=k.ident[:, :], in_=k.ident[:, :], compare_op=ALU.not_equal, fill=1.0,
                                   base=0, pattern=[[-1, P]], channel_multiplier=1)
                pool.affine_select(out=k.lower[:, :], in_=k.lower[:, :], compare_op=ALU.is_ge, fill=0.0,
                                   base=-1, pattern=[[-1, P]], channel_multiplier=1)
                pool.affine_select(out=k.head_row[:, :], in_=k.head_row[:, :], compare_op=ALU.is_ge, fill=0.0,
                                   base=0, pattern=[[1, HEADS2 * P]], channel_multiplier=-P).then_inc(flat, 1)
                pool.affine_select(out=k.head_block[:, :], in_=k.head_block[:, :], compare_op=ALU.is_ge, fill=0.0,
                                   base=0, pattern=[[1, F]], channel_multiplier=-per_head).then_inc(flat, 1)
                pool.affine_select(out=k.att1[:, :], in_=k.att1[:, :], compare_op=ALU.is_ge, fill=0.0,
                                   base=0, pattern=[[-per_head, HEADS1]], channel_multiplier=1).then_inc(flat, 1)
                pool.wait_ge(flat, 6)
                pool.affine_select(out=k.head_block[:, :], in_=k.head_block[:, :], compare_op=ALU.is_ge, fill=0.0,
                                   base=per_head - 1, pattern=[[-1, F]], channel_multiplier=per_head)
                pool.affine_select(out=k.head_row[:, :], in_=k.head_row[:, :], compare_op=ALU.is_ge, fill=0.0,
                                   base=P - 1, pattern=[[-1, HEADS2 * P]], channel_multiplier=P)
                pool.affine_select(out=k.att1[:, :], in_=k.att1[:, :], compare_op=ALU.is_ge, fill=0.0,
                                   base=per_head - 1, pattern=[[per_head, HEADS1]],
                                   channel_multiplier=-1).then_inc(made, 1)

            @block.tensor
            def _(pe):
                pe.wait_ge(loaded, 16 * len(loads))
                pe.wait_ge(made, 3)
                pe.transpose(k.bank[1][:, 0:HEADS2], k.att2_rows[:, :],
                             k.ident[0:HEADS2, 0:HEADS2]).then_inc(done, 1)

            @block.vector
            def _(dve):
                dve.wait_ge(made, 3)
                dve.tensor_copy(k.iota_n[:, :], k.iota_i[:, 0:WIN])
                dve.tensor_copy(k.iota_d[:, :], k.iota_i[:, :])
                dve.tensor_copy(k.iota_p[:, :], k.iota_pi[:, :]).then_inc(cast, 1)
                dve.wait_ge(cast, 1)
                dve.tensor_scalar(k.iota_w[:, :], k.iota_p[:, :], -1.0, 1.0 / PARTS, ALU.add,
                                  ALU.mult).then_inc(cast, 1)
                dve.wait_ge(cast, 2)
                dve.tensor_scalar(k.iota_w[:, :], k.iota_w[:, :], ROUND, None, ALU.add).then_inc(cast, 1)
                dve.wait_ge(cast, 3)
                dve.tensor_scalar(k.iota_w[:, :], k.iota_w[:, :], -ROUND, None, ALU.add)
                dve.wait_ge(loaded, 16 * len(loads))
                dve.tensor_scalar(k.att1[:, :], k.att1[:, :], k.att1_col[:, 0:1], None, ALU.mult)
                dve.tensor_copy(k.first[:, :], k.first_i[:, :])
                dve.tensor_copy(k.dst_f[:, :], k.dst_i[:, :]).then_inc(cast, 1)
                dve.memset(k.win_off[:, :], 0.0)
                dve.memset(k.win_step[:, :], 0.0)
                dve.wait_ge(done, 1)
                dve.tensor_copy(k.att2[:, :], k.bank[1][:, 0:HEADS2])
                dve.wait_ge(cast, 4)
                dve.tensor_scalar(k.pad[:, :], k.dst_f[:, :], 0.0, -BIG, ALU.is_lt, ALU.mult)


def place_windows(k):
    nc, T = k.nc, k.tiles
    with Stage(k, "windows") as st:
        placed, local = st.sem("placed"), st.sem("local")
        with st.block() as block:
            @block.vector
            def _(dve):
                dve.tensor_scalar(k.base[:, :], k.first[:, :], k.win_off[:, 0:1], None, ALU.add).then_inc(placed, 1)
                dve.wait_ge(placed, 1)
                dve.tensor_tensor(k.local[:, :].rearrange("p (t j) -> p t j", j=SUB),
                                  k.dst_f[:, :].rearrange("p (t j) -> p t j", j=SUB),
                                  k.base[:, :].unsqueeze(2).to_broadcast([P, T, SUB]),
                                  ALU.subtract).then_inc(local, 1)
                dve.tensor_scalar(k.base_i[:, :], k.base[:, :], 0.0, float(k.n_nodes - WIN), ALU.max, ALU.min)
                dve.tensor_scalar(k.win_off[:, :], k.win_off[:, :], k.win_step[:, 0:1], None, ALU.add)
                dve.wait_ge(local, 1)
                dve.tensor_scalar(k.member[:, :], k.local[:, :], 0.0, None, ALU.is_ge).then_inc(placed, 1)
                dve.wait_ge(placed, 2)
                dve.scalar_tensor_tensor(out=k.member[:, :], in0=k.local[:, :], scalar=float(WIN),
                                         in1=k.member[:, :], op0=ALU.is_lt, op1=ALU.mult)


def store_local_rows(k):
    nc, cols = k.nc, k.tiles * SUB
    blocks = ceil_div(cols, P)
    rows = k.wide[:, 0, :].bitcast(BF16)[:, 0:blocks * P]
    with Stage(k, "locals") as st:
        turned, copied, stored = st.sem("turned"), st.sem("copied"), st.sem("stored")
        with st.block() as block:
            @block.tensor
            def _(pe):
                for b in range(blocks):
                    n = min(P, cols - b * P)
                    pe.transpose(k.bank[b][0:n, 0:P], k.local[:, b * P:b * P + n], k.ident[:, :]).then_inc(turned, 1)

            @block.scalar
            def _(act):
                for b in range(blocks):
                    n = min(P, cols - b * P)
                    act.wait_ge(turned, b + 1)
                    act.copy(rows[0:n, b * P:(b + 1) * P], k.bank[b][0:n, 0:P]).then_inc(copied, 1)

            @block.sync
            def _(sp):
                flat = k.local_rows.rearrange("t (j e) -> (t j) e", e=P)
                for b in range(blocks):
                    n = min(P, cols - b * P)
                    sp.wait_ge(copied, b + 1)
                    sp.dma_start(flat[b * P:b * P + n, :], rows[0:n, b * P:(b + 1) * P]).then_inc(stored, 16)
                sp.wait_ge(stored, 16 * blocks)


def choose_passes(k, n_edges):
    nc = k.nc
    passes = ceil_div(k.n_nodes, WIN)
    place_windows(k)
    with Stage(k, "choice") as st:
        counted, summed, step = st.sem("counted"), st.sem("summed"), st.sem("step")
        with st.block() as block:
            @block.vector
            def _(dve):
                dve.tensor_reduce(k.small[:, 0:1], k.member[:, :], AX.X, ALU.add).then_inc(counted, 1)
                dve.wait_ge(summed, 1)
                dve.tensor_scalar(k.small[:, 1:2], k.bank[0][:, 0:1], float(n_edges), None,
                                  ALU.is_equal).then_inc(step, 1)
                dve.wait_ge(step, 1)
                dve.tensor_scalar(k.passes_i[:, :], k.small[:, 1:2], float(1 - passes), float(passes),
                                  ALU.mult, ALU.add)
                dve.tensor_scalar(k.win_step[:, :], k.small[:, 1:2], float(-WIN), float(WIN), ALU.mult, ALU.add)
                dve.tensor_scalar(k.first[:, :], k.first[:, :], k.small[:, 1:2], None, ALU.mult)

            @block.tensor
            def _(pe):
                pe.wait_ge(counted, 1)
                pe.matmul(k.bank[0][:, 0:1], k.ones[:, :], k.small[:, 0:1], start=True,
                          stop=True).then_inc(summed, 1)
    k.passes = nc.values_load(k.passes_i[0:1, 0:1], min_val=1, max_val=passes,
                              skip_runtime_bounds_check_because="it is 1 or the number of windows")


def reset_windows(k):
    with Stage(k, "rewind") as st:
        with st.block() as block:
            @block.vector
            def _(dve):
                dve.memset(k.win_off[:, :], 0.0)



def chunks(n):
    return [(c, min(c + CHUNK, n)) for c in range(0, n, CHUNK)]


def product_stage(k, name, count, product, engine, take):
    with Stage(k, name) as st:
        ready, taken = st.sem("product_ready"), st.sem("product_taken")

        with st.block() as block:
            @block.tensor
            def _(pe):
                for c in range(count):
                    wait_count(pe, taken, c + 1 - BANKS)
                    product(pe, c, k.bank[c % BANKS]).then_inc(ready, 1)

            def taker(eng):
                for c in range(count):
                    eng.wait_ge(ready, c + 1)
                    take(eng, c, k.bank[c % BANKS]).then_inc(taken, 1)

            if engine == "scalar":
                @block.scalar
                def _(act):
                    taker(act)
            else:
                @block.vector
                def _(dve):
                    taker(dve)


def to_feature_major(k, name, src, dst, func=None, scale=1.0, bias=0.0):
    def product(pe, c, bank):
        lo, hi = chunks(k.n_nodes)[c]
        for b in range(lo // P, hi // P):
            mm = pe.transpose(bank[:, b * P - lo:(b + 1) * P - lo], src[:, b, :], k.ident[:, :])
        return mm

    def take(act, c, bank):
        lo, hi = chunks(k.n_nodes)[c]
        if func is None:
            return act.copy(dst[:, lo:hi], bank[:, 0:hi - lo])
        return act.activation(dst[:, lo:hi], bank[:, 0:hi - lo], func, bias=bias, scale=scale)

    product_stage(k, name, len(chunks(k.n_nodes)), product, "scalar", take)


def add_to_nodes(k, name, src, dst):
    def product(pe, c, bank):
        lo, hi = chunks(k.n_nodes)[c]
        for b in range(lo // P, hi // P):
            mm = pe.transpose(bank[:, b * P - lo:(b + 1) * P - lo], src[:, b * P:(b + 1) * P], k.ident[:, :])
        return mm

    def take(dve, c, bank):
        lo, hi = chunks(k.n_nodes)[c]
        d = dst[:, lo // P:hi // P, :]
        return dve.tensor_tensor(d, d, bank[:, 0:hi - lo].rearrange("p (b f) -> p b f", f=F), ALU.add)

    product_stage(k, name, len(chunks(k.n_nodes)), product, "vector", take)


def linear(k, name, weight, src, take, engine="vector"):
    def product(pe, c, bank):
        lo, hi = chunks(k.n_nodes)[c]
        return pe.matmul(bank[:, 0:hi - lo], weight, src[:, lo:hi], start=True, stop=True)

    product_stage(k, name, len(chunks(k.n_nodes)), product, engine,
                  lambda eng, c, bank: take(eng, chunks(k.n_nodes)[c], bank[:, 0:chunks(k.n_nodes)[c][1] - chunks(k.n_nodes)[c][0]]))


def table_rows(k, name, src, weight, bias, table):
    width = weight.shape[1]
    rows = k.wide[:, :, :].rearrange("p a n -> p (a n)")[:, 0:k.blocks * width]
    def product(pe, c, bank):
        return pe.matmul(bank[:, 0:width], src[:, c * P:(c + 1) * P], weight, start=True, stop=True)

    def take(dve, c, bank):
        d = rows[:, c * width:(c + 1) * width]
        if bias is None:
            return dve.tensor_copy(d, bank[:, 0:width])
        return dve.tensor_tensor(d, bank[:, 0:width], bias, ALU.add)

    product_stage(k, name, k.blocks, product, "vector", take)
    if table is not None:
        store_table(k, name, rows.rearrange("p (b f) -> p b f", f=width), table)


def store_table(k, name, rows, table):
    with Stage(k, name + "_store") as st:
        stored = st.sem("stored")
        with st.block() as block:
            @block.sync
            def _(sp):
                sp.dma_start(table.rearrange("(b p) f -> p b f", p=P), rows).then_inc(stored, 16)
                sp.wait_ge(stored, 16)


def store_parts(k, name, rows, rest, parts, table):
    width = table.shape[2]
    groups = [(b, min(b + 5, k.blocks)) for b in range(0, k.blocks, 5)]
    G = len(groups)

    def cut(a, g):
        return a[:, groups[g][0] * width:groups[g][1] * width]

    with Stage(k, name) as st:
        rounded, left, stored = ([st.sem(f"rounded{c}") for c in range(PARTS)],
                                 [st.sem(f"left{c}") for c in range(PARTS - 1)], st.sem("stored"))
        with st.block() as block:
            @block.scalar
            def _(act):
                for g in range(G):
                    act.copy(cut(parts[0], g), cut(rows, g)).then_inc(rounded[0], 1)
                for c in range(1, PARTS):
                    for g in range(G):
                        act.wait_ge(left[c - 1], g + 1)
                        act.copy(cut(parts[c], g), cut(rest, g)).then_inc(rounded[c], 1)

            @block.vector
            def _(dve):
                for c in range(PARTS - 1):
                    for g in range(G):
                        dve.wait_ge(rounded[c], g + 1)
                        if c > 0:
                            dve.wait_ge(left[c - 1], g + 1)
                        dve.tensor_tensor(cut(rest, g), cut(rows if c == 0 else rest, g), cut(parts[c], g),
                                          ALU.subtract).then_inc(left[c], 1)

            @block.sync
            def _(sp):
                to = table.rearrange("(b p) c f -> p b c f", p=P)
                for c in range(PARTS):
                    sp.wait_ge(rounded[c], G)
                    sp.dma_start(to[:, :, c, :], parts[c].rearrange("p (b f) -> p b f", f=width)).then_inc(stored, 16)
                sp.wait_ge(stored, 16 * PARTS)


def layer_norm(k, name, src, dst, relu):
    B = k.blocks
    sq = k.wide[:, 0, :].rearrange("p (b f) -> p b f", f=F)
    cen = k.wide[:, 1, :].rearrange("p (b f) -> p b f", f=F)

    def wide(stat):
        return stat[:, :].unsqueeze(2).to_broadcast([P, B, F])

    with Stage(k, name) as st:
        step, squared, rooted = st.sem("step"), st.sem("squared"), st.sem("rooted")
        with st.block() as block:
            @block.vector
            def _(dve):
                dve.tensor_reduce(k.stat[:, :], src[:, :, :], AX.X, ALU.add).then_inc(step, 1)
                dve.wait_ge(step, 1)
                dve.tensor_scalar(k.stat[:, :], k.stat[:, :], 1.0 / F, None, ALU.mult).then_inc(step, 1)
                dve.wait_ge(step, 2)
                dve.tensor_tensor(cen, src[:, :, :], wide(k.stat), ALU.subtract).then_inc(step, 1)
                dve.wait_ge(squared, 1)
                dve.tensor_reduce(k.stat[:, :], sq, AX.X, ALU.add).then_inc(step, 1)
                dve.wait_ge(rooted, 1)
                dve.reciprocal(k.stat2[:, :], k.stat2[:, :]).then_inc(step, 1)
                dve.wait_ge(step, 5)
                if relu:
                    dve.scalar_tensor_tensor(out=dst[:, :, :], in0=cen, scalar=0.0, in1=wide(k.stat2),
                                             op0=ALU.max, op1=ALU.mult)
                else:
                    dve.tensor_tensor(dst[:, :, :], cen, wide(k.stat2), ALU.mult)

            @block.scalar
            def _(act):
                act.wait_ge(step, 3)
                act.square(sq, cen).then_inc(squared, 1)
                act.wait_ge(step, 4)
                act.activation(k.stat2[:, :], k.stat[:, :], ACT.Sqrt, bias=k.eps[:, 0:1],
                               scale=1.0 / F).then_inc(rooted, 1)


def vector_stage(k, name, *ops):
    with Stage(k, name) as st:
        step = st.sem("step")
        with st.block() as block:
            @block.vector
            def _(dve):
                for n, op in enumerate(ops):
                    wait_count(dve, step, n)
                    op(dve).then_inc(step, 1)



def gathered(k, slot, width):
    return k.g[slot][:, :, :].rearrange("p j f -> p (j f)")[:, 0:SUB * width].rearrange(
        "p (j f) -> p j f", f=width)


def load_indices(k, sp, idx_loaded, t):
    sp.dma_start(k.idx[t.slot][:, :],
                 k.ins["src_rows"][bass.ds(t.t, 1), :, :].rearrange("o p j -> (o p) j")).then_inc(
                     idx_loaded[t.slot], 16)


def gather(k, pool, table, width, idx_loaded, gathers_begun, rows_loaded, t):
    pool.wait_ge(idx_loaded[t.slot], (t.rounds + 1) * 16)
    pool.sem_inc(gathers_begun, 1)
    g = gathered(k, t.slot, width)
    for j in range(SUB):
        pool.indirect_dma_start(out=g[:, j, :], out_offset=None, in_=table,
                                in_offset=bass.IndirectOffsetOnAxis(ap=k.idx[t.slot][:, j:j + 1], axis=0)
                                ).then_inc(rows_loaded[t.slot][j], 16)


def gather_sems(st):
    idx_loaded = [st.sem(f"idx_loaded{i}") for i in range(RING)]
    rows_loaded = [[st.pool_dma_sem(f"rows_loaded{i}_{j}") for j in range(SUB)] for i in range(RING)]
    return idx_loaded, st.sem("gathers_begun"), rows_loaded


def make_onehot(k, dve, t):
    return dve.tensor_tensor(k.onehot[t.slot][:, :, :],
                             k.local[:, bass.ds(t.t * SUB, SUB)].unsqueeze(2).to_broadcast([P, SUB, WIN]),
                             k.iota_n[:, :].unsqueeze(1).to_broadcast([P, SUB, WIN]), ALU.is_equal)


def window_base(k, eng, t):
    return eng.value_load(k.base_i[0:1, bass.ds(t.t, 1)], min_val=0, max_val=k.n_nodes - WIN)


def repeated(k, one_pass, rows=False):
    reset_windows(k)
    with k.nc.Fori(0, k.passes):
        place_windows(k)
        if rows:
            store_local_rows(k)
        one_pass()


def count_degrees(k):
    nc, cols, highs = k.nc, k.tiles * SUB, k.n_nodes // DIGIT
    steps = cols // COUNT
    high_f, work = k.wide[:, 0, 0:cols], k.wide[:, 1, 0:cols]
    high, low = k.acc[:, 0, :].bitcast(BF16)[:, 0:cols], k.acc[:, 1, :].bitcast(BF16)[:, 0:cols]
    found = k.h[0:highs, 0, 0:DIGIT]

    def rows(t, n, offset):
        return k.g[t.slot][:, :, :].rearrange("p j f -> p (j f)").bitcast(BF16)[
            :, offset:offset + COUNT * n].rearrange("p (c n) -> p c n", n=n)

    def high_rows(t):
        return rows(t, highs, 0)

    def low_rows(t):
        return rows(t, DIGIT, COUNT * highs)

    def one_hots(eng, out, digits, n, t):
        return eng.tensor_tensor(out, digits[:, bass.ds(t.t * COUNT, COUNT)].unsqueeze(2).to_broadcast([P, COUNT, n]),
                                 k.iota_d[:, 0:n].unsqueeze(1).to_broadcast([P, COUNT, n]), ALU.is_equal)

    with Stage(k, "deg") as st:
        step, digits, high_ready, low_ready, counted = (st.sem("step"), st.sem("digits"), st.sem("high_ready"),
                                                        st.sem("low_ready"), st.sem("counted"))
        rooted, inverted, stored, spread = st.sem("rooted"), st.sem("inverted"), st.sem("stored"), st.sem("spread")
        with st.block() as block:
            @block.vector
            def _(dve):
                dve.tensor_scalar(work, k.dst_f[:, :], 1.0 / DIGIT, -(DIGIT - 1) / (2.0 * DIGIT), ALU.mult,
                                  ALU.add).then_inc(step, 1)
                dve.wait_ge(step, 1)
                dve.tensor_scalar(work, work, ROUND, None, ALU.add).then_inc(step, 1)
                dve.wait_ge(step, 2)
                dve.tensor_scalar(high_f, work, -ROUND, None, ALU.add).then_inc(step, 1)
                dve.wait_ge(step, 3)
                dve.tensor_copy(high, high_f).then_inc(digits, 1)
                dve.scalar_tensor_tensor(out=low, in0=high_f, scalar=-float(DIGIT), in1=k.dst_f[:, :],
                                         op0=ALU.mult, op1=ALU.add).then_inc(digits, 1)
                dve.wait_ge(digits, 2)

                def both(t):
                    wait_count(dve, counted, t.t + 1 - RING)
                    one_hots(dve, high_rows(t), high, highs, t).then_inc(high_ready, 1)
                    one_hots(dve, low_rows(t), low, DIGIT, t).then_inc(low_ready, 1)
                over_tiles(dve, steps, [(0, both)])
                dve.wait_ge(rooted, 1)
                dve.reciprocal(found, found).then_inc(inverted, 1)

            @block.tensor
            def _(pe):
                def counts(t):
                    pe.wait_ge(high_ready, t.t + 1)
                    pe.wait_ge(low_ready, t.t + 1)
                    for c in range(COUNT):
                        first = isinstance(t.t, int) and t.t == 0 and c == 0
                        mm = pe.matmul(k.bank[0][0:highs, 0:DIGIT], high_rows(t)[:, c, :], low_rows(t)[:, c, :],
                                       start=first, stop=c == COUNT - 1, skip_group_check=True)
                    mm.then_inc(counted, 1)
                over_tiles(pe, steps, [(0, counts)])

            @block.scalar
            def _(act):
                act.wait_ge(counted, steps)
                act.activation(found, k.bank[0][0:highs, 0:DIGIT], ACT.Sqrt, bias=k.ones[0:highs, 0:1],
                               scale=1.0).then_inc(rooted, 1)

            @block.sync
            def _(sp):
                sp.wait_ge(inverted, 1)
                sp.dma_start(k.isd.rearrange("(h l) -> h l", l=DIGIT), found).then_inc(stored, 16)
                sp.wait_ge(stored, 16)
                with nc.allow_non_contiguous_dma(reason="one number per node"):
                    sp.dma_start(k.inv_sqrt_deg[:, :], k.isd.rearrange("(o n) -> o n", o=1).to_broadcast(
                        [P, k.n_nodes])).then_inc(spread, 16)
                    sp.dma_start(k.inv_sqrt_deg_nm[:, :], k.isd.rearrange("(b p) -> p b", p=P)).then_inc(spread, 16)
                sp.wait_ge(spread, 32)


def sum_neighbours(k, name, table):
    def one_pass():
        with Stage(k, name) as st:
            idx_loaded, gathers_begun, rows_loaded = gather_sems(st)
            onehot_ready, sums_ready, added = st.sem("onehot_ready"), st.sem("sums_ready"), st.sem("added")
            with st.block() as block:
                @block.sync
                def _(sp):
                    def indices(t):
                        wait_count(sp, sums_ready, t.t + 1 - RING)
                        load_indices(k, sp, idx_loaded, t)
                    over_tiles(sp, k.tiles, [(0, indices)])

                @block.gpsimd
                def _(pool):
                    def rows(t):
                        wait_count(pool, sums_ready, t.t + 1 - RING)
                        gather(k, pool, table, F, idx_loaded, gathers_begun, rows_loaded, t)
                    over_tiles(pool, k.tiles, [(0, rows)])

                @block.tensor
                def _(pe):
                    def sums(t):
                        pe.wait_ge(onehot_ready, t.t + 1)
                        wait_count(pe, added, t.t - 1)
                        g = gathered(k, t.slot, F)
                        for j in range(SUB):
                            pe.wait_ge(rows_loaded[t.slot][j], (t.rounds + 1) * 16)
                            mm = pe.matmul(k.bank[t.two][:, 0:WIN], g[:, j, :], k.onehot[t.slot][:, j, :],
                                           start=(j == 0), stop=(j == SUB - 1))
                        mm.then_inc(sums_ready, 1)
                    over_tiles(pe, k.tiles, [(0, sums)])

                @block.vector
                def _(dve):
                    def onehot(t):
                        wait_count(dve, sums_ready, t.t - 1)
                        make_onehot(k, dve, t).then_inc(onehot_ready, 1)

                    def add(t):
                        at = window_base(k, dve, t)
                        dve.wait_ge(sums_ready, t.t + 1)
                        wait_count(dve, added, t.t)
                        a = k.acc[:, 0, bass.ds(at, WIN)]
                        dve.tensor_tensor(a, a, k.bank[t.two][:, 0:WIN], ALU.add).then_inc(added, 1)
                    over_tiles(dve, k.tiles, [(0, onehot), (1, add)])
    repeated(k, one_pass)


def half_rounds(t):
    return t.rounds * 2 + (1 if t.slot >= 2 else 0)


def load_window(k, sp, table, at, dst_loaded, win_loaded, t):
    width = table.shape[2]
    sp.dma_start(k.dst_row[t.slot][:, :],
                 k.local_rows[bass.ds(t.t, 1), :].to_broadcast([WROWS, TILE])).then_inc(dst_loaded[t.slot], 16)
    sp.dma_start(k.window[t.slot][:, 0:width],
                 table[bass.ds(at, WIN), :, :].rearrange("n c f -> (n c) f")).then_inc(win_loaded[t.slot], 16)


def make_onehot_t(k, dve, t):
    return dve.tensor_scalar(k.onehot_t[t.two][:, :], k.dst_row[t.slot][:, :], k.iota_w[0:WROWS, 0:1], None,
                             ALU.is_equal)


def scatter_filtered(k, table):
    attr = k.ins["attr_rows"]
    depth = attr.shape[1]

    def one_pass():
        with Stage(k, "filt") as st:
            loads_begun = st.sem("loads_begun")
            dst_loaded = [st.sem(f"dst_loaded{i}") for i in range(RING)]
            win_loaded = [st.sem(f"win_loaded{i}") for i in range(RING)]
            attr_loaded = [st.sem(f"attr_loaded{i}") for i in range(2)]
            src_loaded = [st.sem(f"src_loaded{i}") for i in range(2)]
            scattered = [[st.pool_dma_sem(f"scattered{i}_{j}") for j in range(SUB)] for i in range(2)]
            onehot_t_ready, filter_ready, rows_ready = (st.sem("onehot_t_ready"), st.sem("filter_ready"),
                                                        st.sem("rows_ready"))
            copied, msg_ready, same_ready = st.sem("copied"), st.sem("msg_ready"), st.sem("same_ready")
            before_ready, row_picked, row_ready = st.sem("before_ready"), st.sem("row_picked"), st.sem("row_ready")
            joined, out_ready, begun = st.sem("joined"), st.sem("out_ready"), st.sem("scatters_begun")

            def same(t):
                return gathered(k, t.two, F)

            def out_rows(t):
                return k.g[t.slot][:, :, :].rearrange("p j f -> p (j f)")[:, SUB * F:].rearrange(
                    "p (j f) -> p j f", f=F)

            with st.block() as block:
                @block.sync
                def _(sp):
                    def loads(t):
                        at = window_base(k, sp, t)
                        wait_count(sp, rows_ready, t.t + 1 - RING)
                        sp.sem_inc(loads_begun, 1)
                        load_window(k, sp, table, at, dst_loaded, win_loaded, t)
                        wait_count(sp, filter_ready, t.t - 1)
                        sp.dma_start(k.attr[t.two][:, :],
                                     attr[bass.ds(t.t, 1), :, :].rearrange("o c e -> (o c) e")).then_inc(
                                         attr_loaded[t.two], 16)
                        wait_count(sp, before_ready, t.t - 1)
                        sp.sem_inc(loads_begun, 1)
                        sp.dma_start(k.src_row[t.two][:, :],
                                     k.ins["src_flat"][bass.ds(t.t, 1), :].to_broadcast([P, TILE])).then_inc(
                                         src_loaded[t.two], 16)
                    over_tiles(sp, k.tiles, [(0, loads)])

                @block.tensor
                def _(pe):
                    def filters(t):
                        pe.wait_ge(attr_loaded[t.two], (half_rounds(t) + 1) * 16)
                        wait_count(pe, msg_ready, t.t - 1)
                        for j in range(SUB):
                            mm = pe.matmul(k.bank[t.two][:, j * F:(j + 1) * F],
                                           k.attr[t.two][0:depth, j * P:(j + 1) * P],
                                           k.w["L3_gnn_k2f_W"][:, :], start=True, stop=True)
                        mm.then_inc(filter_ready, 1)
                        pe.wait_ge(onehot_t_ready, t.t + 1)
                        pe.wait_ge(win_loaded[t.slot], (t.rounds + 1) * 16)
                        wait_count(pe, copied, t.t - 1)
                        for j in range(SUB):
                            mm = pe.matmul(k.bank[2 + t.two][:, j * F:(j + 1) * F],
                                           k.onehot_t[t.two][:, j * P:(j + 1) * P], k.window[t.slot][:, 0:F],
                                           start=True, stop=True)
                        mm.then_inc(rows_ready, 1)

                    def join(t):
                        pe.wait_ge(msg_ready, t.t + 1)
                        pe.wait_ge(same_ready, t.t + 1)
                        wait_count(pe, out_ready, t.t - 1)
                        for j in range(SUB):
                            mm = pe.matmul(k.bank[4 + t.two][:, j * F:(j + 1) * F], same(t)[:, j, :],
                                           k.msg[t.two][:, j, :], start=True, stop=True)
                        mm.then_inc(joined, 1)
                    over_tiles(pe, k.tiles, [(2, join), (0, filters)])

                @block.scalar
                def _(act):
                    def copy_rows(t):
                        act.wait_ge(rows_ready, t.t + 1)
                        wait_count(act, msg_ready, t.t - 1)
                        act.copy(k.zact[t.two][:, 0, :], k.bank[2 + t.two][:, :]).then_inc(copied, 1)

                    def copy_out(t):
                        act.wait_ge(joined, t.t + 1)
                        for j in range(SUB):
                            wait_count(act, scattered[t.two][j], (half_rounds(t) - 1) * 16)
                        act.copy(out_rows(t).rearrange("p j f -> p (j f)"),
                                 k.bank[4 + t.two][:, :]).then_inc(out_ready, 1)
                    over_tiles(act, k.tiles, [(2, copy_out), (0, copy_rows)])

                @block.vector
                def _(dve):
                    def onehots(t):
                        wait_count(dve, rows_ready, t.t - 1)
                        dve.wait_ge(dst_loaded[t.slot], (t.rounds + 1) * 16)
                        make_onehot_t(k, dve, t).then_inc(onehot_t_ready, 1)

                    def messages(t):
                        mine = k.src_f[:, bass.ds(t.t * SUB, SUB)]
                        row = k.src_row[t.two][:, :].rearrange("p (j e) -> p j e", e=P)
                        wait_count(dve, joined, t.t - 1)
                        dve.wait_ge(src_loaded[t.two], (half_rounds(t) + 1) * 16)
                        dve.tensor_tensor(same(t), row, mine.unsqueeze(2).to_broadcast([P, SUB, P]),
                                          ALU.is_equal).then_inc(same_ready, 1)
                        dve.wait_ge(same_ready, t.t + 1)
                        wait_count(dve, row_picked, t.t)
                        dve.tensor_tensor(k.earlier[:, :, :], same(t), k.lower[:, :].unsqueeze(1).to_broadcast(
                            [P, SUB, P]), ALU.mult).then_inc(row_picked_in, 1)
                        dve.wait_ge(copied, t.t + 1)
                        dve.wait_ge(filter_ready, t.t + 1)
                        dve.tensor_tensor(k.msg[t.two][:, :, :],
                                          k.zact[t.two][:, 0, :].rearrange("p (j f) -> p j f", f=F),
                                          k.bank[t.two][:, :].rearrange("p (j f) -> p j f", f=F),
                                          ALU.mult).then_inc(msg_ready, 1)
                        dve.wait_ge(row_picked_in, t.t + 1)
                        dve.tensor_reduce(k.picked[:, 0:SUB], k.earlier[:, :, :], AX.X, ALU.add).then_inc(
                            before_ready, 1)
                        dve.tensor_scalar(k.picked[:, SUB:2 * SUB], mine, -1.0, k.spare[:, 0:1],
                                          ALU.mult, ALU.add).then_inc(away_ready, 1)
                        dve.wait_ge(away_ready, t.t + 1)
                        dve.scalar_tensor_tensor(out=k.picked[:, 2 * SUB:3 * SUB], in0=k.picked[:, 0:SUB], scalar=0.5,
                                                 in1=k.picked[:, SUB:2 * SUB], op0=ALU.is_gt,
                                                 op1=ALU.mult).then_inc(row_picked, 1)
                        dve.wait_ge(row_picked, t.t + 1)
                        for j in range(SUB):
                            wait_count(dve, scattered[t.two][j], (half_rounds(t) - 1) * 16)
                        dve.tensor_tensor(k.idx[t.slot][:, :], k.picked[:, 2 * SUB:3 * SUB], mine,
                                          ALU.add).then_inc(row_ready, 1)
                    row_picked_in, away_ready = st.sem("earlier_ready"), st.sem("away_ready")
                    over_tiles(dve, k.tiles, [(0, onehots), (1, messages)])

                @block.gpsimd
                def _(pool):
                    def scatter(t):
                        pool.wait_ge(out_ready, t.t + 1)
                        pool.wait_ge(row_ready, t.t + 1)
                        for j in range(SUB):
                            wait_count(pool, scattered[t.two][j], half_rounds(t) * 16)
                        pool.sem_inc(begun, 1)
                        for j in range(SUB):
                            pool.indirect_dma_start(
                                out=k.sums[t.two][j], out_offset=bass.IndirectOffsetOnAxis(
                                    ap=k.idx[t.slot][:, j:j + 1], axis=0),
                                in_=out_rows(t)[:, j, :], in_offset=None,
                                compute_op=ALU.add).then_inc(scattered[t.two][j], 16)
                    over_tiles(pool, k.tiles, [(1, scatter)])
                    for two in range(2):
                        for j in range(SUB):
                            pool.wait_ge(scattered[two][j], 16 * ceil_div(k.tiles - two, 2))
    repeated(k, one_pass, rows=True)


def score_edges(k, name, heads, table, table_dst, kept):
    nc = k.nc
    gat = name == "gat"
    width = F * (2 if gat else 1)
    zs = width // F
    att = k.att2 if gat else k.att1
    cols = SUB * heads

    def z_bank(t, h):
        return k.bank[h * 2 + t.two]

    def outside(t):
        return k.msg[t.two][:, heads + t.slot // 2, :]

    def one_pass():
        with Stage(k, name) as st:
            idx_loaded, gathers_begun, rows_loaded = gather_sems(st)
            loads_begun = st.sem("loads_begun")
            dst_loaded = [st.sem(f"dst_loaded{i}") for i in range(RING)]
            win_loaded = [st.sem(f"win_loaded{i}") for i in range(RING)]
            stored = [st.sem(f"stored{i}") for i in range(RING)]
            onehot_t_ready, z_ready, act_ready = st.sem("onehot_t_ready"), st.sem("z_ready"), st.sem("act_ready")
            slope_ready, score_ready = st.sem("slope_ready"), st.sem("score_ready")
            masked, added = st.sem("masked"), st.sem("added")
            onehot_ready, turned = st.sem("onehot_ready"), st.sem("turned")
            tops, tops_turned, tops_merged, best = (st.sem("tops"), st.sem("tops_turned"),
                                                    st.sem("tops_merged"), st.sem("best"))
            outside_ready, exclusive = st.sem("outside_ready"), st.sem("exclusive")
            with st.block() as block:
                @block.sync
                def _(sp):
                    def loads(t):
                        at = window_base(k, sp, t)
                        wait_count(sp, z_ready, t.t + 1 - RING)
                        sp.sem_inc(loads_begun, 1)
                        load_indices(k, sp, idx_loaded, t)
                        load_window(k, sp, table_dst, at, dst_loaded, win_loaded, t)

                    def keep(t):
                        for j in range(SUB):
                            sp.wait_ge(rows_loaded[t.slot][j], (t.rounds + 1) * 16)
                        sp.dma_start(kept[bass.ds(t.t, 1), :, :].rearrange("o p f -> (o p) f"),
                                     gathered(k, t.slot, width).rearrange("p j f -> p (j f)")).then_inc(
                                         stored[t.slot], 16)
                    over_tiles(sp, k.tiles, [(0, loads), (2, keep)])
                    for slot in range(RING):
                        sp.wait_ge(stored[slot], 16 * ceil_div(k.tiles - slot, RING))

                @block.gpsimd
                def _(pool):
                    def rows(t):
                        wait_count(pool, z_ready, t.t + 1 - RING)
                        wait_count(pool, stored[t.slot], t.rounds * 16)
                        gather(k, pool, table, width, idx_loaded, gathers_begun, rows_loaded, t)
                    over_tiles(pool, k.tiles, [(0, rows)])

                @block.tensor
                def _(pe):
                    def sums(t):
                        pe.wait_ge(win_loaded[t.slot], (t.rounds + 1) * 16)
                        pe.wait_ge(onehot_t_ready, t.t + 1)
                        wait_count(pe, act_ready, t.t - 1)
                        g = gathered(k, t.slot, width)
                        for j in range(SUB):
                            pe.wait_ge(rows_loaded[t.slot][j], (t.rounds + 1) * 16)
                            for h in range(zs):
                                pe.matmul(z_bank(t, h)[:, j * P:(j + 1) * P], g[:, j, h * F:(h + 1) * F],
                                          k.ident[:, :], is_transpose=True, start=(j == 0), stop=False,
                                          skip_group_check=True)
                        for h in range(zs):
                            mm = pe.matmul(z_bank(t, h)[:, :], k.window[t.slot][:, h * F:(h + 1) * F],
                                           k.onehot_t[t.two][:, :], start=False, stop=True,
                                           skip_group_check=True)
                        mm.then_inc(z_ready, 1)

                    def scores(t):
                        pe.wait_ge(act_ready, t.t + 1)
                        wait_count(pe, exclusive if gat else masked, t.t - 1)
                        for h in range(zs):
                            for j in range(SUB):
                                lhs = k.zact[t.two][:, h, j * P:(j + 1) * P]
                                if gat:
                                    mm = pe.matmul(k.bank[4 + t.two][:, h * SUB + j:h * SUB + j + 1], lhs,
                                                   att[:, h:h + 1], start=True, stop=True)
                                else:
                                    mm = pe.matmul(k.bank[4 + t.two][:, j * heads:(j + 1) * heads], lhs,
                                                   att[:, :], start=True, stop=True)
                        mm.then_inc(score_ready, 1)

                    def turn(t):
                        pe.wait_ge(exclusive, t.t + 1)
                        wait_count(pe, tops, t.t)
                        for h in range(heads):
                            mm = pe.transpose(k.bank[6][:, h * P:(h + 1) * P],
                                              k.msg[t.two][:, h, :], k.ident[:, :])
                        mm.then_inc(turned, 1)

                    def turn_tops(t):
                        pe.wait_ge(tops, t.t + 1)
                        wait_count(pe, best, t.t)
                        pe.transpose(k.bank[7][0:heads, 0:P], k.tops[:, t.two, :],
                                     k.ident[:, :]).then_inc(tops_turned, 1)
                    if gat:
                        over_tiles(pe, k.tiles, [(2, scores), (3, turn), (4, turn_tops), (0, sums)])
                    else:
                        over_tiles(pe, k.tiles, [(2, scores), (0, sums)])

                @block.scalar
                def _(act):
                    def activate(t):
                        act.wait_ge(z_ready, t.t + 1)
                        wait_count(act, score_ready, t.t - 1)
                        if gat:
                            for h in range(zs):
                                a = act.mul(k.zact[t.two][:, h, :], z_bank(t, h)[:, :], 0.2)
                            a.then_inc(slope_ready, 1)
                        else:
                            act.activation(k.zact[t.two][:, 0, :], z_bank(t, 0)[:, :],
                                           ACT.Tanh).then_inc(act_ready, 1)

                    def penalties(t):
                        act.wait_ge(onehot_ready, t.t + 1)
                        wait_count(act, exclusive, t.t + 1 - RING)
                        act.activation(outside(t), k.onehot[t.slot][:, :, :].rearrange("p j n -> p (j n)"),
                                       ACT.Copy, bias=-BIG, scale=BIG).then_inc(outside_ready, 1)
                    over_tiles(act, k.tiles, [(0, activate), (1, penalties)] if gat else [(0, activate)])

                @block.vector
                def _(dve):
                    def onehots(t):
                        wait_count(dve, z_ready, t.t - 1)
                        dve.wait_ge(dst_loaded[t.slot], (t.rounds + 1) * 16)
                        make_onehot_t(k, dve, t).then_inc(onehot_t_ready, 1)

                    def leaky(t):
                        wait_count(dve, outside_ready, t.t + 1 - RING)
                        make_onehot(k, dve, t).then_inc(onehot_ready, 1)
                        dve.wait_ge(slope_ready, t.t + 1)
                        for h in range(zs):
                            za = k.zact[t.two][:, h, :]
                            m = dve.tensor_tensor(za, za, z_bank(t, h)[:, :], ALU.max)
                        m.then_inc(act_ready, 1)

                    def pick(t):
                        dve.wait_ge(score_ready, t.t + 1)
                        s = k.bank[4 + t.two][:, 0:cols]
                        m = k.member[:, bass.ds(t.t * SUB, SUB)]
                        mine = k.scores[:, bass.ds(t.t * cols, cols)]
                        picked_s = k.picked[:, 0:cols]
                        if gat:
                            s = s.rearrange("p (h j) -> p h j", j=SUB)
                            m = m.unsqueeze(1).to_broadcast([P, heads, SUB])
                            ps = picked_s.rearrange("p (h j) -> p h j", j=SUB)
                        else:
                            s = s.rearrange("p (j h) -> p j h", h=heads)
                            m = m.unsqueeze(2).to_broadcast([P, SUB, heads])
                            ps = picked_s.rearrange("p (j h) -> p j h", h=heads)
                        wait_count(dve, added, t.t)
                        dve.tensor_tensor(ps, s, m, ALU.mult).then_inc(masked, 1)
                        if gat:
                            dve.wait_ge(outside_ready, t.t + 1)
                            wait_count(dve, turned, t.t - 1)
                            dve.tensor_tensor(k.msg[t.two][:, 0:heads, :].rearrange("p h (j n) -> p h j n", n=WIN),
                                              outside(t).rearrange("p (j n) -> p j n", n=WIN).unsqueeze(1)
                                              .to_broadcast([P, heads, SUB, WIN]),
                                              s.unsqueeze(3).to_broadcast([P, heads, SUB, WIN]),
                                              ALU.add).then_inc(exclusive, 1)
                        dve.wait_ge(masked, t.t + 1)
                        dve.tensor_tensor(mine, mine, picked_s, ALU.add).then_inc(added, 1)

                    def top(t):
                        dve.wait_ge(turned, t.t + 1)
                        wait_count(dve, tops_turned, t.t - 1)
                        dve.tensor_reduce(k.tops[:, t.two, :],
                                          k.bank[6][:, 0:heads * P].rearrange("p (h e) -> p h e", e=P),
                                          AX.X, ALU.max).then_inc(tops, 1)

                    def best_of_nodes(t):
                        at = window_base(k, dve, t)
                        dve.wait_ge(tops_turned, t.t + 1)
                        wait_count(dve, best, t.t)
                        dve.tensor_reduce(k.tile_top[:, :], k.bank[7][0:heads, 0:P].rearrange(
                            "h (j n) -> h n j", n=WIN), AX.X, ALU.max).then_inc(tops_merged, 1)
                        dve.wait_ge(tops_merged, t.t + 1)
                        m = k.node_top[:, bass.ds(at, WIN)]
                        dve.tensor_tensor(m, m, k.tile_top[:, :], ALU.max).then_inc(best, 1)
                    if gat:
                        over_tiles(dve, k.tiles, [(0, onehots), (1, leaky), (2, pick), (3, top),
                                                  (4, best_of_nodes)])
                    else:
                        over_tiles(dve, k.tiles, [(0, onehots), (2, pick)])
    repeated(k, one_pass, rows=True)


def kept_rows(k, sp, kept, width, rows_loaded, t):
    sp.dma_start(gathered(k, t.slot, width).rearrange("p j f -> p (j f)"),
                 kept[bass.ds(t.t, 1), :, :].rearrange("o p f -> (o p) f")).then_inc(rows_loaded[t.slot], 16)


def weigh_additive(k):
    heads, per_head = HEADS1, F // HEADS1

    def weight_sums(t):
        return k.bank[4 + t.slot][0:heads, 0:WIN]

    def msg(t):
        return k.msg[t.two][:, :, :] if t.slot < 2 else k.zact[t.two][:, 1, :].rearrange("p (j f) -> p j f", f=F)

    def one_pass():
        with Stage(k, "addw") as st:
            rows_loaded = [st.sem(f"rows_loaded{i}") for i in range(RING)]
            weight_ready, onehot_ready, msg_ready = st.sem("weight_ready"), st.sem("onehot_ready"), st.sem("msg_ready")
            sums_ready, added = st.sem("sums_ready"), st.sem("added")
            copied, turned, turns_begun = st.sem("copied"), st.sem("turned"), st.sem("turns_begun")
            with st.block() as block:
                @block.sync
                def _(sp):
                    def loads(t):
                        wait_count(sp, msg_ready, t.t + 1 - RING)
                        kept_rows(k, sp, k.kept1, F, rows_loaded, t)
                    over_tiles(sp, k.tiles, [(0, loads)], head=2)

                @block.scalar
                def _(act):
                    def weights(t):
                        wait_count(act, sums_ready, t.t + 1 - RING)
                        act.activation(k.weight[t.slot][:, :],
                                       k.scores[:, bass.ds(t.t * SUB * heads, SUB * heads)],
                                       ACT.Exp).then_inc(weight_ready, 1)

                    def copy(t):
                        act.wait_ge(sums_ready, t.t + 1)
                        wait_count(act, turned, t.t - 1)
                        act.copy(k.tile_rows[t.two][:, 0:F], k.bank[t.two][0:WIN, 0:F]).then_inc(copied, 1)
                    over_tiles(act, k.tiles, [(0, weights), (2, copy)], head=2)

                @block.tensor
                def _(pe):
                    def sums(t):
                        pe.wait_ge(msg_ready, t.t + 1)
                        pe.wait_ge(onehot_ready, t.t + 1)
                        pe.wait_ge(weight_ready, t.t + 1)
                        wait_count(pe, copied, t.t - 1)
                        wait_count(pe, added, t.t + 1 - RING)
                        for j in range(SUB):
                            pe.matmul(k.bank[t.two][0:WIN, 0:F], k.onehot[t.slot][:, j, :], msg(t)[:, j, :],
                                      start=(j == 0), stop=(j == SUB - 1))
                        for j in range(SUB):
                            mm = pe.matmul(weight_sums(t),
                                           k.weight[t.slot][:, j * heads:(j + 1) * heads],
                                           k.onehot[t.slot][:, j, :], start=(j == 0), stop=(j == SUB - 1))
                        mm.then_inc(sums_ready, 1)

                    def turn(t):
                        pe.wait_ge(copied, t.t + 1)
                        wait_count(pe, added, t.t - 1)
                        pe.sem_inc(turns_begun, 1)
                        pe.transpose(k.bank[2 + t.two][:, 0:WIN], k.tile_rows[t.two][:, 0:F],
                                     k.ident[0:WIN, 0:WIN]).then_inc(turned, 1)
                    over_tiles(pe, k.tiles, [(4, turn), (2, sums)], head=2)

                @block.vector
                def _(dve):
                    def messages(t):
                        wait_count(dve, sums_ready, t.t + 1 - RING)
                        make_onehot(k, dve, t).then_inc(onehot_ready, 1)
                        dve.wait_ge(weight_ready, t.t + 1)
                        dve.wait_ge(rows_loaded[t.slot], (t.rounds + 1) * 16)
                        g = gathered(k, t.slot, F).rearrange("p j (h c) -> p (j h) c", h=heads)
                        dve.tensor_tensor(msg(t).rearrange("p j (h c) -> p (j h) c", h=heads), g,
                                          k.weight[t.slot][:, :].unsqueeze(2).to_broadcast([P, SUB * heads, per_head]),
                                          ALU.mult).then_inc(msg_ready, 1)

                    def add(t):
                        at = window_base(k, dve, t)
                        dve.wait_ge(turned, t.t + 1)
                        dve.wait_ge(sums_ready, t.t + 1)
                        wait_count(dve, added, t.t)
                        a = k.acc[:, 0, bass.ds(at, WIN)]
                        dve.tensor_tensor(a, a, k.bank[2 + t.two][:, 0:WIN], ALU.add)
                        z = k.node_sum1[:, bass.ds(at, WIN)]
                        dve.tensor_tensor(z, z, weight_sums(t), ALU.add).then_inc(added, 1)
                    over_tiles(dve, k.tiles, [(0, messages), (4, add)], head=2)
    repeated(k, one_pass)


def store_tops(k):
    nc, B = k.nc, k.blocks
    whole, rest = k.top_rows[:, 0, :], k.top_rows[:, 1, :]

    def part(c):
        return k.top_parts[:, :, c, :]

    def by_node(a):
        return a.rearrange("p (b h) -> p b h", h=HEADS2)

    with Stage(k, "tops") as st:
        turned, step, stored = st.sem("turned"), st.sem("step"), st.sem("stored")
        with st.block() as block:
            @block.tensor
            def _(pe):
                for b in range(B):
                    mm = pe.transpose(k.bank[0][:, b * HEADS2:(b + 1) * HEADS2], k.node_top[:, b * P:(b + 1) * P],
                                      k.ident[0:HEADS2, 0:HEADS2])
                mm.then_inc(turned, 1)

            @block.vector
            def _(dve):
                dve.wait_ge(turned, 1)
                dve.tensor_copy(whole, k.bank[0][:, 0:B * HEADS2]).then_inc(step, 1)
                for c in range(PARTS):
                    source = whole if c == 0 else rest
                    dve.wait_ge(step, 2 * c + 1)
                    dve.tensor_copy(part(c), by_node(source)).then_inc(step, 1)
                    if c < PARTS - 1:
                        dve.wait_ge(step, 2 * c + 2)
                        dve.tensor_tensor(by_node(rest), by_node(source), part(c), ALU.subtract).then_inc(step, 1)

            @block.sync
            def _(sp):
                sp.wait_ge(step, 2 * PARTS)
                with nc.allow_non_contiguous_dma(reason="a few bytes per node"):
                    sp.dma_start(k.parts_top.rearrange("(b p) c h -> p b (c h)", p=P),
                                 k.top_parts[:, :, :, :].rearrange("p b c h -> p b (c h)")).then_inc(stored, 16)
                sp.wait_ge(stored, 16)


def weigh_gat(k):
    heads = HEADS2
    cols = heads * SUB

    def weight_sums(t):
        return k.bank[4 + t.slot][0:heads, 0:WIN]

    def by_head(w):
        return w.rearrange("p (h j) -> p h j", j=SUB)

    def one_pass():
        with Stage(k, "gatw") as st:
            rows_loaded = [st.sem(f"rows_loaded{i}") for i in range(RING)]
            dst_loaded = [st.sem(f"dst_loaded{i}") for i in range(RING)]
            win_loaded = [st.sem(f"win_loaded{i}") for i in range(RING)]
            loads_begun = st.sem("loads_begun")
            onehot_ready, onehot_t_ready, tops_ready = (st.sem("onehot_ready"), st.sem("onehot_t_ready"),
                                                        st.sem("tops_ready"))
            shift_ready, arg_ready, weight_ready = st.sem("shift_ready"), st.sem("arg_ready"), st.sem("weight_ready")
            scaled_ready, sums_ready, copied = st.sem("scaled_ready"), st.sem("sums_ready"), st.sem("copied")
            turned, added, turns_begun = st.sem("turned"), st.sem("added"), st.sem("turns_begun")
            with st.block() as block:
                @block.sync
                def _(sp):
                    def loads(t):
                        at = window_base(k, sp, t)
                        wait_count(sp, tops_ready, t.t + 1 - RING)
                        sp.sem_inc(loads_begun, 1)
                        load_window(k, sp, k.parts_top, at, dst_loaded, win_loaded, t)

                    def rows(t):
                        wait_count(sp, sums_ready, t.t + 1 - RING)
                        kept_rows(k, sp, k.kept2, 2 * F, rows_loaded, t)
                    with k.nc.allow_non_contiguous_dma(reason="the maxima's windows are a few bytes per node"):
                        over_tiles(sp, k.tiles, [(0, loads), (1, rows)], head=2)

                @block.scalar
                def _(act):
                    def weights(t):
                        act.wait_ge(arg_ready, t.t + 1)
                        wait_count(act, sums_ready, t.t + 1 - RING)
                        act.activation(k.weight[t.slot][:, 0:cols], k.shifted[t.two][:, :],
                                       ACT.Exp).then_inc(weight_ready, 1)

                    def copy(t):
                        act.wait_ge(sums_ready, t.t + 1)
                        wait_count(act, turned, t.t - 1)
                        act.copy(k.tile_rows[t.two][:, :], k.bank[t.two][0:WIN, 0:heads * F]).then_inc(copied, 1)
                    over_tiles(act, k.tiles, [(1, weights), (2, copy)], head=2)

                @block.tensor
                def _(pe):
                    def tops(t):
                        pe.wait_ge(onehot_t_ready, t.t + 1)
                        pe.wait_ge(win_loaded[t.slot], (t.rounds + 1) * 16)
                        wait_count(pe, shift_ready, t.t)
                        for j in range(SUB):
                            mm = pe.matmul(k.bank[3][:, j * heads:(j + 1) * heads],
                                           k.onehot_t[t.two][:, j * P:(j + 1) * P], k.window[t.slot][:, 0:heads],
                                           start=True, stop=True)
                        mm.then_inc(tops_ready, 1)

                    def sums(t):
                        pe.wait_ge(scaled_ready, t.t + 1)
                        pe.wait_ge(rows_loaded[t.slot], (t.rounds + 1) * 16)
                        wait_count(pe, copied, t.t - 1)
                        wait_count(pe, added, t.t + 1 - RING)
                        g = gathered(k, t.slot, 2 * F)
                        for h in range(heads):
                            for j in range(SUB):
                                pe.matmul(k.bank[t.two][0:WIN, h * F:(h + 1) * F], k.scaled[t.slot][:, h, j, :],
                                          g[:, j, h * F:(h + 1) * F], start=(j == 0), stop=(j == SUB - 1))
                        w = by_head(k.weight[t.slot][:, 0:cols])
                        for j in range(SUB):
                            mm = pe.matmul(weight_sums(t), w[:, :, j], k.onehot[t.slot][:, j, :],
                                           start=(j == 0), stop=(j == SUB - 1))
                        mm.then_inc(sums_ready, 1)

                    def turn(t):
                        pe.wait_ge(copied, t.t + 1)
                        wait_count(pe, added, t.t)
                        pe.sem_inc(turns_begun, 1)
                        for h in range(heads):
                            mm = pe.transpose(k.bank[2][:, h * WIN:(h + 1) * WIN],
                                              k.tile_rows[t.two][:, h * F:(h + 1) * F], k.ident[0:WIN, 0:WIN])
                        mm.then_inc(turned, 1)
                    over_tiles(pe, k.tiles, [(4, turn), (2, sums), (0, tops)], head=2)

                @block.vector
                def _(dve):
                    def onehots(t):
                        wait_count(dve, sums_ready, t.t + 1 - RING)
                        make_onehot(k, dve, t).then_inc(onehot_ready, 1)
                        wait_count(dve, tops_ready, t.t - 1)
                        dve.wait_ge(dst_loaded[t.slot], (t.rounds + 1) * 16)
                        make_onehot_t(k, dve, t).then_inc(onehot_t_ready, 1)

                    def shift(t):
                        dve.wait_ge(tops_ready, t.t + 1)
                        wait_count(dve, weight_ready, t.t - 1)
                        dve.tensor_tensor(by_head(k.shifted[t.two][:, :]),
                                          by_head(k.scores[:, bass.ds(t.t * cols, cols)]),
                                          k.bank[3][:, 0:cols].rearrange("p (j h) -> p h j", h=heads),
                                          ALU.subtract).then_inc(shift_ready, 1)

                    def limit(t):
                        dve.wait_ge(shift_ready, t.t + 1)
                        dve.tensor_scalar(k.shifted[t.two][:, :], k.shifted[t.two][:, :], 1.0, None,
                                          ALU.min).then_inc(arg_ready, 1)

                    def scale(t):
                        dve.wait_ge(weight_ready, t.t + 1)
                        dve.wait_ge(onehot_ready, t.t + 1)
                        dve.tensor_tensor(k.scaled[t.slot][:, :, :, :],
                                          k.onehot[t.slot][:, :, :].unsqueeze(1).to_broadcast([P, heads, SUB, WIN]),
                                          by_head(k.weight[t.slot][:, 0:cols]).unsqueeze(3).to_broadcast(
                                              [P, heads, SUB, WIN]), ALU.mult).then_inc(scaled_ready, 1)

                    def add(t):
                        at = window_base(k, dve, t)
                        dve.wait_ge(turned, t.t + 1)
                        dve.wait_ge(sums_ready, t.t + 1)
                        wait_count(dve, added, t.t)
                        a = k.acc[:, :, bass.ds(at, WIN)]
                        dve.tensor_tensor(a, a, k.bank[2][:, 0:heads * WIN].rearrange(
                            "p (a n) -> p a n", n=WIN), ALU.add)
                        z = k.node_sum[:, bass.ds(at, WIN)]
                        dve.tensor_tensor(z, z, weight_sums(t), ALU.add).then_inc(added, 1)
                    over_tiles(dve, k.tiles, [(2, scale), (0, onehots), (1, shift), (1, limit), (4, add)], head=2)
    repeated(k, one_pass, rows=True)



def gcn_layer(k):
    nc, B, N = k.nc, k.blocks, k.n_nodes
    count_degrees(k)
    layer_norm(k, "n0", k.x, k.h, relu=True)
    own = k.wide[:, 0, :].rearrange("p (b f) -> p b f", f=F)
    vector_stage(k, "rows0", lambda dve: dve.tensor_tensor(
        own, k.h[:, :, :], k.inv_sqrt_deg_nm[:, :].unsqueeze(2).to_broadcast([P, B, F]), ALU.mult))
    store_table(k, "rows0", own, k.table1)
    to_feature_major(k, "own0", own, k.acc[:, 0, :])
    sum_neighbours(k, "agg0", k.table1)
    vector_stage(k, "deg1", lambda dve: dve.tensor_tensor(k.fa[:, :], k.acc[:, 0, :], k.inv_sqrt_deg[:, :], ALU.mult))
    linear(k, "gcn1", k.w["L0_gnn_W1"][:, :], k.fa,
           lambda act, lh, bank: act.activation(k.fb[:, lh[0]:lh[1]], bank, ACT.Relu,
                                                bias=k.w["L0_gnn_b1"][:, 0:1]), engine="scalar")
    vector_stage(k, "rows1", lambda dve: dve.tensor_tensor(k.acc[:, 0, :], k.fb[:, :], k.inv_sqrt_deg[:, :], ALU.mult))
    rows = k.wide[:, 0, :].rearrange("p (b f) -> p b f", f=F)
    turn_to_nodes(k, "turn1", k.acc[:, 0, :], rows)
    store_table(k, "rows1", rows, k.table1)
    sum_neighbours(k, "agg1", k.table1)
    vector_stage(k, "deg2", lambda dve: dve.tensor_tensor(k.fa[:, :], k.acc[:, 0, :], k.inv_sqrt_deg[:, :], ALU.mult))
    logits = k.wide[:, 0, :].rearrange("p (b f) -> p b f", f=F)
    product_stage(k, "gcn2", B,
                  lambda pe, b, bank: pe.matmul(bank[:, 0:F], k.fa[:, b * P:(b + 1) * P], k.w["L0_gnn_W2"][:, :],
                                                start=True, stop=True),
                  "vector",
                  lambda dve, b, bank: dve.tensor_tensor(logits[:, b, :], bank[:, 0:F], k.w["L0_gnn_b2"][:, :],
                                                         ALU.add))

    def wide(stat):
        return stat[:, :].unsqueeze(2).to_broadcast([P, B, F])

    with Stage(k, "soft") as st:
        step, raised = st.sem("step"), st.sem("raised")
        with st.block() as block:
            @block.vector
            def _(dve):
                dve.tensor_reduce(k.stat[:, :], logits, AX.X, ALU.max).then_inc(step, 1)
                dve.wait_ge(step, 1)
                dve.tensor_tensor(logits, logits, wide(k.stat), ALU.subtract).then_inc(step, 1)
                dve.wait_ge(raised, 1)
                dve.tensor_reduce(k.stat[:, :], logits, AX.X, ALU.add).then_inc(step, 1)
                dve.wait_ge(step, 3)
                dve.reciprocal(k.stat2[:, :], k.stat[:, :]).then_inc(step, 1)
                dve.wait_ge(step, 4)
                dve.tensor_tensor(logits, logits, wide(k.stat2), ALU.mult).then_inc(step, 1)
                dve.wait_ge(step, 5)
                dve.tensor_tensor(k.x[:, :, :], k.x[:, :, :], logits, ALU.add)

            @block.scalar
            def _(act):
                act.wait_ge(step, 2)
                act.activation(logits, logits, ACT.Exp).then_inc(raised, 1)


def turn_to_nodes(k, name, src, dst):
    def product(pe, c, bank):
        lo, hi = chunks(k.n_nodes)[c]
        for b in range(lo // P, hi // P):
            mm = pe.transpose(bank[:, b * P - lo:(b + 1) * P - lo], src[:, b * P:(b + 1) * P], k.ident[:, :])
        return mm

    def take(act, c, bank):
        lo, hi = chunks(k.n_nodes)[c]
        return act.copy(dst[:, lo // P:hi // P, :], bank[:, 0:hi - lo].rearrange("p (b f) -> p b f", f=F))

    product_stage(k, name, len(chunks(k.n_nodes)), product, "scalar", take)


def node_parts(k):
    h = k.h[:, :, :].rearrange("p b f -> p (b f)").bitcast(BF16)
    return [h[:, 0:k.n_nodes], h[:, k.n_nodes:], k.acc[:, 1, :].bitcast(BF16)[:, 0:k.n_nodes]]


def additive_layer(k):
    layer_norm(k, "n1", k.x, k.h, relu=True)
    to_feature_major(k, "turn2", k.h, k.fa)
    table_rows(k, "proj", k.fa, k.w["L1_gnn_W"][:, :], None, k.table1)
    store_parts(k, "proj_parts", k.wide[:, 0, :], k.wide[:, 1, :], node_parts(k), k.parts1)
    per_edge = k.tiles * SUB
    scores = k.scores[:, :].rearrange("p (e h) -> p e h", h=HEADS1)
    vector_stage(k, "pad1", lambda dve: dve.tensor_copy(
        scores, k.pad[:, :].unsqueeze(2).to_broadcast([P, per_edge, HEADS1])))
    score_edges(k, "add", HEADS1, k.table1, k.parts1, k.kept1)
    with Stage(k, "max1") as st:
        step, turned, spread = st.sem("step"), st.sem("turned"), st.sem("spread")
        top = k.small[:, 0:HEADS1]
        with st.block() as block:
            @block.vector
            def _(dve):
                dve.memset(k.small[:, :], 0.0)
                dve.memset(k.node_sum1[:, :], 0.0)
                dve.memset(k.acc[:, 0, :], 0.0).then_inc(step, 1)
                dve.wait_ge(step, 1)
                dve.tensor_reduce(top, scores.rearrange("p e h -> p h e"), AX.X, ALU.max).then_inc(step, 1)
                dve.wait_ge(turned, 1)
                dve.tensor_reduce(k.small[0:HEADS1, 8:9], k.bank[0][0:HEADS1, 0:P], AX.X, ALU.max).then_inc(step, 1)
                dve.wait_ge(step, 3)
                dve.tensor_scalar(k.small[0:HEADS1, 12:12 + HEADS1], k.ident[0:HEADS1, 0:HEADS1],
                                  k.small[0:HEADS1, 8:9], None, ALU.mult).then_inc(step, 1)
                dve.wait_ge(spread, 1)
                dve.tensor_copy(top, k.bank[1][:, 0:HEADS1]).then_inc(step, 1)
                dve.wait_ge(step, 5)
                dve.tensor_tensor(scores, scores, top.unsqueeze(1).to_broadcast([P, per_edge, HEADS1]), ALU.subtract)

            @block.tensor
            def _(pe):
                pe.wait_ge(step, 2)
                pe.transpose(k.bank[0][0:HEADS1, 0:P], top, k.ident[:, :]).then_inc(turned, 1)
                pe.wait_ge(step, 4)
                pe.matmul(k.bank[1][:, 0:HEADS1], k.ones[0:HEADS1, :], k.small[0:HEADS1, 12:12 + HEADS1],
                          start=True, stop=True).then_inc(spread, 1)
    weigh_additive(k)
    vector_stage(k, "norm1",
                 lambda dve: dve.tensor_scalar(k.node_sum1[:, :], k.node_sum1[:, :], 1e-12, None, ALU.max),
                 lambda dve: dve.reciprocal(k.node_sum1[:, :], k.node_sum1[:, :]))
    linear(k, "div1", k.head_block[:, :], k.node_sum1,
           lambda dve, lh, bank: dve.tensor_tensor(k.fa[:, lh[0]:lh[1]], k.acc[:, 0, lh[0]:lh[1]], bank, ALU.mult))
    add_to_nodes(k, "sum1", k.fa, k.x)


def gat_layer(k):
    N = k.n_nodes
    w = k.w
    layer_norm(k, "n2", k.x, k.h, relu=True)
    inner = k.acc[:, 0, :].rearrange("p (b f) -> p b f", f=F)
    layer_norm(k, "n2i", k.h, inner, relu=False)
    vector_stage(k, "res2", lambda dve: dve.tensor_tensor(k.x[:, :, :], k.x[:, :, :], k.h[:, :, :], ALU.add))
    to_feature_major(k, "turn3", inner, k.fa, func=ACT.Relu, scale=w["L2_gnn_gamma"][:, 0:1],
                     bias=w["L2_gnn_beta"][:, 0:1])
    table_rows(k, "left", k.fa, w["L2_gnn_Wl"][:, :], w["L2_gnn_bl"][:, :], k.table2)
    table_rows(k, "right", k.fa, w["L2_gnn_Wr"][:, :], w["L2_gnn_br"][:, :], None)
    wide = k.wide[:, :, :].rearrange("p a n -> p (a n)")
    store_parts(k, "right_parts", wide, wide,
                [k.acc[:, 0, :].bitcast(BF16), k.acc[:, 1, :].bitcast(BF16),
                 k.h[:, :, :].rearrange("p b f -> p (b f)").bitcast(BF16)], k.parts2)
    linear(k, "resw", w["L2_gnn_res_W"][:, :], k.fa,
           lambda act, lh, bank: act.activation(k.fb[:, lh[0]:lh[1]], bank, ACT.Identity,
                                                bias=w["L2_gnn_bias"][:, 0:1]), engine="scalar")
    scores = k.scores[:, 0:k.tiles * SUB * HEADS2].rearrange("p (t h j) -> p t h j", h=HEADS2, j=SUB)
    vector_stage(k, "pad2",
                 lambda dve: dve.tensor_copy(scores[:, :, 0, :], k.pad[:, :].rearrange("p (t j) -> p t j", j=SUB)),
                 lambda dve: dve.tensor_copy(scores[:, :, 1, :], k.pad[:, :].rearrange("p (t j) -> p t j", j=SUB)),
                 lambda dve: dve.memset(k.node_top[:, :], -BIG))
    score_edges(k, "gat", HEADS2, k.table2, k.parts2, k.kept2)
    cs = chunks(N)

    def spread_rows(name, rows, dst):
        def product(pe, c, bank):
            h, (lo, hi) = c // len(cs), cs[c % len(cs)]
            return pe.matmul(bank[:, 0:hi - lo], k.head_row[:, h * P:(h + 1) * P], rows[:, lo:hi],
                             start=True, stop=True)

        def take(act, c, bank):
            h, (lo, hi) = c // len(cs), cs[c % len(cs)]
            return act.copy(dst[:, h, lo:hi], bank[:, 0:hi - lo])
        product_stage(k, name, HEADS2 * len(cs), product, "scalar", take)

    store_tops(k)
    vector_stage(k, "zero2", lambda dve: dve.memset(k.acc[:, :, :], 0.0),
                 lambda dve: dve.memset(k.node_sum[:, :], 0.0))
    weigh_gat(k)
    vector_stage(k, "norm2",
                 lambda dve: dve.tensor_scalar(k.node_sum[:, :], k.node_sum[:, :], 1e-16, None, ALU.add),
                 lambda dve: dve.reciprocal(k.node_sum[:, :], k.node_sum[:, :]),
                 lambda dve: dve.tensor_scalar(k.node_sum[:, :], k.node_sum[:, :], 1.0 / HEADS2, None, ALU.mult))
    spread_rows("sums2", k.node_sum, k.wide)
    vector_stage(k, "mean2",
                 lambda dve: dve.tensor_tensor(k.acc[:, :, :], k.acc[:, :, :], k.wide[:, :, :], ALU.mult),
                 lambda dve: dve.tensor_tensor(k.acc[:, 0, :], k.acc[:, 0, :], k.acc[:, 1, :], ALU.add),
                 lambda dve: dve.tensor_tensor(k.fb[:, :], k.fb[:, :], k.acc[:, 0, :], ALU.add))
    add_to_nodes(k, "sum2", k.fb, k.x)


def ssp_linear(k, name, src, weight, bias, dst, residual, scratch, keep=None):
    cs = chunks(k.n_nodes)
    low, soft = scratch
    soft = keep if keep is not None else soft
    with Stage(k, name) as st:
        folded, raised, logged, soft_ready = st.sem("folded"), st.sem("raised"), st.sem("logged"), st.sem("soft_ready")
        ready, taken = st.sem("ready"), st.sem("taken")
        with st.block() as block:
            @block.scalar
            def _(act):
                for c, (lo, hi) in enumerate(cs):
                    act.wait_ge(folded, c + 1)
                    act.activation(low[:, lo:hi], low[:, lo:hi], ACT.Exp).then_inc(raised, 1)
                    act.wait_ge(raised, c + 1)
                    act.activation(low[:, lo:hi], low[:, lo:hi], ACT.Ln, bias=k.half[:, 0:1],
                                   scale=0.5).then_inc(logged, 1)

            @block.tensor
            def _(pe):
                for c, (lo, hi) in enumerate(cs):
                    pe.wait_ge(soft_ready, c + 1)
                    pe.matmul(k.bank[c][:, 0:hi - lo], weight, soft[:, lo:hi], start=True,
                              stop=True).then_inc(ready, 1)

            @block.vector
            def _(dve):
                for lo, hi in cs:
                    dve.scalar_tensor_tensor(out=low[:, lo:hi], in0=src[:, lo:hi], scalar=-1.0, in1=src[:, lo:hi],
                                             op0=ALU.mult, op1=ALU.min).then_inc(folded, 1)
                for c in range(len(cs) + 1):
                    if c < len(cs):
                        lo, hi = cs[c]
                        dve.wait_ge(logged, c + 1)
                        dve.scalar_tensor_tensor(out=soft[:, lo:hi], in0=src[:, lo:hi], scalar=0.0,
                                                 in1=low[:, lo:hi], op0=ALU.max, op1=ALU.add).then_inc(soft_ready, 1)
                    if c > 0:
                        lo, hi = cs[c - 1]
                        dve.wait_ge(ready, c)
                        if residual is None:
                            dve.tensor_scalar(dst[:, lo:hi], k.bank[c - 1][:, 0:hi - lo], bias, None,
                                              ALU.add).then_inc(taken, 1)
                        else:
                            dve.scalar_tensor_tensor(out=dst[:, lo:hi], in0=k.bank[c - 1][:, 0:hi - lo],
                                                     scalar=bias, in1=residual[:, lo:hi], op0=ALU.add,
                                                     op1=ALU.add).then_inc(taken, 1)


def load_sources(k):
    B, nq = k.blocks, k.tiles * SUB
    raw = k.scores[:, 0:nq].bitcast(I32)
    k.src_f = k.scores[:, nq:2 * nq]
    k.earlier = k.fb[:, 0:SUB * P].rearrange("p (j e) -> p j e", e=P)
    zeros = k.wide[:, 0, :]
    with Stage(k, "srcs") as st:
        loaded, cleared, zeroed = st.sem("loaded"), st.sem("cleared"), st.sem("zeroed")
        with st.block() as block:
            @block.vector
            def _(dve):
                dve.memset(zeros, 0.0).then_inc(cleared, 1)
                dve.tensor_scalar(k.spare[:, :], k.iota_p[:, :], float(k.n_nodes), None, ALU.add)
                dve.wait_ge(loaded, 16)
                dve.tensor_copy(k.src_f, raw)

            @block.sync
            def _(sp):
                sp.dma_start(raw, k.ins["src_edges"]).then_inc(loaded, 16)
                sp.wait_ge(cleared, 1)
                for two in k.sums:
                    for table in two:
                        sp.dma_start(table[0:k.n_nodes, :].rearrange("(b p) f -> p b f", p=P),
                                     zeros.rearrange("p (b f) -> p b f", f=F)).then_inc(zeroed, 16)
                        sp.dma_start(table[k.n_nodes:k.n_nodes + P, :], zeros[:, 0:F]).then_inc(zeroed, 16)
                sp.wait_ge(loaded, 16)
                sp.wait_ge(zeroed, 32 * 2 * SUB)


def collect_sums(k):
    tables = [table for two in k.sums for table in two]
    total = k.h
    with Stage(k, "coll") as st:
        loaded = [st.sem(f"loaded{i}") for i in range(3)]
        added = st.sem("added")
        bufs = [k.wide[:, 0, :], k.wide[:, 1, :], k.acc[:, 1, :]]
        with st.block() as block:
            @block.sync
            def _(sp):
                for n, table in enumerate(tables):
                    wait_count(sp, added, n - 2)
                    sp.dma_start(bufs[n % 3].rearrange("p (b f) -> p b f", f=F),
                                 table[0:k.n_nodes, :].rearrange("(b p) f -> p b f", p=P)).then_inc(loaded[n % 3], 16)

            @block.vector
            def _(dve):
                for n in range(len(tables)):
                    dve.wait_ge(loaded[n % 3], 16 * (n // 3 + 1))
                    wait_count(dve, added, n)
                    buf = bufs[n % 3].rearrange("p (b f) -> p b f", f=F)
                    if n == 0:
                        dve.tensor_copy(total[:, :, :], buf).then_inc(added, 1)
                    else:
                        dve.tensor_tensor(total[:, :, :], total[:, :, :], buf, ALU.add).then_inc(added, 1)

    def product(pe, c, bank):
        lo, hi = chunks(k.n_nodes)[c]
        for b in range(lo // P, hi // P):
            mm = pe.transpose(bank[:, b * P - lo:(b + 1) * P - lo], total[:, b, :], k.ident[:, :])
        return mm

    def take(dve, c, bank):
        lo, hi = chunks(k.n_nodes)[c]
        a = k.acc[:, 0, lo:hi]
        return dve.tensor_tensor(a, a, bank[:, 0:hi - lo], ALU.add)

    product_stage(k, "collt", len(chunks(k.n_nodes)), product, "vector", take)


def interaction_layer(k):
    w = k.w
    layer_norm(k, "n3", k.x, k.h, relu=True)
    to_feature_major(k, "turn4", k.h, k.fa)
    scratch = (k.wide[:, 0, :], k.wide[:, 1, :])
    m = k.acc[:, 0, :]
    ssp_linear(k, "xi", k.fa, w["L3_gnn_Wi"][:, :], w["L3_gnn_bi"][:, 0:1], m, None, scratch, keep=k.fb)
    table_rows(k, "xj", k.fb, w["L3_gnn_Wj"][:, :], w["L3_gnn_bj"][:, :], None)
    store_parts(k, "xj_parts", k.wide[:, 0, :], k.wide[:, 0, :], node_parts(k), k.parts1)
    load_sources(k)
    scatter_filtered(k, k.parts1)
    collect_sums(k)
    mid = k.acc[:, 1, :]
    for l in range(k.ins["L3_gnn_res_int_W1"].shape[0]):
        ssp_linear(k, f"ri{l}a", m, w[f"L3_gnn_res_int_W1{l}"][:, :], w[f"L3_gnn_res_int_b1{l}"][:, 0:1], mid,
                   None, scratch)
        ssp_linear(k, f"ri{l}b", mid, w[f"L3_gnn_res_int_W2{l}"][:, :], w[f"L3_gnn_res_int_b2{l}"][:, 0:1], m,
                   m, scratch)
    vector_stage(k, "gate", lambda dve: dve.tensor_scalar(k.fa[:, :], k.fa[:, :], w["L3_gnn_u"][:, 0:1], None,
                                                          ALU.mult))
    ssp_linear(k, "dense", m, w["L3_gnn_dense_W"][:, :], w["L3_gnn_dense_b"][:, 0:1], k.fa, k.fa, scratch)
    for l in range(k.ins["L3_gnn_res_at_W1"].shape[0]):
        ssp_linear(k, f"ra{l}a", k.fa, w[f"L3_gnn_res_at_W1{l}"][:, :], w[f"L3_gnn_res_at_b1{l}"][:, 0:1], mid,
                   None, scratch)
        ssp_linear(k, f"ra{l}b", mid, w[f"L3_gnn_res_at_W2{l}"][:, :], w[f"L3_gnn_res_at_b2{l}"][:, 0:1], k.fa,
                   k.fa, scratch)
    add_to_nodes(k, "sum3", k.fa, k.x)


def store_nodes(k):
    n = k.out.shape[0]
    full = n // P
    with Stage(k, "out") as st:
        stored = st.sem("stored")
        with st.block() as block:
            @block.sync
            def _(sp):
                sp.dma_start(k.out[0:full * P, :].rearrange("(b p) f -> p b f", p=P),
                             k.x[:, 0:full, :]).then_inc(stored, 16)
                sp.dma_start(k.out[full * P:n, :], k.x[0:n - full * P, full, :]).then_inc(stored, 16)
                sp.wait_ge(stored, 32)


def gnn_kernel(nc, ins, out, n_edges):
    with ExitStack() as ctx:
        k = Kernel(nc, ctx, ins, out)
        load_everything(k)
        choose_passes(k, n_edges)
        gcn_layer(k)
        additive_layer(k)
        gat_layer(k)
        interaction_layer(k)
        store_nodes(k)


def kernel(**inputs):
    import numpy as _np
    import concourse.bacc as _bacc
    from concourse import mybir as _mybir
    from concourse.bass_utils import run_bass_kernel_spmd as _run

    arrays = {name: _np.ascontiguousarray(a) for name, a in inputs.items()}
    x, src, dst, attr = (arrays.pop(name) for name in ("x", "src", "dst", "edge_attr_64"))
    n, f = x.shape
    n_edges, depth = attr.shape
    blocks, tiles = ceil_div(n, P), ceil_div(n_edges, 2 * TILE) * 2

    x_rows = _np.zeros((blocks * P, f), x.dtype)
    x_rows[:n] = x
    arrays["x"] = _np.ascontiguousarray(x_rows.reshape(blocks, P, f).transpose(1, 0, 2))
    src_rows, dst_rows = _np.zeros(tiles * TILE, src.dtype), _np.full(tiles * TILE, -1, dst.dtype)
    src_rows[:n_edges], dst_rows[:n_edges] = src, dst
    arrays["src_rows"] = _np.ascontiguousarray(src_rows.reshape(tiles, SUB, P).transpose(0, 2, 1))
    arrays["src_flat"] = src_rows.reshape(tiles, TILE)
    arrays["src_edges"] = _np.ascontiguousarray(
        src_rows.reshape(tiles, SUB, P).transpose(2, 0, 1).reshape(P, tiles * SUB))
    arrays["dst_first"] = _np.ascontiguousarray(dst_rows[::TILE].reshape(1, tiles))
    arrays["dst_edges"] = _np.ascontiguousarray(
        dst_rows.reshape(tiles, SUB, P).transpose(2, 0, 1).reshape(P, tiles * SUB))
    attr_rows = _np.zeros((tiles * TILE, depth), attr.dtype)
    attr_rows[:n_edges] = attr
    arrays["attr_rows"] = _np.ascontiguousarray(attr_rows.reshape(tiles, TILE, depth).transpose(0, 2, 1))

    nc = _bacc.Bacc("TRN2", target_bir_lowering=False, num_devices=1)
    ins = {name: nc.dram_tensor(f"in_{name}", a.shape, _mybir.dt.from_np(a.dtype), kind="ExternalInput").ap()
           for name, a in arrays.items()}
    out = nc.dram_tensor("out_nodes", (n, f), _mybir.dt.from_np(x.dtype), kind="ExternalOutput").ap()
    gnn_kernel(nc, ins, out, n_edges)
    r = _run(nc, [{f"in_{name}": a for name, a in arrays.items()}], core_ids=[0])
    return r.results[0]["out_nodes"]
```
